# Optimizing a Trainium2 kernel written in Bass

```python
import numpy as np
import jax
import jax.numpy as jnp

def _softmax(x, axis=-1):
    return jax.nn.softmax(x, axis=axis)

def _gelu(x):
    return jax.nn.gelu(x, approximate=True)

def _silu(x):
    return jax.nn.silu(x)

def _sigmoid(x):
    return jax.nn.sigmoid(x)

def _layernorm(x, axis=-1, eps=1e-05):
    m = jnp.mean(x, axis=axis, keepdims=True)
    v = jnp.var(x, axis=axis, keepdims=True)
    return (x - m) / jnp.sqrt(v + eps)

def _scatter_add(tgt, idx, src, axis=0):
    return tgt.at[idx].add(src)

def _segment_sum(src, seg, n):
    return jax.ops.segment_sum(src, seg, n)
kernel_name = 'mk_flamingo_gated_d4_seqx_r8_4cd68b'

def setup_inputs(seed: int=0):
    np.random.seed(seed)
    _w = jnp.asarray

    def _rec_inputs():
        import jax
        import jax.numpy as jnp
        _rk = jax.random.key(seed)
        x = -0.0003929 + 0.9999 * jax.random.normal(jax.random.fold_in(_rk, 1), (16, 128, 128), jnp.float32)
        _lenS = 128 - jax.random.randint(jax.random.fold_in(_rk, 7), (16,), 0, max(1, 128 // 4) + 1, jnp.int32)
        _lenS2 = 128 - jax.random.randint(jax.random.fold_in(_rk, 8), (16,), 0, max(1, 128 // 4) + 1, jnp.int32)
        _ctx_1024P = jax.random.normal(jax.random.fold_in(_rk, 11), (16, 16, 128), jnp.float32)
        _ctx_1024c = jax.random.dirichlet(jax.random.fold_in(_rk, 511), 0.3 * jnp.ones((16,), jnp.float32), (16, 128))
        _ctx_1024t = jnp.einsum('bsk,bkd->bsd', _ctx_1024c, _ctx_1024P)
        _ctx_1024t = _ctx_1024t * jax.lax.rsqrt(jnp.mean(jnp.square(_ctx_1024t)) + 1e-12) * 0.953939
        ctx_1024 = 2.81802e-05 + 1.00001 * (_ctx_1024t + 0.3 * jax.random.normal(jax.random.fold_in(_rk, 611), (16, 128, 128), jnp.float32))
        _validS = jnp.arange(128)[None, :] < _lenS[:, None]
        _validS2 = jnp.arange(128)[None, :] < _lenS2[:, None]
        _causal = jnp.tril(jnp.ones((128, 128), dtype=bool))
        mask_1x1xSxS2_ik0 = jnp.where(jnp.broadcast_to(_validS2[0:1, None, None, :], (1, 1, 128, 128)), 0, 1).astype(jnp.int32)
        _g = jax.random.normal(jax.random.fold_in(_rk, 9001), (2, 4), jnp.float32)
        _g = jnp.sign(_g) * jnp.maximum(jnp.abs(_g), 1.0) + (_g == 0) * 1.0
        g_xattn = _g[0]
        g_ffn = _g[1]
        return (x, ctx_1024, mask_1x1xSxS2_ik0, g_xattn, g_ffn)
    x, ctx_1024, mask_1x1xSxS2_ik0, g_xattn, g_ffn = _rec_inputs()

    def _L0_xattn_setup():
        import jax, jax.numpy as jnp
        import numpy as np
        B, L, D = (4, 512, 128)
        key = jax.random.key(seed)
        k1, k2 = jax.random.split(key)
        Q = jax.random.normal(k1, (B, L, D), dtype=jnp.float32)
        K = jax.random.normal(k2, (B, L, D), dtype=jnp.float32)
        return {'Q': Q, 'K': K}
    _L0_xattn_all = _L0_xattn_setup()
    _L0_xattn_in = {k: v for k, v in _L0_xattn_all.items() if k in ()}
    del _L0_xattn_all

    def _L0_ffn_setup():
        import jax, jax.numpy as jnp
        import numpy as np
        D_MODEL = 128
        HIDDEN = 256
        N_EXPERTS = 8
        TOP_K = 2
        key = jax.random.key(seed)
        ks = jax.random.split(key, 5)
        s_in = 1.0 / np.sqrt(D_MODEL)
        s_h = 1.0 / np.sqrt(HIDDEN)
        x = jax.random.normal(ks[0], (4, 256, D_MODEL), dtype=jnp.float32)
        Wr = jax.random.uniform(ks[1], (D_MODEL, N_EXPERTS), minval=-s_in, maxval=s_in, dtype=jnp.float32)
        Wg = jax.random.uniform(ks[2], (N_EXPERTS, D_MODEL, HIDDEN), minval=-s_in, maxval=s_in, dtype=jnp.float32)
        Wu = jax.random.uniform(ks[3], (N_EXPERTS, D_MODEL, HIDDEN), minval=-s_in, maxval=s_in, dtype=jnp.float32)
        Wd = jax.random.uniform(ks[4], (N_EXPERTS, HIDDEN, D_MODEL), minval=-s_h, maxval=s_h, dtype=jnp.float32)
        return {'x': x, 'Wr': Wr, 'Wg': Wg, 'Wu': Wu, 'Wd': Wd}
    _L0_ffn_all = _L0_ffn_setup()
    _L0_ffn_in = {k: v for k, v in _L0_ffn_all.items() if k in ('Wr', 'Wg', 'Wu', 'Wd')}
    del _L0_ffn_all

    def _L1_xattn_setup():
        import jax, jax.numpy as jnp
        import numpy as np
        B, LQ, LK = (8, 256, 256)
        HIST_DIM, COMB_DIM, FUSION_DIM = (128, 128, 128)

        def _linear_params(key, in_dim, out_dim):
            k1, k2 = jax.random.split(key)
            bound = 1.0 / np.sqrt(in_dim)
            W = jax.random.uniform(k1, (out_dim, in_dim), jnp.float32, -bound, bound)
            b = jax.random.uniform(k2, (out_dim,), jnp.float32, -bound, bound)
            return (W, b)

        def _lin(x, W, b):
            return jnp.einsum('bld,fd->blf', x, W) + b
        key = jax.random.key(seed)
        ks = jax.random.split(key, 8)
        hW, hb = _linear_params(ks[0], HIST_DIM, FUSION_DIM)
        cW, cb = _linear_params(ks[1], COMB_DIM, FUSION_DIM)
        qW, qb = _linear_params(ks[2], FUSION_DIM, FUSION_DIM)
        kW, kb = _linear_params(ks[3], FUSION_DIM, FUSION_DIM)
        vW, vb = _linear_params(ks[4], FUSION_DIM, FUSION_DIM)
        oW, ob = _linear_params(ks[5], FUSION_DIM, FUSION_DIM)
        return {'history_features': jax.random.normal(ks[6], (B, LQ, HIST_DIM), jnp.float32), 'combined_features': jax.random.normal(ks[7], (B, LK, COMB_DIM), jnp.float32), 'hW': hW, 'hb': hb, 'cW': cW, 'cb': cb, 'qW': qW, 'qb': qb, 'kW': kW, 'kb': kb, 'vW': vW, 'vb': vb, 'oW': oW, 'ob': ob}
    _L1_xattn_all = _L1_xattn_setup()
    _L1_xattn_in = {k: v for k, v in _L1_xattn_all.items() if k in ('hW', 'hb', 'cW', 'cb', 'qW', 'qb', 'kW', 'kb', 'vW', 'vb', 'oW', 'ob')}
    del _L1_xattn_all

    def _L1_ffn_setup():
        import jax, jax.numpy as jnp
        import numpy as np
        B, S, D = (1, 256, 128)
        E, F = (16, 128)
        NG, TKG, K = (4, 2, 4)
        NSH = 2
        SCALE = 2.5
        STD = 0.02
        EPG = E // NG

        def _route(x_flat, router_w, bias):
            logits = x_flat.astype(jnp.float32) @ router_w.T
            scores = jax.nn.sigmoid(logits)
            s = scores + bias[None, :]
            sg = s.reshape(-1, NG, EPG)
            group_score = jax.lax.top_k(sg, 2)[0].sum(-1)
            gidx = jax.lax.top_k(group_score, TKG)[1]
            gmask = jnp.sum(jax.nn.one_hot(gidx, NG, dtype=jnp.float32), axis=1) > 0
            emask = jnp.repeat(gmask, EPG, axis=1)
            masked = jnp.where(emask, s, -1.0)
            topk_idx = jax.lax.top_k(masked, K)[1]
            tw = jnp.take_along_axis(scores, topk_idx, axis=1)
            tw = tw / (tw.sum(-1, keepdims=True) + 1e-20)
            tw = tw * SCALE
            return (topk_idx, tw)
        key = jax.random.key(seed)
        ks = jax.random.split(key, 8)
        return {'hidden_states': jax.random.normal(ks[0], (B, S, D), jnp.float32), 'router_w': jax.random.normal(ks[1], (E, D), jnp.float32) * STD, 'bias': jnp.zeros((E,), jnp.float32), 'gate_w': jax.random.normal(ks[2], (E, D, F), jnp.float32) * STD, 'up_w': jax.random.normal(ks[3], (E, D, F), jnp.float32) * STD, 'down_w': jax.random.normal(ks[4], (E, F, D), jnp.float32) * STD, 'sh_gate_w': jax.random.normal(ks[5], (D, NSH * F), jnp.float32) * STD, 'sh_up_w': jax.random.normal(ks[6], (D, NSH * F), jnp.float32) * STD, 'sh_down_w': jax.random.normal(ks[7], (NSH * F, D), jnp.float32) * STD}
    _L1_ffn_all = _L1_ffn_setup()
    _L1_ffn_in = {k: v for k, v in _L1_ffn_all.items() if k in ('router_w', 'bias', 'gate_w', 'up_w', 'down_w', 'sh_gate_w', 'sh_up_w', 'sh_down_w')}
    del _L1_ffn_all

    def _L2_xattn_setup():
        import jax, jax.numpy as jnp
        import numpy as np
        import math
        B, S, D, H = (2, 256, 128, 16)
        DK = D // H

        def _split_heads(x):
            b, s, _ = x.shape
            return x.reshape(b, s, H, DK).transpose(0, 2, 1, 3)
        key = jax.random.key(seed)
        ks = jax.random.split(key, 12)
        xavier = math.sqrt(6.0 / (D + D))
        inp = {'query': jax.random.normal(ks[0], (B, S, D), jnp.float32), 'key': jax.random.normal(ks[1], (B, S, D), jnp.float32), 'value': jax.random.normal(ks[2], (B, S, D), jnp.float32), 'mask': jnp.tril(jnp.ones((S, S), jnp.int32))[None, None], 'Wq': jax.random.uniform(ks[3], (D, D), jnp.float32, -xavier, xavier), 'bq': jnp.zeros((D,), jnp.float32), 'Wk': jax.random.uniform(ks[4], (D, D), jnp.float32, -xavier, xavier), 'bk': jnp.zeros((D,), jnp.float32), 'Wv': jax.random.uniform(ks[5], (D, D), jnp.float32, -xavier, xavier), 'bv': jnp.zeros((D,), jnp.float32), 'Wo': jax.random.uniform(ks[6], (D, D), jnp.float32, -xavier, xavier), 'bo': jnp.zeros((D,), jnp.float32)}
        return inp
    _L2_xattn_all = _L2_xattn_setup()
    _L2_xattn_in = {k: v for k, v in _L2_xattn_all.items() if k in ('Wq', 'bq', 'Wk', 'bk', 'Wv', 'bv', 'Wo', 'bo')}
    del _L2_xattn_all

    def _L2_ffn_setup():
        import jax, jax.numpy as jnp
        import numpy as np
        D_MODEL = 128
        NUM_SLOTS = 64
        TOP_K = 8
        B, T = (4, 512)

        def _forward(x, slot_init, slot_scale, w1, b1, w2, b2, gru_wih, gru_whh, gru_bih, gru_bhh, wv, bv, wo, bo, tau):
            Bn, Tn, D = x.shape
            Sn = slot_init.shape[0]
            S = jnp.broadcast_to((slot_init * slot_scale)[None], (Bn, Sn, D)).astype(x.dtype)
            slot_mean = S.mean(axis=1, keepdims=True)
            ctx = jnp.concatenate([x, jnp.broadcast_to(slot_mean, x.shape)], axis=-1)
            h = jax.nn.gelu(ctx @ w1.T + b1, approximate=False)
            route_logits = (h @ w2.T + b2) / (jnp.abs(tau) + 0.1)
            topk_vals, topk_idx = jax.lax.top_k(route_logits, TOP_K)
            topk_w = jax.nn.softmax(topk_vals, axis=-1)
            alpha = jnp.sum(topk_w[..., None] * jax.nn.one_hot(topk_idx, Sn, dtype=x.dtype), axis=-2)
            slot_input = jnp.einsum('bts,btd->bsd', alpha, x)
            slot_wsum = alpha.sum(axis=1) + 1e-08
            gi = (slot_input / slot_wsum[..., None]).reshape(Bn * Sn, D)
            hs = S.reshape(Bn * Sn, D)
            gx = gi @ gru_wih.T + gru_bih
            gh = hs @ gru_whh.T + gru_bhh
            xr, xz, xn = jnp.split(gx, 3, axis=-1)
            hr, hz, hn = jnp.split(gh, 3, axis=-1)
            r = jax.nn.sigmoid(xr + hr)
            z = jax.nn.sigmoid(xz + hz)
            n = jnp.tanh(xn + r * hn)
            h_new = (1.0 - z) * n + z * hs
            S_new = h_new.reshape(Bn, Sn, D)
            slot_values = S_new @ wv.T + bv
            out = jnp.einsum('bts,bsd->btd', alpha, slot_values)
            return out @ wo.T + bo
        key = jax.random.key(seed)
        ks = jax.random.split(key, 16)
        D, S = (D_MODEL, NUM_SLOTS)
        H = D // 2
        sc = lambda fan_in: 1.0 / np.sqrt(fan_in)
        inp = {'x': jax.random.normal(ks[0], (B, T, D), dtype=jnp.float32), 'slot_init': jax.random.normal(ks[1], (S, D), dtype=jnp.float32) * 0.1, 'slot_scale': jnp.ones((S, 1), dtype=jnp.float32), 'w1': jax.random.normal(ks[2], (H, 2 * D), dtype=jnp.float32) * sc(2 * D), 'b1': jnp.zeros((H,), dtype=jnp.float32), 'w2': jax.random.normal(ks[3], (S, H), dtype=jnp.float32) * sc(H), 'b2': jnp.zeros((S,), dtype=jnp.float32), 'gru_wih': jax.random.normal(ks[4], (3 * D, D), dtype=jnp.float32) * sc(D), 'gru_whh': jax.random.normal(ks[5], (3 * D, D), dtype=jnp.float32) * sc(D), 'gru_bih': jnp.zeros((3 * D,), dtype=jnp.float32), 'gru_bhh': jnp.zeros((3 * D,), dtype=jnp.float32), 'wv': jax.random.normal(ks[6], (D, D), dtype=jnp.float32) * sc(D), 'bv': jnp.zeros((D,), dtype=jnp.float32), 'wo': jax.random.normal(ks[7], (D, D), dtype=jnp.float32) * sc(D), 'bo': jnp.zeros((D,), dtype=jnp.float32), 'tau': jnp.ones((1,), dtype=jnp.float32)}
        return inp
    _L2_ffn_all = _L2_ffn_setup()
    _L2_ffn_in = {k: v for k, v in _L2_ffn_all.items() if k in ('slot_init', 'slot_scale', 'w1', 'b1', 'w2', 'b2', 'gru_wih', 'gru_whh', 'gru_bih', 'gru_bhh', 'wv', 'bv', 'wo', 'bo', 'tau')}
    del _L2_ffn_all

    def _L3_xattn_setup():
        import jax, jax.numpy as jnp
        import numpy as np
        D_MODEL = 128
        N_HEADS = 16
        SCALES = (1, 2)
        D_K = D_MODEL // N_HEADS
        HPS = N_HEADS // len(SCALES)

        def _upsample_linear(x, target_len):
            b, h, l, d = x.shape
            if l == target_len:
                return x
            coords = (jnp.arange(target_len, dtype=jnp.float32) + 0.5) * (l / target_len) - 0.5
            coords = jnp.maximum(coords, 0.0)
            i0 = jnp.clip(jnp.floor(coords).astype(jnp.int32), 0, l - 1)
            i1 = jnp.minimum(i0 + 1, l - 1)
            w = (coords - i0.astype(jnp.float32))[None, None, :, None]
            return x[:, :, i0, :] * (1.0 - w) + x[:, :, i1, :] * w
        rng = jax.random.key(seed)
        ks = jax.random.split(rng, 7)
        B, S = (2, 256)
        s = 1.0 / np.sqrt(D_MODEL)
        mkw = lambda k: jax.random.normal(k, (D_MODEL, D_MODEL), jnp.float32) * s
        zb = jnp.zeros((D_MODEL,), jnp.float32)
        return {'query': jax.random.normal(ks[0], (B, S, D_MODEL), jnp.float32), 'key': jax.random.normal(ks[1], (B, S, D_MODEL), jnp.float32), 'value': jax.random.normal(ks[2], (B, S, D_MODEL), jnp.float32), 'w_q': mkw(ks[3]), 'b_q': zb, 'w_k': mkw(ks[4]), 'b_k': zb, 'w_v': mkw(ks[5]), 'b_v': zb, 'w_o': mkw(ks[6]), 'b_o': zb}
    _L3_xattn_all = _L3_xattn_setup()
    _L3_xattn_in = {k: v for k, v in _L3_xattn_all.items() if k in ('w_q', 'b_q', 'w_k', 'b_k', 'w_v', 'b_v', 'w_o', 'b_o')}
    del _L3_xattn_all

    def _L3_ffn_setup():
        import jax, jax.numpy as jnp
        import numpy as np
        E = 32
        H = 128
        I = 64
        G = 8
        TKG = 4
        TOPK = 8
        NSH = 2
        SCALE = 2.5
        key = jax.random.key(seed)
        ks = jax.random.split(key, 10)
        s = 0.02
        return {'hidden_states': jax.random.normal(ks[0], (2, 128, H), jnp.float32), 'gate_w': jax.random.normal(ks[1], (E, H), jnp.float32) * s, 'gate_bias': jax.random.normal(ks[2], (E,), jnp.float32) * s, 'w_gate': jax.random.normal(ks[3], (E, I, H), jnp.float32) * s, 'w_up': jax.random.normal(ks[4], (E, I, H), jnp.float32) * s, 'w_down': jax.random.normal(ks[5], (E, H, I), jnp.float32) * s, 'sh_gate': jax.random.normal(ks[6], (I * NSH, H), jnp.float32) * s, 'sh_up': jax.random.normal(ks[7], (I * NSH, H), jnp.float32) * s, 'sh_down': jax.random.normal(ks[8], (H, I * NSH), jnp.float32) * s}
    _L3_ffn_all = _L3_ffn_setup()
    _L3_ffn_in = {k: v for k, v in _L3_ffn_all.items() if k in ('gate_w', 'gate_bias', 'w_gate', 'w_up', 'w_down', 'sh_gate', 'sh_up', 'sh_down')}
    del _L3_ffn_all
    return {'x': x, 'ctx_1024': ctx_1024, 'mask_1x1xSxS2_ik0': mask_1x1xSxS2_ik0, 'g_xattn': g_xattn, 'g_ffn': g_ffn, 'L0_ffn_Wr': _L0_ffn_in['Wr'], 'L0_ffn_Wg': _L0_ffn_in['Wg'], 'L0_ffn_Wu': _L0_ffn_in['Wu'], 'L0_ffn_Wd': _L0_ffn_in['Wd'], 'L1_xattn_hW': _L1_xattn_in['hW'], 'L1_xattn_hb': _L1_xattn_in['hb'], 'L1_xattn_cW': _L1_xattn_in['cW'], 'L1_xattn_cb': _L1_xattn_in['cb'], 'L1_xattn_qW': _L1_xattn_in['qW'], 'L1_xattn_qb': _L1_xattn_in['qb'], 'L1_xattn_kW': _L1_xattn_in['kW'], 'L1_xattn_kb': _L1_xattn_in['kb'], 'L1_xattn_vW': _L1_xattn_in['vW'], 'L1_xattn_vb': _L1_xattn_in['vb'], 'L1_xattn_oW': _L1_xattn_in['oW'], 'L1_xattn_ob': _L1_xattn_in['ob'], 'L1_ffn_router_w': _L1_ffn_in['router_w'], 'L1_ffn_bias': _L1_ffn_in['bias'], 'L1_ffn_gate_w': _L1_ffn_in['gate_w'], 'L1_ffn_up_w': _L1_ffn_in['up_w'], 'L1_ffn_down_w': _L1_ffn_in['down_w'], 'L1_ffn_sh_gate_w': _L1_ffn_in['sh_gate_w'], 'L1_ffn_sh_up_w': _L1_ffn_in['sh_up_w'], 'L1_ffn_sh_down_w': _L1_ffn_in['sh_down_w'], 'L2_xattn_Wq': _L2_xattn_in['Wq'], 'L2_xattn_bq': _L2_xattn_in['bq'], 'L2_xattn_Wk': _L2_xattn_in['Wk'], 'L2_xattn_bk': _L2_xattn_in['bk'], 'L2_xattn_Wv': _L2_xattn_in['Wv'], 'L2_xattn_bv': _L2_xattn_in['bv'], 'L2_xattn_Wo': _L2_xattn_in['Wo'], 'L2_xattn_bo': _L2_xattn_in['bo'], 'L2_ffn_slot_init': _L2_ffn_in['slot_init'], 'L2_ffn_slot_scale': _L2_ffn_in['slot_scale'], 'L2_ffn_w1': _L2_ffn_in['w1'], 'L2_ffn_b1': _L2_ffn_in['b1'], 'L2_ffn_w2': _L2_ffn_in['w2'], 'L2_ffn_b2': _L2_ffn_in['b2'], 'L2_ffn_gru_wih': _L2_ffn_in['gru_wih'], 'L2_ffn_gru_whh': _L2_ffn_in['gru_whh'], 'L2_ffn_gru_bih': _L2_ffn_in['gru_bih'], 'L2_ffn_gru_bhh': _L2_ffn_in['gru_bhh'], 'L2_ffn_wv': _L2_ffn_in['wv'], 'L2_ffn_bv': _L2_ffn_in['bv'], 'L2_ffn_wo': _L2_ffn_in['wo'], 'L2_ffn_bo': _L2_ffn_in['bo'], 'L2_ffn_tau': _L2_ffn_in['tau'], 'L3_xattn_w_q': _L3_xattn_in['w_q'], 'L3_xattn_b_q': _L3_xattn_in['b_q'], 'L3_xattn_w_k': _L3_xattn_in['w_k'], 'L3_xattn_b_k': _L3_xattn_in['b_k'], 'L3_xattn_w_v': _L3_xattn_in['w_v'], 'L3_xattn_b_v': _L3_xattn_in['b_v'], 'L3_xattn_w_o': _L3_xattn_in['w_o'], 'L3_xattn_b_o': _L3_xattn_in['b_o'], 'L3_ffn_gate_w': _L3_ffn_in['gate_w'], 'L3_ffn_gate_bias': _L3_ffn_in['gate_bias'], 'L3_ffn_w_gate': _L3_ffn_in['w_gate'], 'L3_ffn_w_up': _L3_ffn_in['w_up'], 'L3_ffn_w_down': _L3_ffn_in['w_down'], 'L3_ffn_sh_gate': _L3_ffn_in['sh_gate'], 'L3_ffn_sh_up': _L3_ffn_in['sh_up'], 'L3_ffn_sh_down': _L3_ffn_in['sh_down']}

def reference(x, ctx_1024, mask_1x1xSxS2_ik0, g_xattn, g_ffn, L0_ffn_Wr, L0_ffn_Wg, L0_ffn_Wu, L0_ffn_Wd, L1_xattn_hW, L1_xattn_hb, L1_xattn_cW, L1_xattn_cb, L1_xattn_qW, L1_xattn_qb, L1_xattn_kW, L1_xattn_kb, L1_xattn_vW, L1_xattn_vb, L1_xattn_oW, L1_xattn_ob, L1_ffn_router_w, L1_ffn_bias, L1_ffn_gate_w, L1_ffn_up_w, L1_ffn_down_w, L1_ffn_sh_gate_w, L1_ffn_sh_up_w, L1_ffn_sh_down_w, L2_xattn_Wq, L2_xattn_bq, L2_xattn_Wk, L2_xattn_bk, L2_xattn_Wv, L2_xattn_bv, L2_xattn_Wo, L2_xattn_bo, L2_ffn_slot_init, L2_ffn_slot_scale, L2_ffn_w1, L2_ffn_b1, L2_ffn_w2, L2_ffn_b2, L2_ffn_gru_wih, L2_ffn_gru_whh, L2_ffn_gru_bih, L2_ffn_gru_bhh, L2_ffn_wv, L2_ffn_bv, L2_ffn_wo, L2_ffn_bo, L2_ffn_tau, L3_xattn_w_q, L3_xattn_b_q, L3_xattn_w_k, L3_xattn_b_k, L3_xattn_w_v, L3_xattn_b_v, L3_xattn_w_o, L3_xattn_b_o, L3_ffn_gate_w, L3_ffn_gate_bias, L3_ffn_w_gate, L3_ffn_w_up, L3_ffn_w_down, L3_ffn_sh_gate, L3_ffn_sh_up, L3_ffn_sh_down):
    import jax
    import jax.numpy as jnp

    def _L0_xattn_ref(Q, K):
        import jax, jax.numpy as jnp
        import numpy as np
        B, L, D = (4, 512, 128)
        scores = jnp.einsum('btd,bsd->bts', K, K)
        Lq = Q.shape[1]
        mask = jnp.tril(jnp.ones((Lq, Lq), dtype=scores.dtype))
        scores = scores * mask[None, :, :]
        Q_proj = jnp.einsum('bts,bsd->btd', scores, Q)
        return Q + Q_proj

    def _L0_ffn_ref(x, Wr, Wg, Wu, Wd):
        import jax, jax.numpy as jnp
        import numpy as np
        D_MODEL = 128
        HIDDEN = 256
        N_EXPERTS = 8
        TOP_K = 2
        bsz, seq_len, d_model = x.shape
        flat = x.reshape(-1, d_model)
        logits = flat @ Wr
        topk_vals, topk_idx = jax.lax.top_k(logits, TOP_K)
        topk_w = jax.nn.softmax(topk_vals, axis=-1)
        combine = jnp.sum(jax.nn.one_hot(topk_idx, N_EXPERTS, dtype=flat.dtype) * topk_w[..., None], axis=1)
        out = jnp.zeros_like(flat)
        for e in range(N_EXPERTS):
            g = flat @ Wg[e]
            u = flat @ Wu[e]
            y = jax.nn.silu(g) * u @ Wd[e]
            out = out + y * combine[:, e:e + 1]
        return out.reshape(bsz, seq_len, d_model)

    def _L1_xattn_ref(history_features, combined_features, hW, hb, cW, cb, qW, qb, kW, kb, vW, vb, oW, ob):
        import jax, jax.numpy as jnp
        import numpy as np
        B, LQ, LK = (8, 256, 256)
        HIST_DIM, COMB_DIM, FUSION_DIM = (128, 128, 128)

        def _linear_params(key, in_dim, out_dim):
            k1, k2 = jax.random.split(key)
            bound = 1.0 / np.sqrt(in_dim)
            W = jax.random.uniform(k1, (out_dim, in_dim), jnp.float32, -bound, bound)
            b = jax.random.uniform(k2, (out_dim,), jnp.float32, -bound, bound)
            return (W, b)

        def _lin(x, W, b):
            return jnp.einsum('bld,fd->blf', x, W) + b
        h = _lin(history_features, hW, hb)
        c = _lin(combined_features, cW, cb)
        q = _lin(h, qW, qb)
        k = _lin(c, kW, kb)
        v = _lin(c, vW, vb)
        scale = 1.0 / jnp.sqrt(jnp.float32(FUSION_DIM))
        scores = jnp.einsum('bqf,bkf->bqk', q, k) * scale
        attn = jax.nn.softmax(scores, axis=-1)
        attn_out = jnp.einsum('bqk,bkf->bqf', attn, v)
        return _lin(attn_out + q, oW, ob)

    def _L1_ffn_ref(hidden_states, router_w, bias, gate_w, up_w, down_w, sh_gate_w, sh_up_w, sh_down_w):
        import jax, jax.numpy as jnp
        import numpy as np
        B, S, D = (1, 256, 128)
        E, F = (16, 128)
        NG, TKG, K = (4, 2, 4)
        NSH = 2
        SCALE = 2.5
        STD = 0.02
        EPG = E // NG

        def _route(x_flat, router_w, bias):
            logits = x_flat.astype(jnp.float32) @ router_w.T
            scores = jax.nn.sigmoid(logits)
            s = scores + bias[None, :]
            sg = s.reshape(-1, NG, EPG)
            group_score = jax.lax.top_k(sg, 2)[0].sum(-1)
            gidx = jax.lax.top_k(group_score, TKG)[1]
            gmask = jnp.sum(jax.nn.one_hot(gidx, NG, dtype=jnp.float32), axis=1) > 0
            emask = jnp.repeat(gmask, EPG, axis=1)
            masked = jnp.where(emask, s, -1.0)
            topk_idx = jax.lax.top_k(masked, K)[1]
            tw = jnp.take_along_axis(scores, topk_idx, axis=1)
            tw = tw / (tw.sum(-1, keepdims=True) + 1e-20)
            tw = tw * SCALE
            return (topk_idx, tw)
        x = hidden_states.reshape(-1, D)
        topk_idx, tw = _route(x, router_w, bias)
        combine = (jax.nn.one_hot(topk_idx, E, dtype=tw.dtype) * tw[..., None]).sum(1)
        h = jnp.einsum('td,edf->etf', x, gate_w)
        u = jnp.einsum('td,edf->etf', x, up_w)
        y = jnp.einsum('etf,efd->etd', jax.nn.silu(h) * u, down_w)
        routed = jnp.einsum('etd,te->td', y, combine)
        sh = jax.nn.silu(x @ sh_gate_w) * (x @ sh_up_w) @ sh_down_w
        return (routed + sh).reshape(hidden_states.shape)

    def _L2_xattn_ref(query, key, value, mask, Wq, bq, Wk, bk, Wv, bv, Wo, bo):
        import jax, jax.numpy as jnp
        import numpy as np
        import math
        B, S, D, H = (2, 256, 128, 16)
        DK = D // H

        def _split_heads(x):
            b, s, _ = x.shape
            return x.reshape(b, s, H, DK).transpose(0, 2, 1, 3)
        q = _split_heads(query @ Wq.T + bq)
        k = _split_heads(key @ Wk.T + bk)
        v = _split_heads(value @ Wv.T + bv)
        scale = 1.0 / math.sqrt(DK)
        scores = jnp.einsum('bhqd,bhkd->bhqk', q, k) * scale
        scores = jnp.where(mask == 0, jnp.float32(-1000000000.0), scores)
        attn = jax.nn.softmax(scores, axis=-1)
        out = jnp.einsum('bhqk,bhkd->bhqd', attn, v)
        out = out.transpose(0, 2, 1, 3).reshape(query.shape[0], -1, D)
        return out @ Wo.T + bo

    def _L2_ffn_ref(x, slot_init, slot_scale, w1, b1, w2, b2, gru_wih, gru_whh, gru_bih, gru_bhh, wv, bv, wo, bo, tau):
        import jax, jax.numpy as jnp
        import numpy as np
        D_MODEL = 128
        NUM_SLOTS = 64
        TOP_K = 8
        B, T = (4, 512)

        def _forward(x, slot_init, slot_scale, w1, b1, w2, b2, gru_wih, gru_whh, gru_bih, gru_bhh, wv, bv, wo, bo, tau):
            Bn, Tn, D = x.shape
            Sn = slot_init.shape[0]
            S = jnp.broadcast_to((slot_init * slot_scale)[None], (Bn, Sn, D)).astype(x.dtype)
            slot_mean = S.mean(axis=1, keepdims=True)
            ctx = jnp.concatenate([x, jnp.broadcast_to(slot_mean, x.shape)], axis=-1)
            h = jax.nn.gelu(ctx @ w1.T + b1, approximate=False)
            route_logits = (h @ w2.T + b2) / (jnp.abs(tau) + 0.1)
            topk_vals, topk_idx = jax.lax.top_k(route_logits, TOP_K)
            topk_w = jax.nn.softmax(topk_vals, axis=-1)
            alpha = jnp.sum(topk_w[..., None] * jax.nn.one_hot(topk_idx, Sn, dtype=x.dtype), axis=-2)
            slot_input = jnp.einsum('bts,btd->bsd', alpha, x)
            slot_wsum = alpha.sum(axis=1) + 1e-08
            gi = (slot_input / slot_wsum[..., None]).reshape(Bn * Sn, D)
            hs = S.reshape(Bn * Sn, D)
            gx = gi @ gru_wih.T + gru_bih
            gh = hs @ gru_whh.T + gru_bhh
            xr, xz, xn = jnp.split(gx, 3, axis=-1)
            hr, hz, hn = jnp.split(gh, 3, axis=-1)
            r = jax.nn.sigmoid(xr + hr)
            z = jax.nn.sigmoid(xz + hz)
            n = jnp.tanh(xn + r * hn)
            h_new = (1.0 - z) * n + z * hs
            S_new = h_new.reshape(Bn, Sn, D)
            slot_values = S_new @ wv.T + bv
            out = jnp.einsum('bts,bsd->btd', alpha, slot_values)
            return out @ wo.T + bo
        return _forward(x, slot_init, slot_scale, w1, b1, w2, b2, gru_wih, gru_whh, gru_bih, gru_bhh, wv, bv, wo, bo, tau)

    def _L3_xattn_ref(query, key, value, w_q, b_q, w_k, b_k, w_v, b_v, w_o, b_o):
        import jax, jax.numpy as jnp
        import numpy as np
        D_MODEL = 128
        N_HEADS = 16
        SCALES = (1, 2)
        D_K = D_MODEL // N_HEADS
        HPS = N_HEADS // len(SCALES)

        def _upsample_linear(x, target_len):
            b, h, l, d = x.shape
            if l == target_len:
                return x
            coords = (jnp.arange(target_len, dtype=jnp.float32) + 0.5) * (l / target_len) - 0.5
            coords = jnp.maximum(coords, 0.0)
            i0 = jnp.clip(jnp.floor(coords).astype(jnp.int32), 0, l - 1)
            i1 = jnp.minimum(i0 + 1, l - 1)
            w = (coords - i0.astype(jnp.float32))[None, None, :, None]
            return x[:, :, i0, :] * (1.0 - w) + x[:, :, i1, :] * w
        B, S, _ = query.shape
        inv_scale = 1.0 / np.sqrt(D_K).astype(np.float32)

        def proj(x, W, b):
            return (x @ W + b).reshape(B, S, N_HEADS, D_K).transpose(0, 2, 1, 3)
        Q = proj(query, w_q, b_q)
        K = proj(key, w_k, b_k)
        V = proj(value, w_v, b_v)
        outs = []
        for i, f in enumerate(SCALES):
            hs = slice(i * HPS, (i + 1) * HPS)
            Qd = Q[:, hs, ::f]
            Kd = K[:, hs, ::f]
            Vd = V[:, hs, ::f]
            scores = jnp.einsum('bhqd,bhkd->bhqk', Qd, Kd) * inv_scale
            attn = jax.nn.softmax(scores, axis=-1)
            o = jnp.einsum('bhqk,bhkd->bhqd', attn, Vd)
            outs.append(_upsample_linear(o, S))
        out = jnp.concatenate(outs, axis=1)
        out = out.transpose(0, 2, 1, 3).reshape(B, S, D_MODEL)
        return out @ w_o + b_o

    def _L3_ffn_ref(hidden_states, gate_w, gate_bias, w_gate, w_up, w_down, sh_gate, sh_up, sh_down):
        import jax, jax.numpy as jnp
        import numpy as np
        E = 32
        H = 128
        I = 64
        G = 8
        TKG = 4
        TOPK = 8
        NSH = 2
        SCALE = 2.5
        B, S, Hd = hidden_states.shape
        h = hidden_states.reshape(-1, Hd)
        logits = h.astype(jnp.float32) @ gate_w.T
        scores = jax.nn.sigmoid(logits)
        sc = scores + gate_bias
        grp = sc.reshape(-1, G, E // G)
        group_scores = jax.lax.top_k(grp, 2)[0].sum(-1)
        gidx = jax.lax.top_k(group_scores, TKG)[1]
        gmask = jnp.sum(jax.nn.one_hot(gidx, G, dtype=sc.dtype), axis=1)
        smask = jnp.repeat(gmask, E // G, axis=1)
        masked = jnp.where(smask > 0, sc, jnp.zeros_like(sc))
        tki = jax.lax.top_k(masked, TOPK)[1]
        tkw = jnp.take_along_axis(scores, tki, axis=1)
        tkw = tkw / (tkw.sum(-1, keepdims=True) + 1e-20)
        tkw = tkw * SCALE
        combine = (jax.nn.one_hot(tki, E, dtype=tkw.dtype) * tkw[..., None]).sum(1)
        g = jax.nn.silu(jnp.einsum('th,eih->tei', h, w_gate))
        u = jnp.einsum('th,eih->tei', h, w_up)
        routed = jnp.einsum('tei,ehi->th', g * u * combine[:, :, None], w_down)
        sg = jax.nn.silu(h @ sh_gate.T)
        shared = sg * (h @ sh_up.T) @ sh_down.T
        return (routed + shared).reshape(B, S, Hd)
    x = x + jnp.tanh(g_xattn[0]) * _L0_xattn_ref(_layernorm(x, axis=-1), ctx_1024)
    x = x + jnp.tanh(g_ffn[0]) * _L0_ffn_ref(_layernorm(x, axis=-1), L0_ffn_Wr, L0_ffn_Wg, L0_ffn_Wu, L0_ffn_Wd)
    x = x + jnp.tanh(g_xattn[1]) * _L1_xattn_ref(_layernorm(x, axis=-1), ctx_1024, L1_xattn_hW, L1_xattn_hb, L1_xattn_cW, L1_xattn_cb, L1_xattn_qW, L1_xattn_qb, L1_xattn_kW, L1_xattn_kb, L1_xattn_vW, L1_xattn_vb, L1_xattn_oW, L1_xattn_ob)
    x = x + jnp.tanh(g_ffn[1]) * _L1_ffn_ref(_layernorm(x, axis=-1), L1_ffn_router_w, L1_ffn_bias, L1_ffn_gate_w, L1_ffn_up_w, L1_ffn_down_w, L1_ffn_sh_gate_w, L1_ffn_sh_up_w, L1_ffn_sh_down_w)
    x = x + jnp.tanh(g_xattn[2]) * _L2_xattn_ref(_layernorm(x, axis=-1), ctx_1024, ctx_1024, mask_1x1xSxS2_ik0, L2_xattn_Wq, L2_xattn_bq, L2_xattn_Wk, L2_xattn_bk, L2_xattn_Wv, L2_xattn_bv, L2_xattn_Wo, L2_xattn_bo)
    x = x + jnp.tanh(g_ffn[2]) * _L2_ffn_ref(_layernorm(x, axis=-1), L2_ffn_slot_init, L2_ffn_slot_scale, L2_ffn_w1, L2_ffn_b1, L2_ffn_w2, L2_ffn_b2, L2_ffn_gru_wih, L2_ffn_gru_whh, L2_ffn_gru_bih, L2_ffn_gru_bhh, L2_ffn_wv, L2_ffn_bv, L2_ffn_wo, L2_ffn_bo, L2_ffn_tau)
    x = x + jnp.tanh(g_xattn[3]) * _L3_xattn_ref(_layernorm(x, axis=-1), ctx_1024, ctx_1024, L3_xattn_w_q, L3_xattn_b_q, L3_xattn_w_k, L3_xattn_b_k, L3_xattn_w_v, L3_xattn_b_v, L3_xattn_w_o, L3_xattn_b_o)
    x = x + jnp.tanh(g_ffn[3]) * _L3_ffn_ref(_layernorm(x, axis=-1), L3_ffn_gate_w, L3_ffn_gate_bias, L3_ffn_w_gate, L3_ffn_w_up, L3_ffn_w_down, L3_ffn_sh_gate, L3_ffn_sh_up, L3_ffn_sh_down)
    return x

_drawn_inputs = setup_inputs


def setup_inputs(seed=0):
    import zlib

    import numpy as np

    out = dict(_drawn_inputs(seed))
    spreads = {'L1_ffn_bias': (0.0, 2.0),
     'L2_xattn_bq': (0.0, 0.1),
     'L2_xattn_bk': (0.0, 0.1),
     'L2_xattn_bv': (0.0, 0.8),
     'L2_xattn_bo': (0.0, 2.0),
     'L2_ffn_slot_scale': (1.0, 0.6),
     'L2_ffn_b1': (0.0, 0.8),
     'L2_ffn_b2': (0.0, 2.0),
     'L2_ffn_gru_bih': (0.0, 0.8),
     'L2_ffn_gru_bhh': (0.0, 0.8),
     'L2_ffn_bv': (0.0, 2.0),
     'L2_ffn_bo': (0.0, 2.0),
     'L3_xattn_b_q': (0.0, 0.8),
     'L3_xattn_b_k': (0.0, 2.0),
     'L3_xattn_b_v': (0.0, 2.0),
     'L3_xattn_b_o': (0.0, 2.0)}
    factors = {'g_ffn': 8.0,
     'L0_ffn_Wr': 8.0,
     'L0_ffn_Wg': 8.0,
     'L0_ffn_Wu': 8.0,
     'L0_ffn_Wd': 8.0,
     'L1_xattn_hW': 8.0,
     'L1_xattn_hb': 8.0,
     'L1_xattn_cW': 8.0,
     'L1_xattn_cb': 8.0,
     'L1_xattn_qW': 8.0,
     'L1_xattn_qb': 8.0,
     'L1_xattn_kW': 8.0,
     'L1_xattn_kb': 64.0,
     'L1_xattn_vW': 8.0,
     'L1_xattn_vb': 52.344,
     'L1_xattn_oW': 8.0,
     'L1_xattn_ob': 64.0,
     'L1_ffn_router_w': 8.0,
     'L1_ffn_gate_w': 8.0,
     'L1_ffn_up_w': 8.0,
     'L1_ffn_down_w': 8.0,
     'L1_ffn_sh_gate_w': 8.0,
     'L1_ffn_sh_up_w': 8.0,
     'L1_ffn_sh_down_w': 8.0,
     'L2_xattn_Wv': 8.0,
     'L2_xattn_Wo': 8.0,
     'L2_ffn_slot_init': 8.0,
     'L2_ffn_w1': 8.0,
     'L2_ffn_w2': 8.0,
     'L2_ffn_gru_wih': 8.0,
     'L2_ffn_gru_whh': 8.0,
     'L2_ffn_wv': 8.0,
     'L2_ffn_wo': 8.0,
     'L3_xattn_w_q': 8.0,
     'L3_xattn_w_k': 8.0,
     'L3_xattn_w_v': 8.0,
     'L3_xattn_w_o': 8.0,
     'L3_ffn_gate_w': 64.0,
     'L3_ffn_gate_bias': 64.0,
     'L3_ffn_w_gate': 64.0,
     'L3_ffn_w_up': 60.038,
     'L3_ffn_w_down': 60.805,
     'L3_ffn_sh_gate': 41.247,
     'L3_ffn_sh_up': 37.518,
     'L3_ffn_sh_down': 36.631}
    for name, (base, spread) in spreads.items():
        noise = np.random.default_rng([zlib.crc32(name.encode()), seed]).standard_normal(out[name].shape)
        drawn = base * np.exp(spread * noise) if base else spread * noise
        out[name] = jnp.asarray(drawn.astype(out[name].dtype))
    for name, factor in factors.items():
        out[name] = (out[name] * factor).astype(out[name].dtype)
    return out
```

```python
from contextlib import ExitStack

import numpy as np

import concourse.bass as bass
from concourse import mybir

F32 = mybir.dt.float32
BF16 = mybir.dt.bfloat16
I32 = mybir.dt.int32
ALU = mybir.AluOpType
ACT = mybir.ActivationFunctionType
AX = mybir.AxisListType

P = 128
NB = 16
GB = 4
NG = NB // GB
TG = GB * P
PHASES = 8
LN_EPS = 1e-5
LOWEST = -3.0e38
TAKEN = 3.0e38
MASKED = -1.0e30

HEADS, DK = 16, 8
HEAD_TILES = 4
VW = DK + 1
HALF = P // 2

SLOTS = 64
SLOT_HID = 64
SLOT_TOP = 8

MOE = {
    1: dict(E=8, F=256, SH=0, K=2, GK=0),
    3: dict(E=16, F=128, SH=256, K=4, GK=2),
    7: dict(E=32, F=64, SH=128, K=8, GK=4),
}
for _m in MOE.values():
    _m["NR"] = _m["E"] * _m["F"] // P
    _m["NC"] = _m["NR"] + _m["SH"] // P
    _m["EG"] = 4
SCALE_ROUTED = 2.5
TURN = 6
RING = TURN + 2

SMALL = dict(
    gates=(P, PHASES),
    hW=(P, P), qWT=(P, P), cW=(P, P), kWT=(P, P), vWT=(P, P), oWT=(P, P),
    hb=(P, 1), qb=(P, 1), cb=(P, 1), kb=(P, 1), vb=(P, 1), ob=(P, 1),
    Wr1=(P, 8), Wr3=(P, 16), Wr7=(P, 32), rb3=(P, 16), rb7=(P, 32),
    Wq4=(P, HEAD_TILES * P), Wk4=(P, HEAD_TILES * P), Wv4=(P, P), Wo4=(P, P),
    bq4=(P, HEAD_TILES), bk4=(P, HEAD_TILES), bv4=(P, 1), bo4=(P, 1),
    Wq6=(P, HEAD_TILES * P), Wk6=(P, HEAD_TILES * P), Wv6=(P, P), Wo6=(P, P),
    bq6=(P, HEAD_TILES), bk6=(P, HEAD_TILES), bv6=(P, 1), bo6=(P, 1),
    slot_init=(SLOTS, P), slot_scale=(SLOTS, 1), w1x=(P, SLOT_HID), w1m=(P, SLOT_HID),
    b1=(SLOT_HID, 1), w2=(SLOT_HID + 1, SLOTS), wih=(P, 3 * P), whh=(P, 3 * P),
    bih=(P, 3), bhh=(P, 3), wv=(P, P), woT=(P, P), bv5=(P, 1), bo5=(P, 1), tau=(P, 1),
)
CONST = dict(ident=(P, P), causal=(P, P), up=(HALF, P))


def columns(table):
    at, n = {}, 0
    for name, (rows, cols) in table.items():
        at[name] = (rows, n, cols)
        n += cols
    return at, n


SMALL_AT, SMALL_N = columns(SMALL)
CONST_AT, CONST_N = columns(CONST)
SEL_AT, SEL_N = {}, P
for _p, _m in MOE.items():
    SEL_AT[_p] = SEL_N
    SEL_N += _m["NR"] * P


class Steps:

    def __init__(self, eng, sem):
        self.eng, self.sem, self.n = eng, sem, 0

    def add(self, instruction):
        instruction.then_inc(self.sem, 1)
        self.n += 1
        return self.n

    def settle(self, n=None):
        self.eng.wait_ge(self.sem, self.n if n is None else n)

    def restart(self):
        if self.n:
            self.settle()
        self.eng.sem_clear(self.sem)
        self.n = 0


def build(nc, small_d, const_d, constb_d, x_d, ctx_d, mask_d, moe_d, out_d, phases=PHASES):
    last = NG * phases
    with ExitStack() as ctx:
        def sb(name, shape, dt=F32):
            return ctx.enter_context(nc.sbuf_tensor(name, shape, dt))

        sems = {}

        def sem(name):
            if name not in sems:
                sems[name] = ctx.enter_context(nc.semaphore(name))
            return sems[name]

        T = ctx.enter_context(nc.psum_tensor("T", [P, TG], F32))
        Y = ctx.enter_context(nc.psum_tensor("Y", [P, TG], F32))
        B = [ctx.enter_context(nc.psum_tensor(f"B{i}", [P, TG], F32)) for i in range(6)]

        X = sb("X", [P, NB * P])
        CT = sb("CT", [P, NB * P])
        small = sb("small", [P, SMALL_N])
        const = sb("const", [P, CONST_N])
        constb = sb("constb", [P, SEL_N], BF16)
        mask_i = sb("mask_i", [P, P], I32)
        moe_w = {p: [sb(f"moe{p}_{n}", [P, m["NC"] * P]) for n in ("gate", "up", "down")]
                 for p, m in MOE.items()}

        def S(name, a=0, b=None):
            rows, at, cols = SMALL_AT[name]
            return small[0:rows, at + a:at + (cols if b is None else b)]

        def K(name):
            rows, at, cols = CONST_AT[name]
            return const[0:rows, at:at + cols]

        ident = K("ident")
        identb = constb[:, 0:P]

        xhat = [sb(f"xhat{i}", [P, TG]) for i in range(2)]
        xhat_t = [sb(f"xhat_t{i}", [P, TG]) for i in range(2)]
        cg = [sb(f"cg{i}", [P, TG]) for i in range(2)]
        ysb = sb("ysb", [P, TG])
        tgate = sb("tgate", [P, PHASES])
        ybias = sb("ybias", [P, PHASES])

        stats = sb("stats", [P, GB, 6])
        mv = sb("mv", [P, GB, 2])
        var = sb("var", [P, GB])
        rstd = sb("rstd", [P, GB])
        minus_half = sb("minus_half", [P, GB])

        shared = sb("shared", [P, 19 * TG])

        class Area:
            def __init__(self):
                self.at = 0

            def tile(self, shape):
                n = int(np.prod(shape[1:]))
                a = shared[0:shape[0], self.at:self.at + n]
                self.at += n
                assert self.at <= 19 * TG
                if len(shape) == 3:
                    a = a.rearrange("p (a b) -> p a b", a=shape[1])
                elif len(shape) == 4:
                    a = a.rearrange("p (a b c) -> p a b c", a=shape[1], b=shape[2])
                return a

        def token_tile(g, j):
            return X[:, bass.ds(g * TG + j * P, P)]

        def norm(dve, st, g, s):
            s, h = s
            for j in range(GB):
                st.add(nc.vector.bn_stats(out=stats[:, j, :], in_=token_tile(g, j)))
            st.settle()
            for j in range(GB):
                st.add(nc.vector.bn_aggr(out=mv[:, j, :], in_=stats[:, j, :]))
            st.settle()
            nc.vector.tensor_scalar(var[:], mv[:, :, 1], LN_EPS, None, ALU.add).then_inc(sem("var_ready"), 1)
            dve.wait_ge(sem("rstd_ready"), s + 2)
            for j in range(GB):
                ins = nc.vector.tensor_scalar(xhat[h][:, j * P:(j + 1) * P], token_tile(g, j),
                                              mv[:, j, 0:1], rstd[:, j:j + 1], ALU.subtract, ALU.mult)
            ins.then_inc(sem("xhat_ready"), 1)

        def finish_dve(dve, g, s):
            dve.wait_ge(sem("yt_ready"), s)
            nc.vector.tensor_tensor(X[:, bass.ds(g * TG, TG)], X[:, bass.ds(g * TG, TG)], T[:],
                                    ALU.add).then_inc(sem("x_updated"), 1)
            dve.wait_ge(sem("x_updated"), s)

        def finish_pe(pe, s):
            pe.wait_ge(sem("xhat_t_ready"), s + 1)
            pe.wait_ge(sem("ysb_ready"), s)
            for j in range(GB):
                ins = nc.tensor.transpose(T[:, j * P:(j + 1) * P], ysb[:, j * P:(j + 1) * P], ident)
            ins.then_inc(sem("yt_ready"), 1)

        def norm_pe(pe, s, h):
            pe.wait_ge(sem("xhat_ready"), s + 1)
            if not isinstance(s, int) or s > 1:
                pe.wait_ge(sem("x_updated"), s - 1)
            elif s == 1:
                pe.wait_ge(sem("xhat_t_ready"), s)
            for j in range(GB):
                ins = nc.tensor.transpose(T[:, j * P:(j + 1) * P], xhat[h][:, j * P:(j + 1) * P], ident)
            ins.then_inc(sem("xt_ready"), 1)

        def norm_act(act, s, h):
            act.wait_ge(sem("xt_ready"), s + 1)
            nc.scalar.copy(xhat_t[h][:], T[:]).then_inc(sem("xhat_t_ready"), 1)

        def result_act(act, p, s):
            act.wait_ge(sem("y_ready"), s + 1)
            if not isinstance(s, int) or s > 0:
                act.wait_ge(sem("yt_ready"), s)
            nc.scalar.activation(ysb[:], Y[:], ACT.Identity, bias=ybias[:, p:p + 1],
                                 scale=tgate[:, p:p + 1]).then_inc(sem("ysb_ready"), 1)

        def stages(eng, p, st=None):
            if st:
                st.restart()
            with eng.Fori(0, NG // 2) as r:
                for g, before, after, h in ((2 * r, r * -2 + 3, 2 * r + 1, 0), (2 * r + 1, 2 * r, r * -2 + 2, 1)):
                    yield g, before, after, h
                    if st:
                        st.restart()

        sm = [sb(f"sm{i}", [P, TG]) for i in range(2)]

        def p0_pe(pe):
            pe.wait_ge(sem("ctx_loaded"), 16)
            for g in range(NG):
                h = g % 2
                if g >= 2:
                    pe.wait_ge(sem("p0_masked"), g - 1)
                for j in range(GB):
                    kt = CT[:, g * TG + j * P:g * TG + (j + 1) * P]
                    ins = nc.tensor.matmul(B[h][:, j * P:(j + 1) * P], kt, kt, start=True, stop=True)
                ins.then_inc(sem("p0_scores"), 1)
                if g > 0:
                    finish_pe(pe, g)
                pe.wait_ge(sem("p0_masked"), g + 1)
                pe.wait_ge(sem("xhat_ready"), g + 1)
                if g > 0:
                    pe.wait_ge(sem("ysb_ready"), g)
                for j in range(GB):
                    o, q = Y[:, j * P:(j + 1) * P], xhat[h][:, j * P:(j + 1) * P]
                    nc.tensor.matmul(o, q, sm[h][:, j * P:(j + 1) * P], start=True, stop=False)
                    ins = nc.tensor.matmul(o, q, ident, start=False, stop=True)
                ins.then_inc(sem("y_ready"), 1)
                norm_pe(pe, g + 1, 1 - h)

        def p0_dve(dve, st):
            for g in range(NG):
                h = g % 2
                st.restart()
                dve.wait_ge(sem("p0_scores"), g + 1)
                if g >= 2:
                    dve.wait_ge(sem("y_ready"), g - 1)
                nc.vector.tensor_tensor(
                    sm[h][:].rearrange("p (j t) -> p j t", j=GB),
                    B[h][:].rearrange("p (j t) -> p j t", j=GB),
                    K("causal").unsqueeze(1).to_broadcast([P, GB, P]), ALU.mult).then_inc(sem("p0_masked"), 1)
                if g > 0:
                    finish_dve(dve, g - 1, g)
                norm(dve, st, (g + 1) % NG, (g + 1, 1 - h))

        def p0_act(act):
            for g in range(NG):
                result_act(act, 0, g)
                norm_act(act, g + 1, (g + 1) % 2)

        wqh = sb("wqh", [P, P])
        wkc = sb("wkc", [P, P])
        wvc = sb("wvc", [P, P])
        wvo = sb("wvo", [P, P])
        bcols = sb("bcols", [P, 16])
        slots = sb("slots", [SLOTS, P])
        mean_w = sb("mean_w", [SLOTS, 1])
        hs_t = sb("hs_t", [P, SLOTS])
        mean_t = sb("mean_t", [P, 1])
        b1x = sb("b1x", [SLOT_HID, 1])
        gh_rz = sb("gh_rz", [P, 2, SLOTS])
        gh_n = sb("gh_n", [P, SLOTS])
        brz = sb("brz", [P, 2])
        rtau = sb("rtau", [P, 1])
        maskb = sb("maskb", [P, GB, P], BF16)
        mtmp = sb("mtmp", [P, P])

        def setup_pe(pe):
            pe.wait_ge(sem("small_loaded"), 16)
            mm = nc.tensor.matmul
            mm(B[2][:, 0:P], S("hW"), S("qWT"), start=True, stop=True)
            mm(B[2][:, P:2 * P], S("cW"), S("kWT"), start=True, stop=True)
            mm(B[2][:, 2 * P:3 * P], S("cW"), S("vWT"), start=True, stop=True)
            mm(B[2][:, 3 * P:4 * P], S("wv"), S("woT"), start=True, stop=True)
            mm(B[3][:, 0:1], S("qWT"), S("hb"), start=True, stop=True)
            mm(B[3][:, 1:2], S("kWT"), S("cb"), start=True, stop=True)
            mm(B[3][:, 2:3], S("vWT"), S("cb"), start=True, stop=True)
            mm(B[3][:, 3:4], S("Wo4"), S("bv4"), start=True, stop=True)
            mm(B[3][:, 4:5], S("woT"), S("bv5"), start=True, stop=True)
            mm(B[3][:, 5:6], S("Wo6"), S("bv6"), start=True, stop=True).then_inc(sem("setup_mm"), 1)
            pe.wait_ge(sem("setup_slots"), 1)
            nc.tensor.transpose(B[4][:, 0:SLOTS], slots[:], ident[0:SLOTS, 0:SLOTS])
            mm(B[4][:, SLOTS:SLOTS + 1], slots[:], mean_w[:], start=True, stop=True).then_inc(sem("setup_mm"), 1)
            pe.wait_ge(sem("setup_slots"), 2)
            mm(B[5][0:SLOT_HID, 0:1], S("w1m"), mean_t[:], start=True, stop=True)
            for c in range(3):
                mm(B[5][:, SLOTS * (c + 1):SLOTS * (c + 2)], S("whh", c * P, (c + 1) * P), hs_t[:],
                   start=True, stop=True)
            pe.wait_ge(sem("setup_slots"), 3)
            mm(B[4][:, P:P + 1], S("oWT"), bcols[:, 2:3], start=True, stop=True).then_inc(sem("setup_mm"), 1)

        def setup_dve(dve, st):
            st.restart()
            v = nc.vector
            dve.wait_ge(sem("small_loaded"), 16)
            st.add(v.memset(mean_w[:], 1.0 / SLOTS))
            v.tensor_scalar(slots[:], S("slot_init"), S("slot_scale"), None, ALU.mult).then_inc(sem("setup_slots"), 1)
            dve.wait_ge(sem("setup_mm"), 1)
            for k, w in enumerate((wqh, wkc, wvc, wvo)):
                st.add(v.tensor_copy(w[:], B[2][:, k * P:(k + 1) * P]))
            for k, b in enumerate(("qb", "kb", "vb", "bo4", "bo5", "bo6")):
                st.add(v.tensor_tensor(bcols[:, k:k + 1], B[3][:, k:k + 1], S(b), ALU.add))
            st.add(v.tensor_tensor(brz[:], S("bih", 0, 2), S("bhh", 0, 2), ALU.add))
            st.add(v.tensor_scalar(rtau[:], S("tau"), -1.0, None, ALU.mult))
            st.settle()
            st.add(v.tensor_tensor(rtau[:], rtau[:], S("tau"), ALU.max))
            st.settle()
            st.add(v.tensor_scalar(rtau[:], rtau[:], 0.1, None, ALU.add))
            st.settle()
            st.add(v.reciprocal(rtau[:], rtau[:]))
            dve.wait_ge(sem("setup_mm"), 2)
            st.add(v.tensor_copy(hs_t[:], B[4][:, 0:SLOTS]))
            st.add(v.tensor_copy(mean_t[:], B[4][:, SLOTS:SLOTS + 1]))
            st.settle()
            v.engine_nop().then_inc(sem("setup_slots"), 2)
            dve.wait_ge(sem("setup_mm"), 3)
            st.add(v.tensor_tensor(b1x[:], B[5][0:SLOT_HID, 0:1], S("b1"), ALU.add))
            for c in range(2):
                st.add(v.tensor_scalar(gh_rz[:, c, :], B[5][:, SLOTS * (c + 1):SLOTS * (c + 2)],
                                       brz[:, c:c + 1], None, ALU.add))
            st.add(v.tensor_scalar(gh_n[:], B[5][:, 3 * SLOTS:4 * SLOTS], S("bhh", 2, 3), None, ALU.add))
            st.add(v.tensor_tensor(bcols[:, 6:7], B[4][:, P:P + 1], S("ob"), ALU.add))
            st.settle()
            for p, k in ((2, 6), (4, 3), (5, 4), (6, 5)):
                st.add(v.tensor_tensor(ybias[:, p:p + 1], bcols[:, k:k + 1], tgate[:, p:p + 1], ALU.mult))
            st.add(v.tensor_scalar(mtmp[:], mask_i[:], 0, None, ALU.is_equal))
            st.settle()
            st.add(v.tensor_scalar(maskb[:], mtmp[:].unsqueeze(1).to_broadcast([P, GB, P]), MASKED, None, ALU.mult))
            st.settle()
            v.engine_nop().then_inc(sem("setup_done"), 1)

        area1 = Area()
        su = [area1.tile([P, TG]) for i in range(RING)]
        sh = [area1.tile([P, TG]) for i in range(2)]
        sg = [area1.tile([P, TG]) for i in range(2)]
        hh = [area1.tile([P, TG]) for i in range(3)]
        cw_t = sb("cw_t", [96, TG], BF16)
        parts = sb("parts", [P, GB, 96], BF16)
        route = {}
        for p, m in MOE.items():
            E, NGR = m["E"], m["E"] // m["EG"]
            t = dict(
                vals=sb(f"vals{p}", [P, GB, E + 8 - m["K"]]), rep=sb(f"rep{p}", [P, GB, 8]),
                work=sb(f"work{p}", [P, GB, E + 8 - m["K"]]), m8=sb(f"m8_{p}", [P, GB, 8]),
                msk=sb(f"msk{p}", [P, GB, E]), sig=sb(f"sig{p}", [P, GB, E]),
                w=sb(f"w{p}", [P, GB, E]), tot=sb(f"tot{p}", [P, GB]), rec=sb(f"rec{p}", [P, GB]),
                comb=sb(f"comb{p}", [P, GB, E]), r1=sb(f"r1_{p}", [P, GB, E]),
                parts=parts)
            t["part"] = t["parts"][:, :, 0:3 * E].rearrange("p j (a e) -> p j a e", a=3)
            if m["GK"]:
                t.update(
                    s=sb(f"s{p}", [P, GB * NGR, 4]), pair=sb(f"pair{p}", [P, GB * NGR, 6]),
                    gv=sb(f"gv{p}", [P, GB, NGR + 8 - m["GK"]]), grep=sb(f"grep{p}", [P, GB, 8]),
                    gwork=sb(f"gwork{p}", [P, GB, NGR + 8 - m["GK"]]), gm=sb(f"gm{p}", [P, GB, NGR]),
                    gz=sb(f"gz{p}", [P, GB, NGR]), ms=sb(f"ms{p}", [P, GB * NGR, 4]))
            route[p] = t

        def route_setup(st):
            st.add(nc.vector.memset(parts[:], 0.0))
            for p, m in MOE.items():
                t = route[p]
                st.add(nc.vector.memset(t["vals"][:], LOWEST))
                st.add(nc.vector.memset(t["rep"][:], LOWEST))
                if m["GK"]:
                    st.add(nc.vector.memset(t["gv"][:], LOWEST))
                    st.add(nc.vector.memset(t["grep"][:], LOWEST))
            st.settle()

        def top_k(st, vals, m8, rep, work, k):
            for j in range(GB):
                st.add(nc.vector.max(out=m8[:, j, :], in_=vals[:, j, :]))
            st.settle()
            if k < 8:
                st.add(nc.vector.tensor_copy(rep[:, :, 0:k], m8[:, :, 0:k]))
                st.settle()
            else:
                rep = m8
            yield
            for j in range(GB):
                st.add(nc.vector.match_replace(out=work[:, j, :], in_to_replace=rep[:, j, :],
                                               in_values=vals[:, j, :], imm_value=TAKEN))
            st.settle()

        def split(st, t):
            v, parts = nc.vector, t["part"]
            st.add(v.tensor_copy(parts[:, :, 0, :], t["comb"][:]))
            st.settle()
            st.add(v.tensor_tensor(t["r1"][:], t["comb"][:], parts[:, :, 0, :], ALU.subtract))
            st.settle()
            st.add(v.tensor_copy(parts[:, :, 1, :], t["r1"][:]))
            st.settle()
            v.tensor_tensor(parts[:, :, 2, :], t["r1"][:], parts[:, :, 1, :], ALU.subtract)\
                .then_inc(sem("weights_ready"), 1)

        def per_expert(a, E):
            return a.unsqueeze(2).to_broadcast([P, GB, E])

        def normed(dve, st, t, E, factor, eps):
            v = nc.vector
            st.add(v.tensor_reduce(t["tot"][:], t["w"][:], AX.X, ALU.add))
            st.settle()
            st.add(v.tensor_scalar(t["tot"][:], t["tot"][:], eps, None, ALU.add))
            st.settle()
            st.add(v.reciprocal(t["rec"][:], t["tot"][:]))
            st.settle()
            st.add(v.scalar_tensor_tensor(t["comb"][:], t["w"][:], factor, per_expert(t["rec"][:], E),
                                          ALU.mult, ALU.mult))
            st.settle()

        def route_top2(dve, st, p, g):
            m, t, v = MOE[p], route[p], nc.vector
            E = m["E"]
            dve.wait_ge(sem(f"logits{p}"), g + 1)
            st.add(v.tensor_copy(t["vals"][:, :, 0:E], B[5][:, 0:GB * E].rearrange("p (j e) -> p j e", j=GB)))
            st.settle()
            yield
            yield from top_k(st, t["vals"], t["m8"], t["rep"], t["work"], m["K"])
            v.tensor_tensor(t["r1"][:], t["vals"][:, :, 0:E], t["m8"][:, :, 0:1].to_broadcast([P, GB, E]),
                            ALU.subtract).then_inc(sem("shifted"), 1)
            st.add(v.tensor_scalar(t["msk"][:], t["work"][:, :, 0:E], TAKEN, None, ALU.is_equal))
            st.settle()
            yield
            yield
            dve.wait_ge(sem("exp_ready"), g + 1)
            st.add(v.tensor_tensor(t["w"][:], t["sig"][:], t["msk"][:], ALU.mult))
            st.settle()
            normed(dve, st, t, E, 1.0, 0.0)
            yield
            split(st, t)

        def route_groups(dve, st, p, g):
            m, t, v = MOE[p], route[p], nc.vector
            E, NGR = m["E"], m["E"] // m["EG"]
            dve.wait_ge(sem(f"sig_ready{p}"), g + 1)
            st.add(v.tensor_tensor(t["s"][:].rearrange("p (j n) e -> p j (n e)", j=GB), t["sig"][:],
                                   S(f"rb{p}").unsqueeze(1).to_broadcast([P, GB, E]), ALU.add))
            st.settle()
            at = 0
            for d in (1, 2, 3):
                st.add(v.tensor_tensor(t["pair"][:, :, at:at + 4 - d], t["s"][:, :, 0:4 - d],
                                       t["s"][:, :, d:4], ALU.add))
                at += 4 - d
            st.settle()
            st.add(v.tensor_reduce(t["gv"][:, :, 0:NGR], t["pair"][:].rearrange("p (j n) e -> p j n e", j=GB),
                                   AX.X, ALU.max))
            st.settle()
            yield
            yield from top_k(st, t["gv"], t["m8"], t["grep"], t["gwork"], m["GK"])
            st.add(v.tensor_scalar(t["gm"][:], t["gwork"][:, :, 0:NGR], TAKEN, None, ALU.is_equal))
            st.settle()
            yield
            fill = -1.0 if p == 3 else 0.0
            gm = t["gm"][:].rearrange("p j n -> p (j n)").unsqueeze(2).to_broadcast([P, GB * NGR, 4])
            st.add(v.tensor_tensor(t["ms"][:], t["s"][:], gm, ALU.mult))
            if fill:
                st.add(v.tensor_scalar(t["gz"][:], t["gm"][:], 1.0, -fill, ALU.subtract, ALU.mult))
            st.settle()
            vals = t["vals"][:, :, 0:E]
            if fill:
                gz = t["gz"][:].rearrange("p j n -> p (j n)").unsqueeze(2).to_broadcast([P, GB * NGR, 4])
                st.add(v.tensor_tensor(t["ms"][:], t["ms"][:], gz, ALU.add))
                st.settle()
            st.add(v.tensor_scalar(vals, t["ms"][:].rearrange("p (j n) e -> p j (n e)", j=GB), 0.0, None, ALU.add))
            st.settle()
            yield
            yield from top_k(st, t["vals"], t["m8"], t["rep"], t["work"], m["K"])
            st.add(v.tensor_scalar(t["msk"][:], t["work"][:, :, 0:E], TAKEN, None, ALU.is_equal))
            st.settle()
            st.add(v.tensor_tensor(t["w"][:], t["sig"][:], t["msk"][:], ALU.mult))
            st.settle()
            normed(dve, st, t, E, SCALE_ROUTED, 1e-20)
            yield
            split(st, t)

        FINISH_AT, NORM_AT = 9, 11

        def moe_pe(pe, p):
            m = MOE[p]
            NC, NR, E = m["NC"], m["NR"], m["E"]
            wg, wu, wd = moe_w[p]
            pe.wait_ge(sem(f"moe{p}_loaded"), 48)
            pe.wait_ge(sem("constb_loaded"), 16)
            for g, _, _, h in stages(pe, p):
                s = NG * p + g
                xt = xhat_t[h]
                pe.wait_ge(sem("xhat_t_ready"), s + 1)
                for j in range(GB):
                    ins = nc.tensor.matmul(B[5][:, j * E:(j + 1) * E], xt[:, j * P:(j + 1) * P], S(f"Wr{p}"),
                                           start=True, stop=True)
                ins.then_inc(sem(f"logits{p}"), 1)
                for i in range(NC + TURN + 1):
                    if i < NC:
                        if i >= 2:
                            pe.wait_ge(sem(f"su_ready{p}"), g * NC + i - 1)
                        w = slice(i * P, (i + 1) * P)
                        nc.tensor.matmul(B[i % 2][:], wg[:, w], xt[:], start=True, stop=True)\
                            .then_inc(sem(f"gate_mm{p}"), 1)
                        nc.tensor.matmul(B[2 + i % 2][:], wu[:, w], xt[:], start=True, stop=True)\
                            .then_inc(sem(f"up_mm{p}"), 1)
                    if i == TURN - 1:
                        pe.wait_ge(sem("weights_ready"), NG * {1: 0, 3: 1, 7: 2}[p] + g + 1)
                        for j in range(GB):
                            ins = nc.tensor.transpose(
                                B[4][0:96, 0:TG // 2].bitcast(BF16)[:, j * P:(j + 1) * P],
                                route[p]["parts"][:, j, :], identb)
                        ins.then_inc(sem(f"cw_mm{p}"), 1)
                    if i == FINISH_AT:
                        finish_pe(pe, s)
                    if i == NORM_AT:
                        norm_pe(pe, s + 1, 1 - h)
                    c = i - TURN
                    if 0 <= c < NR:
                        if c == 0:
                            pe.wait_ge(sem(f"cw_ready{p}"), g + 1)
                        if c >= 2:
                            pe.wait_ge(sem(f"hh_ready{p}"), g * NR + c - 1)
                        at = SEL_AT[p] + c * P
                        nc.tensor.matmul(B[4 + c % 2][:], constb[0:3 * E, at:at + P], cw_t[0:3 * E, :],
                                         start=True, stop=True).then_inc(sem(f"bc_mm{p}"), 1)
                    c -= 1
                    if 0 <= c < NC:
                        if c == 0:
                            pe.wait_ge(sem("ysb_ready"), s)
                        if c < NR:
                            pe.wait_ge(sem(f"hh_ready{p}"), g * NR + c + 1)
                            src = hh[c % 3]
                        else:
                            pe.wait_ge(sem(f"su_ready{p}"), g * NC + c + 1)
                            src = sh[c - NR]
                        ins = nc.tensor.matmul(Y[:], wd[:, c * P:(c + 1) * P], src[:],
                                               start=(c == 0), stop=(c == NC - 1))
                        ins.then_inc(sem(f"down_mm{p}") if c < NC - 1 else sem("y_ready"), 1)

        def moe_act(act, p):
            m = MOE[p]
            NC, NR, E = m["NC"], m["NR"], m["E"]
            for g, _, _, h in stages(act, p):
                s = NG * p + g
                if m["GK"]:
                    act.wait_ge(sem(f"logits{p}"), g + 1)
                    nc.scalar.activation(route[p]["sig"][:], B[5][:, 0:GB * E].rearrange("p (j e) -> p j e", j=GB),
                                         ACT.Sigmoid).then_inc(sem(f"sig_ready{p}"), 1)
                for i in range(NC + TURN + 1):
                    if i < NC:
                        act.wait_ge(sem(f"gate_mm{p}"), g * NC + i + 1)
                        if i >= 2:
                            act.wait_ge(sem(f"su_ready{p}"), g * NC + i - 1)
                        nc.scalar.activation(sg[i % 2][:], B[i % 2][:], ACT.Silu).then_inc(sem(f"sg_ready{p}"), 1)
                    if not m["GK"] and i == 3:
                        act.wait_ge(sem("shifted"), g + 1)
                        nc.scalar.activation(route[p]["sig"][:], route[p]["r1"][:], ACT.Exp)\
                            .then_inc(sem("exp_ready"), 1)
                    if i == TURN - 1:
                        act.wait_ge(sem(f"cw_mm{p}"), g + 1)
                        nc.scalar.copy(cw_t[0:3 * E, :], B[4][0:3 * E, 0:TG // 2].bitcast(BF16))\
                            .then_inc(sem(f"cw_ready{p}"), 1)
                    if i == NORM_AT:
                        norm_act(act, s + 1, 1 - h)
                result_act(act, p, s)

        def moe_dve(dve, st, p):
            m = MOE[p]
            NC, NR = m["NC"], m["NR"]
            for g, before, after, h in stages(dve, p, st):
                s = NG * p + g
                pieces = route_groups(dve, st, p, g) if m["GK"] else route_top2(dve, st, p, g)
                for i in range(NC + TURN + 1):
                    next(pieces, None)
                    if i < NC:
                        dve.wait_ge(sem(f"sg_ready{p}"), g * NC + i + 1)
                        dve.wait_ge(sem(f"up_mm{p}"), g * NC + i + 1)
                        if i == NR:
                            dve.wait_ge(sem("y_ready"), s)
                        dst = su[i % RING] if i < NR else sh[i - NR]
                        nc.vector.tensor_tensor(dst[:], sg[i % 2][:], B[2 + i % 2][:], ALU.mult)\
                            .then_inc(sem(f"su_ready{p}"), 1)
                    if i == FINISH_AT:
                        finish_dve(dve, before, s)
                    if i == NORM_AT:
                        norm(dve, st, after, (s + 1, 1 - h))
                    c = i - TURN
                    if 0 <= c < NR:
                        dve.wait_ge(sem(f"bc_mm{p}"), g * NR + c + 1)
                        dve.wait_ge(sem(f"su_ready{p}"), g * NC + c + 1)
                        if c < 3:
                            dve.wait_ge(sem("y_ready"), s)
                        else:
                            dve.wait_ge(sem(f"down_mm{p}"), g * (NC - 1) + c - 2)
                        nc.vector.tensor_tensor(hh[c % 3][:], su[c % RING][:], B[4 + c % 2][:], ALU.mult)\
                            .then_inc(sem(f"hh_ready{p}"), 1)

        area2 = Area()
        q2 = area2.tile([P, TG])
        k2 = area2.tile([P, TG])
        v2 = area2.tile([P, TG])
        pr2 = area2.tile([P, TG])
        pn2 = area2.tile([P, TG])
        pt2 = area2.tile([P, TG])
        aq2 = area2.tile([P, TG])
        mx2 = sb("mx2", [P, GB])
        nb2 = sb("nb2", [P, GB])
        rs2 = sb("rs2", [P, GB])
        ri2 = sb("ri2", [P, GB])
        SCALE2 = float(P) ** -0.5

        def p2_pe(pe):
            p, mm = 2, nc.tensor.matmul
            for g, _, _, h in stages(pe, p):
                s = NG * p + g
                pe.wait_ge(sem("cg_ready"), g + 1)
                mm(B[0][:], wkc[:], cg[h][:], start=True, stop=True).then_inc(sem("k_mm2"), 1)
                for j in range(GB):
                    ins = mm(B[1][:, j * P:(j + 1) * P], cg[h][:, j * P:(j + 1) * P], wvc[:], start=True, stop=True)
                ins.then_inc(sem("v_mm2"), 1)
                pe.wait_ge(sem("xhat_t_ready"), s + 1)
                mm(B[2][:], wqh[:], xhat_t[h][:], start=True, stop=True).then_inc(sem("q_mm2"), 1)
                finish_pe(pe, s)
                pe.wait_ge(sem("qk_ready2"), 2 * g + 2)
                for j in range(GB):
                    t = slice(j * P, (j + 1) * P)
                    ins = mm(B[3][:, t], q2[:, t], k2[:, t], start=True, stop=True)
                ins.then_inc(sem("score_mm2"), 1)
                norm_pe(pe, s + 1, 1 - h)
                pe.wait_ge(sem("pn_ready2"), g + 1)
                for j in range(GB):
                    t = slice(j * P, (j + 1) * P)
                    ins = nc.tensor.transpose(B[4][:, t], pn2[:, t], ident)
                ins.then_inc(sem("pt_mm2"), 1)
                pe.wait_ge(sem("v_ready2"), g + 1)
                pe.wait_ge(sem("pt_ready2"), g + 1)
                for j in range(GB):
                    t = slice(j * P, (j + 1) * P)
                    ins = mm(B[5][:, t], v2[:, t], pt2[:, t], start=True, stop=True)
                ins.then_inc(sem("av_mm2"), 1)
                pe.wait_ge(sem("aq_ready2"), g + 1)
                pe.wait_ge(sem("ysb_ready"), s)
                mm(Y[:], S("oWT"), aq2[:], start=True, stop=True).then_inc(sem("y_ready"), 1)

        def p2_act(act):
            p = 2
            for g, _, _, h in stages(act, p):
                s = NG * p + g
                act.wait_ge(sem("k_mm2"), g + 1)
                nc.scalar.activation(k2[:], B[0][:], ACT.Identity, bias=bcols[:, 1:2]).then_inc(sem("qk_ready2"), 1)
                act.wait_ge(sem("q_mm2"), g + 1)
                nc.scalar.activation(q2[:], B[2][:], ACT.Identity, bias=bcols[:, 0:1]).then_inc(sem("qk_ready2"), 1)
                act.wait_ge(sem("nb_ready2"), g + 1)
                for j in range(GB):
                    t = slice(j * P, (j + 1) * P)
                    ins = nc.scalar.activation(pr2[:, t], B[3][:, t], ACT.Exp, bias=nb2[:, j:j + 1], scale=SCALE2,
                                               accum_out=rs2[:, j:j + 1])
                ins.then_inc(sem("exp_ready2"), 1)
                norm_act(act, s + 1, 1 - h)
                act.wait_ge(sem("pt_mm2"), g + 1)
                nc.scalar.copy(pt2[:], B[4][:]).then_inc(sem("pt_ready2"), 1)
                result_act(act, p, s)

        def p2_dve(dve, st):
            p, v = 2, nc.vector
            for g, before, after, h in stages(dve, p, st):
                s = NG * p + g
                dve.wait_ge(sem("v_mm2"), g + 1)
                v.tensor_copy(v2[:], B[1][:]).then_inc(sem("v_ready2"), 1)
                finish_dve(dve, before, s)
                dve.wait_ge(sem("score_mm2"), g + 1)
                st.add(v.tensor_reduce(mx2[:], B[3][:].rearrange("p (j k) -> p j k", j=GB), AX.X, ALU.max))
                st.settle()
                v.tensor_scalar(nb2[:], mx2[:], -SCALE2, None, ALU.mult).then_inc(sem("nb_ready2"), 1)
                norm(dve, st, after, (s + 1, 1 - h))
                dve.wait_ge(sem("exp_ready2"), g + 1)
                st.add(v.reciprocal(ri2[:], rs2[:]))
                st.settle()
                v.tensor_tensor(pn2[:].rearrange("p (j k) -> p j k", j=GB), pr2[:].rearrange("p (j k) -> p j k", j=GB),
                                ri2[:].unsqueeze(2).to_broadcast([P, GB, P]), ALU.mult).then_inc(sem("pn_ready2"), 1)
                dve.wait_ge(sem("av_mm2"), g + 1)
                v.tensor_tensor(aq2[:], B[5][:], q2[:], ALU.add).then_inc(sem("aq_ready2"), 1)

        area4 = Area()
        qh = [area4.tile([P, TG]) for i in range(HEAD_TILES)]
        kh = [area4.tile([P, TG]) for i in range(HEAD_TILES)]
        vh = sb("vh", [P, GB * HEADS, VW])
        vc = sb("vc", [P, GB * HEADS // 4, 2 * VW])
        sd = [area4.tile([P, TG]) for i in range(2)]
        es = [area4.tile([P, TG]) for i in range(2)]
        pt = [area4.tile([P, TG]) for i in range(2)]
        mxh = [sb(f"mxh{i}", [P, HEAD_TILES]) for i in range(2)]
        osb = area4.tile([P, GB, HEADS, DK])
        oc = area4.tile([HALF, GB * HEADS // 2, DK])
        rden = [sb(f"rden{i}", [P, GB * HEADS // 2]) for i in range(2)]
        oT = area4.tile([P, TG])
        SCALEH = float(DK) ** -0.5
        UNITS = [(j, a) for j in range(GB) for a in range(HEADS // HEAD_TILES)]
        NU = len(UNITS)

        def coarse(p, a):
            return p == 6 and a >= 2

        def width(p, a):
            return HALF if coarse(p, a) else P

        def bank_of(a):
            return B[a % 2]

        def out_place(p, j, a, i):
            if p == 4:
                return B[4 + j // 2], (j % 2) * HEADS + 4 * a + i
            return B[4 + a // 2], j * (HEADS // 2) + 4 * (a % 2) + i

        def heads_pe(pe, p):
            mm = nc.tensor.matmul
            base = 0 if p == 4 else NG
            for g, _, _, h in stages(pe, p):
                s = NG * p + g
                pe.wait_ge(sem("cg_ready"), NG * (1 if p == 4 else 2) + g + 1)
                n = 2 * HEAD_TILES * g
                for i in range(HEAD_TILES):
                    mm(B[i][:], S(f"Wk{p}", i * P, (i + 1) * P), cg[h][:], start=True, stop=True)\
                        .then_inc(sem(f"proj_mm{p}"), 1)
                for j in range(GB):
                    ins = mm(B[4][:, j * P:(j + 1) * P], cg[h][:, j * P:(j + 1) * P], S(f"Wv{p}"),
                             start=True, stop=True)
                if p == 6:
                    rows, at, _ = SMALL_AT["Wv6"]
                    for j in range(GB):
                        ins = mm(B[5][0:HALF, j * HALF:(j + 1) * HALF], cg[h][:, j * P:(j + 1) * P:2],
                                 small[:, at + HALF:at + P], start=True, stop=True)
                ins.then_inc(sem(f"v_mm{p}"), 1)
                pe.wait_ge(sem("xhat_t_ready"), s + 1)
                for i in range(HEAD_TILES):
                    pe.wait_ge(sem(f"proj_ready{p}"), n + i + 1)
                    mm(B[i][:], S(f"Wq{p}", i * P, (i + 1) * P), xhat_t[h][:], start=True, stop=True)\
                        .then_inc(sem(f"proj_mm{p}"), 1)
                finish_pe(pe, s)
                pe.wait_ge(sem(f"proj_ready{p}"), n + 2 * HEAD_TILES)
                pe.wait_ge(sem(f"v_ready{p}"), g + 1)
                for t in range(NU + 3):
                    if t < NU:
                        j, a = UNITS[t]
                        w, rows = width(p, a), slice(32 * a, 32 * a + 32)
                        if t >= 2:
                            pe.wait_ge(sem(f"sd_ready{p}"), NU * g + t - 1)
                        bank = bank_of(a)
                        if p == 4:
                            mm(bank[:], identb, maskb[:].rearrange("p a k -> p (a k)"), start=True, stop=False,
                               skip_group_check=True)
                        for i in range(HEAD_TILES):
                            cols = slice(j * P, (j + 1) * P, P // w)
                            ins = mm(bank[0:w, i * w:(i + 1) * w], qh[i][rows, cols], kh[i][rows, cols],
                                     start=(p == 6), stop=True, skip_group_check=(p == 4))
                        ins.then_inc(sem(f"score_mm{p}"), 1)
                    if t == 6:
                        norm_pe(pe, s + 1, 1 - h)
                    u = t - 2
                    if 0 <= u < NU:
                        j, a = UNITS[u]
                        w = width(p, a)
                        pe.wait_ge(sem(f"es_ready{p}"), NU * g + u + 1)
                        if u >= 2:
                            pe.wait_ge(sem(f"pt_ready{p}"), NU * g + u - 1)
                        for i in range(4 * w // P):
                            c = slice(i * P, (i + 1) * P)
                            ins = nc.tensor.transpose(B[2 + u % 2][:, c], es[u % 2][:, c], ident)
                        ins.then_inc(sem(f"pt_mm{p}"), 1)
                    u = t - 3
                    if 0 <= u < NU:
                        j, a = UNITS[u]
                        w = width(p, a)
                        pe.wait_ge(sem(f"pt_ready{p}"), NU * g + u + 1)
                        heads = P // w
                        for i in range(0, HEAD_TILES, heads):
                            bank, n9 = out_place(p, j, a, i)
                            if coarse(p, a):
                                val = vc[:, j * (HEADS // 4) + 2 * (a - 2) + i // 2, :]
                            else:
                                val = vh[:, j * HEADS + 4 * a + i, :]
                            ins = mm(bank[0:w, n9 * VW:(n9 + heads) * VW],
                                     pt[u % 2][:, i // heads * w:(i // heads + 1) * w], val, start=True, stop=True)
                        ins.then_inc(sem(f"pv_mm{p}"), 1)
                if p == 6:
                    pe.wait_ge(sem("oc_ready"), g + 1)
                    mm(B[2][:, 0:GB * HALF], K("up"), oc[:].rearrange("p n d -> p (n d)"), start=True, stop=True)\
                        .then_inc(sem("up_mm"), 1)
                pe.wait_ge(sem(f"osb_ready{p}"), g + 1)
                for j in range(GB):
                    ins = nc.tensor.transpose(B[3][:, j * P:(j + 1) * P],
                                              osb[:, j, :, :].rearrange("p n d -> p (n d)"), ident)
                ins.then_inc(sem(f"oT_mm{p}"), 1)
                pe.wait_ge(sem(f"oT_ready{p}"), g + 1)
                pe.wait_ge(sem("ysb_ready"), s)
                mm(Y[:], S(f"Wo{p}"), oT[:], start=True, stop=True).then_inc(sem("y_ready"), 1)

        def heads_act(act, p):
            for g, _, _, h in stages(act, p):
                s = NG * p + g
                n = 2 * HEAD_TILES * g
                for i in range(2 * HEAD_TILES):
                    dst, b = (kh, f"bk{p}") if i < HEAD_TILES else (qh, f"bq{p}")
                    act.wait_ge(sem(f"proj_mm{p}"), n + i + 1)
                    i4 = i % HEAD_TILES
                    nc.scalar.activation(dst[i4][:], B[i4][:], ACT.Identity, bias=S(b, i4, i4 + 1))\
                        .then_inc(sem(f"proj_ready{p}"), 1)
                for t in range(NU + 1):
                    if t < NU:
                        j, a = UNITS[t]
                        w = width(p, a)
                        act.wait_ge(sem(f"sd_ready{p}"), NU * g + t + 1)
                        if t >= 2:
                            act.wait_ge(sem(f"pt_mm{p}"), NU * g + t - 1)
                        nc.scalar.activation(es[t % 2][0:w, 0:4 * w], sd[t % 2][0:w, 0:4 * w], ACT.Exp,
                                             scale=SCALEH).then_inc(sem(f"es_ready{p}"), 1)
                    if t == 7:
                        norm_act(act, s + 1, 1 - h)
                    u = t - 1
                    if 0 <= u < NU:
                        j, a = UNITS[u]
                        w = width(p, a)
                        act.wait_ge(sem(f"pt_mm{p}"), NU * g + u + 1)
                        if u >= 2:
                            act.wait_ge(sem(f"pv_mm{p}"), NU * g + u - 1)
                        nc.scalar.copy(pt[u % 2][:, 0:4 * w * w // P].rearrange("p (i q) -> p i q", q=w),
                                       B[2 + u % 2][:, 0:4 * w].rearrange("p (i q) -> p i q", q=P)[:, :, 0:w])\
                            .then_inc(sem(f"pt_ready{p}"), 1)
                act.wait_ge(sem(f"oT_mm{p}"), g + 1)
                nc.scalar.copy(oT[:], B[3][:]).then_inc(sem(f"oT_ready{p}"), 1)
                result_act(act, p, s)

        def heads_dve(dve, st, p):
            v = nc.vector
            for g, before, after, h in stages(dve, p, st):
                s = NG * p + g
                dve.wait_ge(sem(f"v_mm{p}"), g + 1)
                ins = v.tensor_copy(vh[:, :, 0:DK], B[4][:].rearrange("p (n d) -> p n d", d=DK))
                if p == 6:
                    for k in range(2):
                        ins = v.tensor_copy(
                            vc[k * HALF:(k + 1) * HALF, :, k * VW:k * VW + DK],
                            B[5][0:HALF, 0:GB * HALF].rearrange("p (n k d) -> p n k d", k=2, d=DK)[:, :, k, :])
                ins.then_inc(sem(f"v_ready{p}"), 1)
                finish_dve(dve, before, s)
                for t in range(NU):
                    j, a = UNITS[t]
                    w = width(p, a)
                    bank = bank_of(a)[0:w, 0:4 * w].rearrange("p (i k) -> p i k", i=4)
                    dve.wait_ge(sem(f"score_mm{p}"), NU * g + t + 1)
                    st.add(v.tensor_reduce(mxh[t % 2][0:w, :], bank, AX.X, ALU.max))
                    st.settle()
                    if t >= 2:
                        dve.wait_ge(sem(f"es_ready{p}"), NU * g + t - 1)
                    v.tensor_tensor(sd[t % 2][0:w, 0:4 * w].rearrange("p (i k) -> p i k", i=4), bank,
                                    mxh[t % 2][0:w, :].unsqueeze(2).to_broadcast([w, 4, w]), ALU.subtract)\
                        .then_inc(sem(f"sd_ready{p}"), 1)
                    if t == 5:
                        norm(dve, st, after, (s + 1, 1 - h))
                dve.wait_ge(sem(f"pv_mm{p}"), NU * (g + 1))
                halves = [(B[4 + k][:, 0:32 * VW].rearrange("p (n d) -> p n d", d=VW), rden[k], k) for k in range(2)]
                outs = []
                for acc, rd, k in halves:
                    w = HALF if (p == 6 and k == 1) else P
                    st.add(v.reciprocal(rd[0:w, :], acc[0:w, :, DK]))
                st.settle()
                for acc, rd, k in halves:
                    w = HALF if (p == 6 and k == 1) else P
                    r3 = rd[0:w, :].unsqueeze(2).to_broadcast([w, 32, DK])
                    if p == 4:
                        ins = v.tensor_tensor(osb[:, 2 * k:2 * k + 2, :, :].rearrange("p j n d -> p (j n) d"),
                                              acc[:, :, 0:DK], r3, ALU.mult)
                    elif k == 0:
                        ins = v.tensor_tensor(osb[:, :, 0:8, :],
                                              acc[:, :, 0:DK].rearrange("p (j n) d -> p j n d", j=GB),
                                              rd[:].rearrange("p (j n) -> p j n", j=GB).unsqueeze(3)
                                              .to_broadcast([P, GB, 8, DK]), ALU.mult)
                    else:
                        v.tensor_tensor(oc[:], acc[0:w, :, 0:DK], r3, ALU.mult).then_inc(sem("oc_ready"), 1)
                        dve.wait_ge(sem("up_mm"), g + 1)
                        ins = v.tensor_copy(osb[:, :, 8:16, :].rearrange("p j n d -> p j (n d)"),
                                            B[2][:, 0:GB * HALF].rearrange("p (j n) -> p j n", j=GB))
                ins.then_inc(sem(f"osb_ready{p}"), 1)

        h5 = sb("h5", [SLOT_HID + 1, TG])
        area5 = Area()
        lg5 = area5.tile([P, GB, SLOTS])
        m85 = area5.tile([P, GB, 8])
        wk5 = area5.tile([P, GB, SLOTS])
        e5 = area5.tile([P, GB, SLOTS])
        tot5 = sb("tot5", [P, GB])
        rec5 = sb("rec5", [P, GB])
        al5 = area5.tile([P, GB, SLOTS])
        at5 = area5.tile([SLOTS, TG])
        ones5 = sb("ones5", [P, P])
        NS = GB * SLOTS
        ws5 = area5.tile([P, NS])
        gi5 = area5.tile([P, NS])
        rz5 = area5.tile([P, 2, NS])
        t5 = area5.tile([P, NS])
        n5 = area5.tile([P, NS])
        hn5 = area5.tile([P, NS])
        sv5 = area5.tile([SLOTS, TG])

        def p5_pe(pe):
            p, mm = 5, nc.tensor.matmul
            for g, _, _, h in stages(pe, p):
                s = NG * p + g
                pe.wait_ge(sem("xhat_t_ready"), s + 1)
                mm(B[0][0:SLOT_HID, :], S("w1x"), xhat_t[h][:], start=True, stop=True).then_inc(sem("h_mm5"), 1)
                finish_pe(pe, s)
                pe.wait_ge(sem("h_ready5"), g + 1)
                for j in range(GB):
                    ins = mm(B[1][:, j * SLOTS:(j + 1) * SLOTS], h5[:, j * P:(j + 1) * P], S("w2"), start=True, stop=True)
                ins.then_inc(sem("logit_mm5"), 1)
                norm_pe(pe, s + 1, 1 - h)
                pe.wait_ge(sem("al_ready5"), g + 1)
                for j in range(GB):
                    mm(B[2][:, j * SLOTS:(j + 1) * SLOTS], xhat[h][:, j * P:(j + 1) * P], al5[:, j, :], start=True, stop=True)
                mm(B[3][:, 0:NS], ones5[:], al5[:].rearrange("p j s -> p (j s)"), start=True, stop=True)\
                    .then_inc(sem("in_mm5"), 1)
                for j in range(GB):
                    ins = nc.tensor.transpose(B[0][0:SLOTS, j * P:(j + 1) * P], al5[:, j, :], ident)
                ins.then_inc(sem("at_mm5"), 1)
                pe.wait_ge(sem("gi_ready5"), g + 1)
                for c in range(2):
                    mm(B[4][:, c * NS:(c + 1) * NS], S("wih", c * P, (c + 1) * P), gi5[:], start=True, stop=True)
                mm(B[5][:, 0:NS], S("wih", 2 * P, 3 * P), gi5[:], start=True, stop=True).then_inc(sem("gx_mm5"), 1)
                pe.wait_ge(sem("hn_ready5"), g + 1)
                for j in range(GB):
                    ins = mm(B[1][0:SLOTS, j * P:(j + 1) * P], hn5[:, j * SLOTS:(j + 1) * SLOTS], wvo[:],
                             start=True, stop=True)
                ins.then_inc(sem("sv_mm5"), 1)
                pe.wait_ge(sem("at_ready5"), g + 1)
                pe.wait_ge(sem("sv_ready5"), g + 1)
                pe.wait_ge(sem("ysb_ready"), s)
                for j in range(GB):
                    t = slice(j * P, (j + 1) * P)
                    ins = mm(Y[:, t], sv5[:, t], at5[:, t], start=True, stop=True)
                ins.then_inc(sem("y_ready"), 1)

        def p5_act(act):
            p = 5
            for g, _, _, h in stages(act, p):
                s = NG * p + g
                act.wait_ge(sem("h_mm5"), g + 1)
                nc.scalar.activation(h5[0:SLOT_HID, :], B[0][0:SLOT_HID, :], ACT.Gelu, bias=b1x[:])\
                    .then_inc(sem("h_ready5"), 1)
                act.wait_ge(sem("shift_ready5"), g + 1)
                nc.scalar.activation(e5[:], e5[:], ACT.Exp, scale=rtau[:]).then_inc(sem("exp_ready5"), 1)
                norm_act(act, s + 1, 1 - h)
                act.wait_ge(sem("at_mm5"), g + 1)
                nc.scalar.copy(at5[:], B[0][0:SLOTS, :]).then_inc(sem("at_ready5"), 1)
                act.wait_ge(sem("rzx_ready5"), g + 1)
                nc.scalar.activation(rz5[:], rz5[:], ACT.Sigmoid).then_inc(sem("rz_ready5"), 1)
                act.wait_ge(sem("nx_ready5"), g + 1)
                nc.scalar.activation(n5[:], t5[:], ACT.Tanh, bias=S("bih", 2, 3)).then_inc(sem("n_ready5"), 1)
                act.wait_ge(sem("sv_mm5"), g + 1)
                nc.scalar.copy(sv5[:], B[1][0:SLOTS, :]).then_inc(sem("sv_ready5"), 1)
                result_act(act, p, s)

        def p5_dve(dve, st):
            p, v = 5, nc.vector

            def bs(a):
                return a.unsqueeze(1).to_broadcast([P, GB, SLOTS])

            def js(a):
                return a.rearrange("p (j s) -> p j s", j=GB)

            for g, before, after, h in stages(dve, p, st):
                s = NG * p + g
                finish_dve(dve, before, s)
                dve.wait_ge(sem("logit_mm5"), g + 1)
                st.add(v.tensor_copy(lg5[:], js(B[1][:, 0:NS])))
                st.settle()
                for j in range(GB):
                    st.add(v.max(out=m85[:, j, :], in_=lg5[:, j, :]))
                st.settle()
                v.tensor_tensor(e5[:], lg5[:], m85[:, :, 0:1].to_broadcast([P, GB, SLOTS]), ALU.subtract)\
                    .then_inc(sem("shift_ready5"), 1)
                for j in range(GB):
                    st.add(v.match_replace(out=wk5[:, j, :], in_to_replace=m85[:, j, :], in_values=lg5[:, j, :],
                                           imm_value=TAKEN))
                st.settle()
                st.add(v.tensor_scalar(wk5[:], wk5[:], TAKEN, None, ALU.is_equal))
                st.settle()
                dve.wait_ge(sem("exp_ready5"), g + 1)
                st.add(v.tensor_tensor(al5[:], e5[:], wk5[:], ALU.mult))
                st.settle()
                st.add(v.tensor_reduce(tot5[:], al5[:], AX.X, ALU.add))
                st.settle()
                st.add(v.reciprocal(rec5[:], tot5[:]))
                st.settle()
                v.tensor_tensor(al5[:], al5[:], rec5[:].unsqueeze(2).to_broadcast([P, GB, SLOTS]), ALU.mult)\
                    .then_inc(sem("al_ready5"), 1)
                norm(dve, st, after, (s + 1, 1 - h))
                dve.wait_ge(sem("in_mm5"), g + 1)
                st.add(v.tensor_scalar(ws5[:], B[3][:, 0:NS], 1e-8, None, ALU.add))
                st.settle()
                st.add(v.reciprocal(ws5[:], ws5[:]))
                st.settle()
                v.tensor_tensor(gi5[:], B[2][:, 0:NS], ws5[:], ALU.mult).then_inc(sem("gi_ready5"), 1)
                dve.wait_ge(sem("gx_mm5"), g + 1)
                for c in range(2):
                    ins = v.tensor_tensor(js(rz5[:, c, :]), js(B[4][:, c * NS:(c + 1) * NS]), bs(gh_rz[:, c, :]), ALU.add)
                ins.then_inc(sem("rzx_ready5"), 1)
                dve.wait_ge(sem("rz_ready5"), g + 1)
                st.add(v.tensor_tensor(js(t5[:]), js(rz5[:, 0, :]), bs(gh_n[:]), ALU.mult))
                st.settle()
                v.tensor_tensor(t5[:], t5[:], B[5][:, 0:NS], ALU.add).then_inc(sem("nx_ready5"), 1)
                dve.wait_ge(sem("n_ready5"), g + 1)
                st.add(v.tensor_tensor(js(hn5[:]), bs(hs_t[:]), js(n5[:]), ALU.subtract))
                st.settle()
                st.add(v.tensor_tensor(hn5[:], hn5[:], rz5[:, 1, :], ALU.mult))
                st.settle()
                v.tensor_tensor(hn5[:], hn5[:], n5[:], ALU.add).then_inc(sem("hn_ready5"), 1)

        block = ctx.enter_context(nc.Block())

        @block.sync
        def _(sp):
            sp.dma_start(const[:], const_d).then_inc(sem("const_loaded"), 16)
            for g in range(NG):
                c = slice(g * TG, (g + 1) * TG)
                sp.dma_start(X[:, c], x_d[:, c]).then_inc(sem(f"x_loaded{g}"), 16)
                if g == 0:
                    sp.dma_start(CT[:], ctx_d).then_inc(sem("ctx_loaded"), 16)
            for p in MOE:
                for k in range(3):
                    sp.dma_start(moe_w[p][k][:], moe_d[p][k]).then_inc(sem(f"moe{p}_loaded"), 16)
            sp.dma_start(mask_i[:], mask_d).then_inc(sem("small_loaded"), 16)
            for g in range(NG):
                sp.wait_ge(sem("x_updated"), last - NG + 1 + g)
                c = slice(g * TG, (g + 1) * TG)
                sp.dma_start(out_d[:, c], X[:, c]).then_inc(sem("stored"), 16)
            sp.wait_ge(sem("stored"), 16 * NG)
            if phases < PHASES:
                for name, n in [("constb_loaded", 16)] + [(f"moe{p}_loaded", 48) for p in MOE]:
                    sp.wait_ge(sem(name), n)

        @block.gpsimd
        def _(pool):
            gp = nc.gpsimd
            gp.memset(minus_half[:], -0.5).then_inc(sem("rstd_ready"), 1)
            pool.wait_ge(sem("rstd_ready"), 1)

            def power(s):
                pool.wait_ge(sem("var_ready"), s + 1)
                gp.tensor_tensor(rstd[:], var[:], minus_half[:], ALU.pow).then_inc(sem("rstd_ready"), 1)

            for s in range(NG + 1):
                power(s)
            turn = 0
            for p in range(1, phases):
                context = p in (2, 4, 6)
                for g, _, _, h in stages(pool, p):
                    s = NG * p + g
                    if context:
                        pool.wait_ge(sem("y_ready"), s - 1)
                        pool.wait_ge(sem("ctx_loaded"), 16)
                        gp.tensor_copy(cg[h][:], CT[:, bass.ds(g * TG, TG)]).then_inc(sem("cg_ready"), 1)
                    power(s + 1)

        @block.scalar
        def _(act):
            act.dma_start(small[:], small_d).then_inc(sem("gates_loaded"), 16)
            act.dma_start(constb[:], constb_d).then_inc(sem("constb_loaded"), 16)
            act.wait_ge(sem("gates_loaded"), 16)
            nc.scalar.activation(tgate[:], S("gates"), ACT.Tanh).then_inc(sem("tgate_ready"), 1)
            act.wait_ge(sem("tgate_ready"), 1)
            act.wait_ge(sem("bias0_ready"), 1)
            norm_act(act, 0, 0)
            p0_act(act)
            act.wait_ge(sem("setup_done"), 1)
            for p in range(1, phases):
                if p in MOE:
                    moe_act(act, p)
                elif p == 2:
                    p2_act(act)
                elif p == 5:
                    p5_act(act)
                else:
                    heads_act(act, p)

        @block.tensor
        def _(pe):
            pe.wait_ge(sem("const_loaded"), 16)
            norm_pe(pe, 0, 0)
            p0_pe(pe)
            pe.wait_ge(sem("gates_loaded"), 16)
            setup_pe(pe)
            pe.wait_ge(sem("setup_done"), 1)
            for p in range(1, phases):
                if p in MOE:
                    moe_pe(pe, p)
                elif p == 2:
                    p2_pe(pe)
                elif p == 5:
                    p5_pe(pe)
                else:
                    heads_pe(pe, p)
            finish_pe(pe, last)

        @block.vector
        def _(dve):
            st = Steps(dve, sem("dve_steps"))
            nc.vector.memset(ybias[:], 0.0).then_inc(sem("bias0_ready"), 1)
            st.add(nc.vector.memset(ones5[:], 1.0))
            st.add(nc.vector.memset(h5[:], 1.0))
            st.add(nc.vector.memset(vh[:], 1.0))
            st.add(nc.vector.memset(vc[:], 0.0))
            st.settle()
            for k in range(2):
                st.add(nc.vector.memset(vc[k * HALF:(k + 1) * HALF, :, k * VW + DK], 1.0))
            route_setup(st)
            dve.wait_ge(sem("const_loaded"), 16)
            for g in range(NG):
                dve.wait_ge(sem(f"x_loaded{g}"), 16)
            norm(dve, st, 0, (0, 0))
            p0_dve(dve, st)
            dve.wait_ge(sem("tgate_ready"), 1)
            dve.wait_ge(sem("gates_loaded"), 16)
            setup_dve(dve, st)
            for p in range(1, phases):
                dve.wait_ge(sem("y_ready"), NG * p)
                if p in MOE:
                    moe_dve(dve, st, p)
                elif p == 2:
                    p2_dve(dve, st)
                elif p == 5:
                    p5_dve(dve, st)
                else:
                    heads_dve(dve, st, p)
            finish_dve(dve, NG - 1, last)


def packed(table, at, n, arrays):
    out = np.zeros((P, n), np.float32)
    for name, (rows, start, cols) in at.items():
        out[0:rows, start:start + cols] = arrays[name]
    return out


def head_tiles(w):
    lead = w.shape[:-1]
    out = np.zeros(lead + (HEAD_TILES, HEADS // HEAD_TILES, 32), w.dtype)
    src = w.reshape(lead + (HEADS // HEAD_TILES, HEAD_TILES, DK))
    for i in range(HEAD_TILES):
        out[..., i, :, 0:DK] = src[..., :, i, :]
    return out.reshape(lead + (HEAD_TILES * P,))


def constants():
    up = np.zeros((HALF, P), np.float32)
    for t in range(P):
        at = max((t + 0.5) * 0.5 - 0.5, 0.0)
        i0 = int(at)
        up[i0, t] += 1.0 - (at - i0)
        up[min(i0 + 1, HALF - 1), t] += at - i0
    return dict(ident=np.eye(P, dtype=np.float32), causal=np.triu(np.ones((P, P), np.float32)), up=up)


def selectors(dtype):
    out = np.zeros((P, SEL_N), np.float32)
    out[:, 0:P] = np.eye(P)
    for p, m in MOE.items():
        f = np.arange(m["NR"] * P)
        for part in range(3):
            out[part * m["E"] + f // m["F"], SEL_AT[p] + f] = 1.0
    return out.astype(dtype)


def layout(**inputs):
    A = {k: np.asarray(v) for k, v in inputs.items()}

    def col(a):
        return a.reshape(-1, 1)

    def per_partition(a):
        return np.broadcast_to(a.reshape(1, -1), (P, a.size))

    x2, f2, x4 = "L1_xattn_", "L2_ffn_", "L2_xattn_"
    x6 = "L3_xattn_"
    small = dict(
        gates=per_partition(np.stack([A["g_xattn"], A["g_ffn"]], 1)),
        Wr1=A["L0_ffn_Wr"], Wr3=A["L1_ffn_router_w"].T, Wr7=A["L3_ffn_gate_w"].T,
        rb3=per_partition(A["L1_ffn_bias"]), rb7=per_partition(A["L3_ffn_gate_bias"]),
        hW=A[x2 + "hW"], qWT=A[x2 + "qW"].T, cW=A[x2 + "cW"], kWT=A[x2 + "kW"].T, vWT=A[x2 + "vW"].T,
        oWT=A[x2 + "oW"].T, **{b: col(A[x2 + b]) for b in ("hb", "qb", "cb", "kb", "vb", "ob")},
        Wq4=head_tiles(A[x4 + "Wq"].T), Wk4=head_tiles(A[x4 + "Wk"].T), Wv4=A[x4 + "Wv"].T, Wo4=A[x4 + "Wo"].T,
        Wq6=head_tiles(A[x6 + "w_q"]), Wk6=head_tiles(A[x6 + "w_k"]), Wv6=A[x6 + "w_v"], Wo6=A[x6 + "w_o"],
        bq4=head_tiles(A[x4 + "bq"]).reshape(HEAD_TILES, P).T, bk4=head_tiles(A[x4 + "bk"]).reshape(HEAD_TILES, P).T,
        bq6=head_tiles(A[x6 + "b_q"]).reshape(HEAD_TILES, P).T, bk6=head_tiles(A[x6 + "b_k"]).reshape(HEAD_TILES, P).T,
        bv4=col(A[x4 + "bv"]), bo4=col(A[x4 + "bo"]), bv6=col(A[x6 + "b_v"]), bo6=col(A[x6 + "b_o"]),
        slot_init=A[f2 + "slot_init"], slot_scale=A[f2 + "slot_scale"],
        w1x=A[f2 + "w1"][:, 0:P].T, w1m=A[f2 + "w1"][:, P:].T, b1=col(A[f2 + "b1"]),
        w2=np.concatenate([A[f2 + "w2"].T, A[f2 + "b2"][None]], 0),
        wih=A[f2 + "gru_wih"].T, whh=A[f2 + "gru_whh"].T,
        bih=A[f2 + "gru_bih"].reshape(3, P).T, bhh=A[f2 + "gru_bhh"].reshape(3, P).T,
        wv=A[f2 + "wv"], woT=A[f2 + "wo"].T, bv5=col(A[f2 + "bv"]), bo5=col(A[f2 + "bo"]),
        tau=per_partition(A[f2 + "tau"]),
    )

    def wide(w):
        return w.transpose(1, 0, 2).reshape(P, -1)

    def chunks(w):
        return w.reshape(-1, P, P).transpose(1, 0, 2).reshape(P, -1)

    l1, l3 = "L1_ffn_", "L3_ffn_"
    moe = {
        1: [wide(A["L0_ffn_Wg"]), wide(A["L0_ffn_Wu"]), chunks(A["L0_ffn_Wd"].reshape(-1, P))],
        3: [np.concatenate([wide(A[l1 + "gate_w"]), A[l1 + "sh_gate_w"]], 1),
            np.concatenate([wide(A[l1 + "up_w"]), A[l1 + "sh_up_w"]], 1),
            np.concatenate([chunks(A[l1 + "down_w"].reshape(-1, P)), chunks(A[l1 + "sh_down_w"])], 1)],
        7: [np.concatenate([A[l3 + "w_gate"].reshape(-1, P).T, A[l3 + "sh_gate"].T], 1),
            np.concatenate([A[l3 + "w_up"].reshape(-1, P).T, A[l3 + "sh_up"].T], 1),
            np.concatenate([chunks(A[l3 + "w_down"].transpose(0, 2, 1).reshape(-1, P)), chunks(A[l3 + "sh_down"].T)], 1)],
    }
    arrays = dict(
        in_small=packed(SMALL, SMALL_AT, SMALL_N, small),
        in_const=packed(CONST, CONST_AT, CONST_N, constants()),
        in_constb=selectors(mybir.dt.np(BF16)),
        in_x=A["x"].transpose(1, 0, 2).reshape(P, NB * P),
        in_ctx_t=A["ctx_1024"].transpose(2, 0, 1).reshape(P, NB * P),
        in_mask=A["mask_1x1xSxS2_ik0"].reshape(P, P),
        **{f"in_moe{p}_{k}": w for p, ws in moe.items() for k, w in enumerate(ws)},
    )
    return {name: np.ascontiguousarray(a) for name, a in arrays.items()}


def describe(nc, arrays, phases=PHASES):
    d = {name: nc.dram_tensor(name, a.shape, mybir.dt.from_np(a.dtype), kind="ExternalInput").ap()
         for name, a in arrays.items()}
    out = nc.dram_tensor("out", (P, NB * P), F32, kind="ExternalOutput").ap()
    build(nc, d["in_small"], d["in_const"], d["in_constb"], d["in_x"], d["in_ctx_t"], d["in_mask"],
          {p: [d[f"in_moe{p}_{k}"] for k in range(3)] for p in MOE}, out, phases=phases)


def kernel(**inputs):
    import concourse.bacc as bacc
    from concourse.bass_utils import run_bass_kernel_spmd as run
    arrays = layout(**inputs)
    nc = bacc.Bacc("TRN2", target_bir_lowering=False, num_devices=1)
    describe(nc, arrays)
    out = run(nc, [arrays], core_ids=[0]).results[0]["out"]
    return np.ascontiguousarray(out.reshape(P, NB, P).transpose(1, 0, 2))
```

```python
from contextlib import ExitStack

import numpy as np

import concourse.bass as bass
from concourse import mybir

F32 = mybir.dt.float32
BF16 = mybir.dt.bfloat16
I32 = mybir.dt.int32
F32R = mybir.dt.float32r
ALU = mybir.AluOpType
ACT = mybir.ActivationFunctionType
AX = mybir.AxisListType

P = 128
NB = 16
GB = 4
NG = NB // GB
TG = GB * P
PHASES = 8
LN_EPS = 1e-5
LOWEST = -3.0e38
TAKEN = 3.0e38
MASKED = -1.0e30

HEADS, DK = 16, 8
HEAD_TILES = 4
VW = 32
HALF = P // 2

SLOTS = 64
SLOT_HID = 64
SLOT_TOP = 8

MOE = {
    1: dict(E=8, F=256, SH=0, K=2, GK=0),
    3: dict(E=16, F=128, SH=256, K=4, GK=2),
    7: dict(E=32, F=64, SH=128, K=8, GK=4),
}
for _m in MOE.values():
    _m["NR"] = _m["E"] * _m["F"] // P
    _m["NC"] = _m["NR"] + _m["SH"] // P
    _m["EG"] = 4
SCALE_ROUTED = 2.5
TURN = 10
DOWN = TURN + 4
RING = DOWN + 2
HI_RING = 5
SPLIT_IN = {1: 0, 3: 2, 7: 4}

SMALL = dict(
    gates=(P, PHASES),
    hW=(P, P), qWT=(P, P), cW=(P, P), kWT=(P, P), vWT=(P, P), oWT=(P, P),
    hb=(P, 1), qb=(P, 1), cb=(P, 1), kb=(P, 1), vb=(P, 1), ob=(P, 1),
    Wr1=(P, 8), Wr3=(P, 16), Wr7=(P, 32), rb3=(P, 16), rb7=(P, 32),
    Wq4=(P, HEAD_TILES * P), Wk4=(P, HEAD_TILES * P), Wv4=(P, P), Wo4=(P, P),
    bq4=(P, HEAD_TILES), bk4=(P, HEAD_TILES), bv4=(P, 1), bo4=(P, 1),
    Wq6=(P, HEAD_TILES * P), Wk6=(P, HEAD_TILES * P), Wv6=(P, P), Wo6=(P, P),
    bq6=(P, HEAD_TILES), bk6=(P, HEAD_TILES), bv6=(P, 1), bo6=(P, 1),
    slot_init=(SLOTS, P), slot_scale=(SLOTS, 1), w1x=(P, SLOT_HID), w1m=(P, SLOT_HID),
    b1=(SLOT_HID, 1), w2=(SLOT_HID + 1, SLOTS), wih=(P, 3 * P), whh=(P, 3 * P),
    bih=(P, 3), bhh=(P, 3), wv=(P, P), woT=(P, P), bv5=(P, 1), bo5=(P, 1), tau=(P, 1),
)
CONST = dict(ident=(P, P), causal=(P, P), up=(P, 2 * P), rowmask=(P, 2))


def columns(table):
    at, n = {}, 0
    for name, (rows, cols) in table.items():
        at[name] = (rows, n, cols)
        n += cols
    return at, n


SMALL_AT, SMALL_N = columns(SMALL)
CONST_AT, CONST_N = columns(CONST)
SEL_AT, SEL_N = {}, P
for _p, _m in MOE.items():
    SEL_AT[_p] = SEL_N
    SEL_N += _m["NR"] * P


class Steps:

    def __init__(self, eng, sem):
        self.eng, self.sem, self.n = eng, sem, 0

    def add(self, instruction):
        instruction.then_inc(self.sem, 1)
        self.n += 1
        return self.n

    def settle(self, n=None):
        self.eng.wait_ge(self.sem, self.n if n is None else n)

    def restart(self):
        if self.n:
            self.settle()
        self.eng.sem_clear(self.sem)
        self.n = 0


def build(nc, small_d, const_d, constb_d, x_d, ctx_d, mask_d, moe_d, out_d, phases=PHASES):
    last = NG * phases
    with ExitStack() as ctx:
        def sb(name, shape, dt=F32):
            return ctx.enter_context(nc.sbuf_tensor(name, shape, dt))

        def two_views(name, shape):
            with nc.sbuf_tensor(name, shape, F32) as full:
                pass
            return full, sb(name + "_r", shape, F32R)

        sems = {}

        def sem(name):
            if name not in sems:
                sems[name] = ctx.enter_context(nc.semaphore(name))
            return sems[name]

        T = ctx.enter_context(nc.psum_tensor("T", [P, TG], F32))
        Y = ctx.enter_context(nc.psum_tensor("Y", [P, TG], F32))
        B = [ctx.enter_context(nc.psum_tensor(f"B{i}", [P, TG], F32)) for i in range(6)]

        X = sb("X", [P, NB * P])
        CT = sb("CT", [P, NB * P])
        small = sb("small", [P, SMALL_N])
        const = sb("const", [P, CONST_N])
        constb = sb("constb", [P, SEL_N], BF16)
        mask_i = sb("mask_i", [P, P], I32)
        WCOLS = max(m["NC"] for m in MOE.values()) * P
        w_hi = [sb(f"{n}_hi", [P, WCOLS], F32R) for n in ("gate", "up", "down")]
        w_raw, w_lo = zip(*[two_views(f"{n}_lo", [P, WCOLS]) for n in ("gate", "up", "down")])

        def S(name, a=0, b=None):
            rows, at, cols = SMALL_AT[name]
            return small[0:rows, at + a:at + (cols if b is None else b)]

        def K(name):
            rows, at, cols = CONST_AT[name]
            return const[0:rows, at:at + cols]

        ident = K("ident")
        identb = constb[:, 0:P]

        xhat = [sb(f"xhat{i}", [P, TG]) for i in range(2)]
        xhat_t = [sb(f"xhat_t{i}", [P, TG]) for i in range(2)]
        cg = [sb(f"cg{i}", [P, TG]) for i in range(2)]
        ysb = sb("ysb", [P, TG])
        tgate = sb("tgate", [P, PHASES])
        ybias = sb("ybias", [P, PHASES])

        stats = sb("stats", [P, GB, 6])
        mv = sb("mv", [P, GB, 2])
        var = sb("var", [P, GB])
        rstd = sb("rstd", [P, GB])
        minus_half = sb("minus_half", [P, GB])
        spare = sb("spare", [P, 1])

        shared, shared_r = two_views("shared", [P, 25 * TG])

        class Area:
            def __init__(self):
                self.at = 0

            def tile(self, shape, of=shared):
                n = int(np.prod(shape[1:]))
                a = of[0:shape[0], self.at:self.at + n]
                self.at += n
                assert self.at <= 25 * TG
                if len(shape) == 3:
                    a = a.rearrange("p (a b) -> p a b", a=shape[1])
                elif len(shape) == 4:
                    a = a.rearrange("p (a b c) -> p a b c", a=shape[1], b=shape[2])
                return a

        def token_tile(g, j):
            return X[:, bass.ds(g * TG + j * P, P)]

        def norm(dve, st, g, s):
            norm_stats(st, g)
            norm_apply(dve, g, *s)

        def norm_stats(st, g):
            for j in range(GB):
                st.add(nc.vector.bn_stats(out=stats[:, j, :], in_=token_tile(g, j)))
            st.settle()
            for j in range(GB):
                st.add(nc.vector.bn_aggr(out=mv[:, j, :], in_=stats[:, j, :]))
            st.settle()
            nc.vector.tensor_scalar(var[:], mv[:, :, 1], LN_EPS, None, ALU.add).then_inc(sem("var_ready"), 1)

        def norm_apply(dve, g, s, h):
            dve.wait_ge(sem("rstd_ready"), s + 2)
            for j in range(GB):
                ins = nc.vector.tensor_scalar(xhat[h][:, j * P:(j + 1) * P], token_tile(g, j),
                                              mv[:, j, 0:1], rstd[:, j:j + 1], ALU.subtract, ALU.mult)
            ins.then_inc(sem("xhat_ready"), 1)

        def finish_dve(dve, g, s):
            dve.wait_ge(sem("yt_ready"), s)
            nc.vector.tensor_tensor(X[:, bass.ds(g * TG, TG)], X[:, bass.ds(g * TG, TG)], T[:],
                                    ALU.add).then_inc(sem("x_updated"), 1)
            dve.wait_ge(sem("x_updated"), s)

        def finish_pe(pe, s):
            pe.wait_ge(sem("xhat_t_ready"), s + 1)
            pe.wait_ge(sem("ysb_ready"), s)
            for j in range(GB):
                ins = nc.tensor.transpose(T[:, j * P:(j + 1) * P], ysb[:, j * P:(j + 1) * P], ident)
            ins.then_inc(sem("yt_ready"), 1)

        def norm_pe(pe, s, h):
            pe.wait_ge(sem("xhat_ready"), s + 1)
            if not isinstance(s, int) or s > 1:
                pe.wait_ge(sem("x_updated"), s - 1)
            elif s == 1:
                pe.wait_ge(sem("xhat_t_ready"), s)
            for j in range(GB):
                ins = nc.tensor.transpose(T[:, j * P:(j + 1) * P], xhat[h][:, j * P:(j + 1) * P], ident)
            ins.then_inc(sem("xt_ready"), 1)

        def norm_act(act, s, h):
            act.wait_ge(sem("xt_ready"), s + 1)
            nc.scalar.copy(xhat_t[h][:], T[:]).then_inc(sem("xhat_t_ready"), 1)

        def result_act(act, p, s):
            act.wait_ge(sem("y_ready"), s + 1)
            if not isinstance(s, int) or s > 0:
                act.wait_ge(sem("yt_ready"), s)
            nc.scalar.activation(ysb[:], Y[:], ACT.Identity, bias=ybias[:, p:p + 1],
                                 scale=tgate[:, p:p + 1]).then_inc(sem("ysb_ready"), 1)

        def weights_hi(act, p, g):
            n = MOE[p]["NC"] * P // NG
            act.wait_ge(sem(f"raw{p}"), 48 * (g + 1))
            for k in range(3):
                ins = nc.scalar.copy(w_hi[k][:, bass.ds(g * n, n)], w_raw[k][:, bass.ds(g * n, n)])
            ins.then_inc(sem(f"w_hi{p}"), 1)

        def weights_lo(pool, p, g):
            n = MOE[p]["NC"] * P // NG
            if p > 1:
                pool.wait_ge(sem(f"raw{p}"), 48 * (g + 1))
                for k in range(3):
                    c = bass.ds(g * n, n)
                    ins = nc.gpsimd.tensor_copy(w_hi[k][:, c], w_raw[k][:, c])
                ins.then_inc(sem(f"w_hi{p}"), 1)
            pool.wait_ge(sem(f"w_hi{p}"), g + 1)
            if p > 1:
                nc.gpsimd.tensor_tensor(spare[:], minus_half[:, 0:1], minus_half[:, 0:1], ALU.add)
            for k in range(3):
                c = bass.ds(g * n, n)
                ins = nc.gpsimd.tensor_tensor(w_lo[k][:, c], w_raw[k][:, c], w_hi[k][:, c].bitcast(F32),
                                              ALU.subtract)
            ins.then_inc(sem(f"w_lo{p}"), 1)

        def stages(eng, p, st=None):
            if st:
                st.restart()
            with eng.Fori(0, NG // 2) as r:
                for g, before, after, h in ((2 * r, r * -2 + 3, 2 * r + 1, 0), (2 * r + 1, 2 * r, r * -2 + 2, 1)):
                    yield g, before, after, h
                    if st:
                        st.restart()

        sm = [sb(f"sm{i}", [P, TG]) for i in range(2)]

        def p0_pe(pe):
            for g in range(NG):
                h = g % 2
                pe.wait_ge(sem(f"ctx_loaded{g}"), 16)
                if g >= 2:
                    pe.wait_ge(sem("p0_masked"), g - 1)
                for j in range(GB):
                    kt = CT[:, g * TG + j * P:g * TG + (j + 1) * P]
                    ins = nc.tensor.matmul(B[h][:, j * P:(j + 1) * P], kt, kt, start=True, stop=True)
                ins.then_inc(sem("p0_scores"), 1)
                if g > 0:
                    finish_pe(pe, g)
                pe.wait_ge(sem("p0_masked"), g + 1)
                pe.wait_ge(sem("xhat_ready"), g + 1)
                if g > 0:
                    pe.wait_ge(sem("ysb_ready"), g)
                for j in range(GB):
                    o, q = Y[:, j * P:(j + 1) * P], xhat[h][:, j * P:(j + 1) * P]
                    nc.tensor.matmul(o, q, sm[h][:, j * P:(j + 1) * P], start=True, stop=False)
                    ins = nc.tensor.matmul(o, q, ident, start=False, stop=True)
                ins.then_inc(sem("y_ready"), 1)
                norm_pe(pe, g + 1, 1 - h)

        def p0_dve(dve, st):
            for g in range(NG):
                h = g % 2
                st.restart()
                dve.wait_ge(sem("p0_scores"), g + 1)
                if g >= 2:
                    dve.wait_ge(sem("y_ready"), g - 1)
                nc.vector.tensor_tensor(
                    sm[h][:].rearrange("p (j t) -> p j t", j=GB),
                    B[h][:].rearrange("p (j t) -> p j t", j=GB),
                    K("causal").unsqueeze(1).to_broadcast([P, GB, P]), ALU.mult).then_inc(sem("p0_masked"), 1)
                if g > 0:
                    finish_dve(dve, g - 1, g)
                if g + 1 < NG:
                    dve.wait_ge(sem(f"x_loaded{g + 1}"), 16)
                norm(dve, st, (g + 1) % NG, (g + 1, 1 - h))

        def p0_act(act):
            for g in range(NG):
                result_act(act, 0, g)
                norm_act(act, g + 1, (g + 1) % 2)
                weights_hi(act, 1, g)

        wqh = sb("wqh", [P, P])
        wkc = sb("wkc", [P, P])
        wvc = sb("wvc", [P, P])
        wvo = sb("wvo", [P, P])
        bcols = sb("bcols", [P, 16])
        slots = sb("slots", [SLOTS, P])
        mean_w = sb("mean_w", [SLOTS, 1])
        hs_t = sb("hs_t", [P, SLOTS])
        mean_t = sb("mean_t", [P, 1])
        b1x = sb("b1x", [SLOT_HID, 1])
        gh_rz = sb("gh_rz", [P, 2, SLOTS])
        gh_n = sb("gh_n", [P, SLOTS])
        brz = sb("brz", [P, 2])
        rtau = sb("rtau", [P, 1])
        maskb = sb("maskb", [P, GB, P], BF16)
        mtmp = sb("mtmp", [P, P])

        def setup_pe(pe):
            pe.wait_ge(sem("small_loaded"), 16)
            mm = nc.tensor.matmul
            mm(B[2][:, 0:P], S("hW"), S("qWT"), start=True, stop=True)
            mm(B[2][:, P:2 * P], S("cW"), S("kWT"), start=True, stop=True)
            mm(B[2][:, 2 * P:3 * P], S("cW"), S("vWT"), start=True, stop=True)
            mm(B[2][:, 3 * P:4 * P], S("wv"), S("woT"), start=True, stop=True)
            mm(B[3][:, 0:1], S("qWT"), S("hb"), start=True, stop=True)
            mm(B[3][:, 1:2], S("kWT"), S("cb"), start=True, stop=True)
            mm(B[3][:, 2:3], S("vWT"), S("cb"), start=True, stop=True)
            mm(B[3][:, 3:4], S("Wo4"), S("bv4"), start=True, stop=True)
            mm(B[3][:, 4:5], S("woT"), S("bv5"), start=True, stop=True)
            mm(B[3][:, 5:6], S("Wo6"), S("bv6"), start=True, stop=True).then_inc(sem("setup_mm"), 1)
            pe.wait_ge(sem("setup_slots"), 1)
            nc.tensor.transpose(B[4][:, 0:SLOTS], slots[:], ident[0:SLOTS, 0:SLOTS])
            mm(B[4][:, SLOTS:SLOTS + 1], slots[:], mean_w[:], start=True, stop=True).then_inc(sem("setup_mm"), 1)
            pe.wait_ge(sem("setup_slots"), 2)
            mm(B[5][0:SLOT_HID, 0:1], S("w1m"), mean_t[:], start=True, stop=True)
            for c in range(3):
                mm(B[5][:, SLOTS * (c + 1):SLOTS * (c + 2)], S("whh", c * P, (c + 1) * P), hs_t[:],
                   start=True, stop=True)
            pe.wait_ge(sem("setup_slots"), 3)
            mm(B[4][:, P:P + 1], S("oWT"), bcols[:, 2:3], start=True, stop=True).then_inc(sem("setup_mm"), 1)

        def setup_dve(dve, st):
            st.restart()
            v = nc.vector
            dve.wait_ge(sem("small_loaded"), 16)
            st.add(v.memset(mean_w[:], 1.0 / SLOTS))
            v.tensor_scalar(slots[:], S("slot_init"), S("slot_scale"), None, ALU.mult).then_inc(sem("setup_slots"), 1)
            dve.wait_ge(sem("setup_mm"), 1)
            for k, w in enumerate((wqh, wkc, wvc, wvo)):
                st.add(v.tensor_copy(w[:], B[2][:, k * P:(k + 1) * P]))
            for k, b in enumerate(("qb", "kb", "vb", "bo4", "bo5", "bo6")):
                st.add(v.tensor_tensor(bcols[:, k:k + 1], B[3][:, k:k + 1], S(b), ALU.add))
            st.add(v.tensor_tensor(brz[:], S("bih", 0, 2), S("bhh", 0, 2), ALU.add))
            st.add(v.tensor_scalar(rtau[:], S("tau"), -1.0, None, ALU.mult))
            st.settle()
            st.add(v.tensor_tensor(rtau[:], rtau[:], S("tau"), ALU.max))
            st.settle()
            st.add(v.tensor_scalar(rtau[:], rtau[:], 0.1, None, ALU.add))
            st.settle()
            st.add(v.reciprocal(rtau[:], rtau[:]))
            dve.wait_ge(sem("setup_mm"), 2)
            st.add(v.tensor_copy(hs_t[:], B[4][:, 0:SLOTS]))
            st.add(v.tensor_copy(mean_t[:], B[4][:, SLOTS:SLOTS + 1]))
            st.settle()
            v.engine_nop().then_inc(sem("setup_slots"), 2)
            dve.wait_ge(sem("setup_mm"), 3)
            st.add(v.tensor_tensor(b1x[:], B[5][0:SLOT_HID, 0:1], S("b1"), ALU.add))
            for c in range(2):
                st.add(v.tensor_scalar(gh_rz[:, c, :], B[5][:, SLOTS * (c + 1):SLOTS * (c + 2)],
                                       brz[:, c:c + 1], None, ALU.add))
            st.add(v.tensor_scalar(gh_n[:], B[5][:, 3 * SLOTS:4 * SLOTS], S("bhh", 2, 3), None, ALU.add))
            st.add(v.tensor_tensor(bcols[:, 6:7], B[4][:, P:P + 1], S("ob"), ALU.add))
            st.settle()
            for p, k in ((2, 6), (4, 3), (5, 4), (6, 5)):
                st.add(v.tensor_tensor(ybias[:, p:p + 1], bcols[:, k:k + 1], tgate[:, p:p + 1], ALU.mult))
            for p in (4, 6):
                for k in range(2):
                    st.add(v.tensor_scalar(bkm[p][:, k, :], S(f"bk{p}"), K("rowmask")[:, k:k + 1], None, ALU.mult))
            st.add(v.tensor_scalar(mtmp[:], mask_i[:], 0, None, ALU.is_equal))
            st.settle()
            st.add(v.tensor_scalar(maskb[:], mtmp[:].unsqueeze(1).to_broadcast([P, GB, P]), MASKED, None, ALU.mult))
            st.settle()
            v.engine_nop().then_inc(sem("setup_done"), 1)

        area1 = Area()
        su_lo = [area1.tile([P, TG], shared_r) for i in range(RING)]
        area1.at = 0
        su = [area1.tile([P, TG]) for i in range(RING)]
        sg = [area1.tile([P, TG]) for i in range(2)]
        su_hi = [area1.tile([P, TG], shared_r) for i in range(HI_RING)]
        x_hi = area1.tile([P, TG], shared_r)
        x_lo = area1.tile([P, TG], shared_r)
        cw_t = sb("cw_t", [96, TG], BF16)
        parts = sb("parts", [P, GB, 96], BF16)
        route = {}
        for p, m in MOE.items():
            E, NGR = m["E"], m["E"] // m["EG"]
            t = dict(
                vals=sb(f"vals{p}", [P, GB, E + 8 - m["K"]]), rep=sb(f"rep{p}", [P, GB, 8]),
                work=sb(f"work{p}", [P, GB, E + 8 - m["K"]]), m8=sb(f"m8_{p}", [P, GB, 8]),
                msk=sb(f"msk{p}", [P, GB, E]), sig=sb(f"sig{p}", [P, GB, E]),
                w=sb(f"w{p}", [P, GB, E]), tot=sb(f"tot{p}", [P, GB]), rec=sb(f"rec{p}", [P, GB]),
                comb=sb(f"comb{p}", [P, GB, E]), r1=sb(f"r1_{p}", [P, GB, E]),
                parts=parts)
            t["part"] = t["parts"][:, :, 0:3 * E].rearrange("p j (a e) -> p j a e", a=3)
            if m["GK"]:
                t.update(
                    s=sb(f"s{p}", [P, GB * NGR, 4]), pair=sb(f"pair{p}", [P, GB * NGR, 6]),
                    gv=sb(f"gv{p}", [P, GB, NGR + 8 - m["GK"]]), grep=sb(f"grep{p}", [P, GB, 8]),
                    gwork=sb(f"gwork{p}", [P, GB, NGR + 8 - m["GK"]]), gm=sb(f"gm{p}", [P, GB, NGR]),
                    gz=sb(f"gz{p}", [P, GB, NGR]), ms=sb(f"ms{p}", [P, GB * NGR, 4]))
            route[p] = t

        def route_setup(st):
            st.add(nc.vector.memset(parts[:], 0.0))
            for p, m in MOE.items():
                t = route[p]
                st.add(nc.vector.memset(t["vals"][:], LOWEST))
                st.add(nc.vector.memset(t["rep"][:], LOWEST))
                if m["GK"]:
                    st.add(nc.vector.memset(t["gv"][:], LOWEST))
                    st.add(nc.vector.memset(t["grep"][:], LOWEST))
            st.settle()

        def top_k(st, vals, m8, rep, work, k):
            for j in range(GB):
                st.add(nc.vector.max(out=m8[:, j, :], in_=vals[:, j, :]))
            st.settle()
            if k < 8:
                st.add(nc.vector.tensor_copy(rep[:, :, 0:k], m8[:, :, 0:k]))
                st.settle()
            else:
                rep = m8
            yield
            for j in range(GB):
                st.add(nc.vector.match_replace(out=work[:, j, :], in_to_replace=rep[:, j, :],
                                               in_values=vals[:, j, :], imm_value=TAKEN))
            st.settle()

        def split(st, t):
            v, parts = nc.vector, t["part"]
            st.add(v.tensor_copy(parts[:, :, 0, :], t["comb"][:]))
            st.settle()
            st.add(v.tensor_tensor(t["r1"][:], t["comb"][:], parts[:, :, 0, :], ALU.subtract))
            st.settle()
            st.add(v.tensor_copy(parts[:, :, 1, :], t["r1"][:]))
            st.settle()
            v.tensor_tensor(parts[:, :, 2, :], t["r1"][:], parts[:, :, 1, :], ALU.subtract)\
                .then_inc(sem("weights_ready"), 1)

        def per_expert(a, E):
            return a.unsqueeze(2).to_broadcast([P, GB, E])

        def normed(dve, st, t, E, factor, eps):
            v = nc.vector
            st.add(v.tensor_reduce(t["tot"][:], t["w"][:], AX.X, ALU.add))
            st.settle()
            st.add(v.tensor_scalar(t["tot"][:], t["tot"][:], eps, None, ALU.add))
            st.settle()
            st.add(v.reciprocal(t["rec"][:], t["tot"][:]))
            st.settle()
            st.add(v.scalar_tensor_tensor(t["comb"][:], t["w"][:], factor, per_expert(t["rec"][:], E),
                                          ALU.mult, ALU.mult))
            st.settle()

        def route_top2(dve, st, p, g):
            m, t, v = MOE[p], route[p], nc.vector
            E = m["E"]
            dve.wait_ge(sem(f"logits{p}"), g + 1)
            st.add(v.tensor_copy(t["vals"][:, :, 0:E], B[5][:, 0:GB * E].rearrange("p (j e) -> p j e", j=GB)))
            st.settle()
            yield
            yield from top_k(st, t["vals"], t["m8"], t["rep"], t["work"], m["K"])
            v.tensor_tensor(t["r1"][:], t["vals"][:, :, 0:E], t["m8"][:, :, 0:1].to_broadcast([P, GB, E]),
                            ALU.subtract).then_inc(sem("shifted"), 1)
            st.add(v.tensor_scalar(t["msk"][:], t["work"][:, :, 0:E], TAKEN, None, ALU.is_equal))
            st.settle()
            yield
            yield
            dve.wait_ge(sem("exp_ready"), g + 1)
            st.add(v.tensor_tensor(t["w"][:], t["sig"][:], t["msk"][:], ALU.mult))
            st.settle()
            normed(dve, st, t, E, 1.0, 0.0)
            yield
            split(st, t)

        def route_groups(dve, st, p, g):
            m, t, v = MOE[p], route[p], nc.vector
            E, NGR = m["E"], m["E"] // m["EG"]
            dve.wait_ge(sem(f"sig_ready{p}"), g + 1)
            st.add(v.tensor_tensor(t["s"][:].rearrange("p (j n) e -> p j (n e)", j=GB), t["sig"][:],
                                   S(f"rb{p}").unsqueeze(1).to_broadcast([P, GB, E]), ALU.add))
            st.settle()
            at = 0
            for d in (1, 2, 3):
                st.add(v.tensor_tensor(t["pair"][:, :, at:at + 4 - d], t["s"][:, :, 0:4 - d],
                                       t["s"][:, :, d:4], ALU.add))
                at += 4 - d
            st.settle()
            st.add(v.tensor_reduce(t["gv"][:, :, 0:NGR], t["pair"][:].rearrange("p (j n) e -> p j n e", j=GB),
                                   AX.X, ALU.max))
            st.settle()
            yield
            yield from top_k(st, t["gv"], t["m8"], t["grep"], t["gwork"], m["GK"])
            st.add(v.tensor_scalar(t["gm"][:], t["gwork"][:, :, 0:NGR], TAKEN, None, ALU.is_equal))
            st.settle()
            yield
            fill = -1.0 if p == 3 else 0.0
            gm = t["gm"][:].rearrange("p j n -> p (j n)").unsqueeze(2).to_broadcast([P, GB * NGR, 4])
            st.add(v.tensor_tensor(t["ms"][:], t["s"][:], gm, ALU.mult))
            if fill:
                st.add(v.tensor_scalar(t["gz"][:], t["gm"][:], 1.0, -fill, ALU.subtract, ALU.mult))
            st.settle()
            vals = t["vals"][:, :, 0:E]
            if fill:
                gz = t["gz"][:].rearrange("p j n -> p (j n)").unsqueeze(2).to_broadcast([P, GB * NGR, 4])
                st.add(v.tensor_tensor(t["ms"][:], t["ms"][:], gz, ALU.add))
                st.settle()
            st.add(v.tensor_scalar(vals, t["ms"][:].rearrange("p (j n) e -> p j (n e)", j=GB), 0.0, None, ALU.add))
            st.settle()
            yield
            yield from top_k(st, t["vals"], t["m8"], t["rep"], t["work"], m["K"])
            st.add(v.tensor_scalar(t["msk"][:], t["work"][:, :, 0:E], TAKEN, None, ALU.is_equal))
            st.settle()
            st.add(v.tensor_tensor(t["w"][:], t["sig"][:], t["msk"][:], ALU.mult))
            st.settle()
            normed(dve, st, t, E, SCALE_ROUTED, 1e-20)
            yield
            split(st, t)

        FINISH_AT, STATS_AT, NORM_AT, NORMED_AT = 9, 10, 12, 14
        MOE_NO = {1: 0, 3: 1, 7: 2}
        def by_pool(c):
            return c % 2 == 1

        def product(out, w, cols, hi, lo, start=True, stop=True):
            nc.tensor.matmul(out, w_hi[w][:, cols], lo, start=start, stop=False)
            nc.tensor.matmul(out, w_hi[w][:, cols], hi, start=False, stop=False)
            return nc.tensor.matmul(out, w_lo[w][:, cols], hi, start=False, stop=stop)

        def moe_pe(pe, p):
            m = MOE[p]
            NC, NR, E = m["NC"], m["NR"], m["E"]
            pe.wait_ge(sem(f"w_lo{p}"), NG)
            pe.wait_ge(sem("constb_loaded"), 16)
            for g, _, _, h in stages(pe, p):
                s = NG * p + g
                pe.wait_ge(sem("xhat_t_ready"), s + 1)
                for j in range(GB):
                    ins = nc.tensor.matmul(B[5][:, j * E:(j + 1) * E], xhat_t[h][:, j * P:(j + 1) * P], S(f"Wr{p}"),
                                           start=True, stop=True)
                ins.then_inc(sem(f"logits{p}"), 1)
                pe.wait_ge(sem("x_lo_ready"), (NG + 1) * MOE_NO[p] + g + 1)
                for i in range(NC + DOWN):
                    if i < NC:
                        if i >= 2:
                            pe.wait_ge(sem(f"su_ready{p}"), g * NC + i - 1)
                        w = slice(i * P, (i + 1) * P)
                        product(B[i % 2][:], 0, w, x_hi, x_lo).then_inc(sem(f"gate_mm{p}"), 1)
                        product(B[2 + i % 2][:], 1, w, x_hi, x_lo).then_inc(sem(f"up_mm{p}"), 1)
                    if i == TURN - 1:
                        pe.wait_ge(sem("weights_ready"), NG * MOE_NO[p] + g + 1)
                        for j in range(GB):
                            ins = nc.tensor.transpose(
                                B[4][0:96, 0:TG // 2].bitcast(BF16)[:, j * P:(j + 1) * P],
                                route[p]["parts"][:, j, :], identb)
                        ins.then_inc(sem(f"cw_mm{p}"), 1)
                    if i == FINISH_AT:
                        finish_pe(pe, s)
                    if i == NORMED_AT:
                        norm_pe(pe, s + 1, 1 - h)
                    c = i - TURN
                    if 0 <= c < NR:
                        if c == 0:
                            pe.wait_ge(sem(f"cw_ready{p}"), g + 1)
                        if c >= 2:
                            pe.wait_ge(sem(f"hh_ready{p}"), g * NR + c - 1)
                        at = SEL_AT[p] + c * P
                        nc.tensor.matmul(B[4 + c % 2][:], constb[0:3 * E, at:at + P], cw_t[0:3 * E, :],
                                         start=True, stop=True).then_inc(sem(f"bc_mm{p}"), 1)
                    c = i - DOWN
                    if 0 <= c < NC:
                        if c == 0:
                            pe.wait_ge(sem("ysb_ready"), s)
                        if by_pool(c):
                            pe.wait_ge(sem(f"lo_pool{p}"), g * (NC // 2) + c // 2 + 1)
                        else:
                            pe.wait_ge(sem(f"lo_dve{p}"), g * (NC - NC // 2) + c // 2 + 1)
                        product(Y[:], 2, slice(c * P, (c + 1) * P), su_hi[c % HI_RING], su_lo[c % RING],
                                start=(c == 0), stop=(c == NC - 1))\
                            .then_inc(sem(f"down_mm{p}") if c < NC - 1 else sem("y_ready"), 1)

        def x_parts_act(act, p, s, h):
            act.wait_ge(sem("xhat_t_ready"), s + 1)
            nc.scalar.copy(x_hi, xhat_t[h][:]).then_inc(sem("x_hi_ready"), 1)

        def x_parts_dve(dve, p, g, h):
            dve.wait_ge(sem("x_hi_ready"), (NG + 1) * MOE_NO[p] + g + 2)
            nc.vector.tensor_tensor(x_lo, xhat_t[h][:], x_hi.bitcast(F32), ALU.subtract).then_inc(sem("x_lo_ready"), 1)

        def moe_act(act, p):
            m = MOE[p]
            NC, NR, E = m["NC"], m["NR"], m["E"]
            act.wait_ge(sem("y_ready"), NG * p)
            x_parts_act(act, p, NG * p, 0)
            for g, _, _, h in stages(act, p):
                s = NG * p + g
                for i in range(NC + DOWN):
                    if i < NC:
                        act.wait_ge(sem(f"gate_mm{p}"), g * NC + i + 1)
                        if i >= 2:
                            act.wait_ge(sem(f"su_ready{p}"), g * NC + i - 1)
                        nc.scalar.activation(sg[i % 2][:], B[i % 2][:], ACT.Silu).then_inc(sem(f"sg_ready{p}"), 1)
                    if m["GK"] and i == 1:
                        act.wait_ge(sem(f"logits{p}"), g + 1)
                        nc.scalar.activation(route[p]["sig"][:], B[5][:, 0:GB * E].rearrange("p (j e) -> p j e", j=GB),
                                             ACT.Sigmoid).then_inc(sem(f"sig_ready{p}"), 1)
                    if not m["GK"] and i == 5:
                        act.wait_ge(sem("shifted"), g + 1)
                        nc.scalar.activation(route[p]["sig"][:], route[p]["r1"][:], ACT.Exp)\
                            .then_inc(sem("exp_ready"), 1)
                    if i == TURN - 1:
                        act.wait_ge(sem(f"cw_mm{p}"), g + 1)
                        nc.scalar.copy(cw_t[0:3 * E, :], B[4][0:3 * E, 0:TG // 2].bitcast(BF16))\
                            .then_inc(sem(f"cw_ready{p}"), 1)
                    if i == NORMED_AT:
                        norm_act(act, s + 1, 1 - h)
                    if i == NC + 1:
                        act.wait_ge(sem(f"up_mm{p}"), NC * (g + 1))
                        x_parts_act(act, p, s + 1, 1 - h)
                    c = i - TURN - 1
                    if 0 <= c < NC:
                        if c < NR:
                            act.wait_ge(sem(f"hh_ready{p}"), g * NR + c + 1)
                        else:
                            act.wait_ge(sem(f"su_ready{p}"), g * NC + c + 1)
                        if c >= HI_RING:
                            act.wait_ge(sem(f"down_mm{p}"), g * (NC - 1) + c - HI_RING + 1)
                        nc.scalar.copy(su_hi[c % HI_RING], su[c % RING]).then_inc(sem(f"hi_ready{p}"), 1)
                result_act(act, p, s)

        def low_part(eng, ops, p, g, c, name):
            eng.wait_ge(sem(f"hi_ready{p}"), g * MOE[p]["NC"] + c + 1)
            ops.tensor_tensor(su_lo[c % RING], su[c % RING], su_hi[c % HI_RING].bitcast(F32), ALU.subtract)\
                .then_inc(sem(f"{name}{p}"), 1)

        def moe_pool(pool, p, g):
            for c in range(MOE[p]["NC"]):
                if by_pool(c):
                    low_part(pool, nc.gpsimd, p, g, c, "lo_pool")

        def moe_dve(dve, st, p):
            m = MOE[p]
            NC, NR = m["NC"], m["NR"]
            x_parts_dve(dve, p, -1, 0)
            for g, before, after, h in stages(dve, p, st):
                s = NG * p + g
                pieces = route_groups(dve, st, p, g) if m["GK"] else route_top2(dve, st, p, g)
                for i in range(NC + DOWN):
                    if i >= 2:
                        next(pieces, None)
                    if i < NC:
                        dve.wait_ge(sem(f"sg_ready{p}"), g * NC + i + 1)
                        dve.wait_ge(sem(f"up_mm{p}"), g * NC + i + 1)
                        if i == 0:
                            dve.wait_ge(sem("y_ready"), s)
                        elif i >= RING:
                            dve.wait_ge(sem(f"down_mm{p}"), g * (NC - 1) + i - RING + 1)
                        nc.vector.tensor_tensor(su[i % RING], sg[i % 2][:], B[2 + i % 2][:], ALU.mult)\
                            .then_inc(sem(f"su_ready{p}"), 1)
                    if i == FINISH_AT:
                        finish_dve(dve, before, s)
                    if i == STATS_AT:
                        norm_stats(st, after)
                    if i == NORM_AT:
                        norm_apply(dve, after, s + 1, 1 - h)
                    if i == NC + 2:
                        x_parts_dve(dve, p, g, 1 - h)
                    c = i - TURN
                    if 0 <= c < NR:
                        dve.wait_ge(sem(f"bc_mm{p}"), g * NR + c + 1)
                        dve.wait_ge(sem(f"su_ready{p}"), g * NC + c + 1)
                        nc.vector.tensor_tensor(su[c % RING], su[c % RING], B[4 + c % 2][:], ALU.mult)\
                            .then_inc(sem(f"hh_ready{p}"), 1)
                    c -= 2
                    if 0 <= c < NC and not by_pool(c):
                        low_part(dve, nc.vector, p, g, c, "lo_dve")

        area2 = Area()
        q2 = area2.tile([P, TG])
        k2 = area2.tile([P, TG])
        v2 = area2.tile([P, TG])
        pr2 = area2.tile([P, TG])
        pn2 = area2.tile([P, TG])
        pt2 = area2.tile([P, TG])
        aq2 = area2.tile([P, TG])
        mx2 = sb("mx2", [P, GB])
        nb2 = sb("nb2", [P, GB])
        rs2 = sb("rs2", [P, GB])
        ri2 = sb("ri2", [P, GB])
        SCALE2 = float(P) ** -0.5

        def p2_pe(pe):
            p, mm = 2, nc.tensor.matmul
            for g, _, _, h in stages(pe, p):
                s = NG * p + g
                pe.wait_ge(sem("cg_ready"), g + 1)
                mm(B[0][:], wkc[:], cg[h][:], start=True, stop=True).then_inc(sem("k_mm2"), 1)
                for j in range(GB):
                    ins = mm(B[1][:, j * P:(j + 1) * P], cg[h][:, j * P:(j + 1) * P], wvc[:], start=True, stop=True)
                ins.then_inc(sem("v_mm2"), 1)
                pe.wait_ge(sem("xhat_t_ready"), s + 1)
                mm(B[2][:], wqh[:], xhat_t[h][:], start=True, stop=True).then_inc(sem("q_mm2"), 1)
                finish_pe(pe, s)
                pe.wait_ge(sem("qk_ready2"), 2 * g + 2)
                for j in range(GB):
                    t = slice(j * P, (j + 1) * P)
                    ins = mm(B[3][:, t], q2[:, t], k2[:, t], start=True, stop=True)
                ins.then_inc(sem("score_mm2"), 1)
                norm_pe(pe, s + 1, 1 - h)
                pe.wait_ge(sem("pn_ready2"), g + 1)
                for j in range(GB):
                    t = slice(j * P, (j + 1) * P)
                    ins = nc.tensor.transpose(B[4][:, t], pn2[:, t], ident)
                ins.then_inc(sem("pt_mm2"), 1)
                pe.wait_ge(sem("v_ready2"), g + 1)
                pe.wait_ge(sem("pt_ready2"), g + 1)
                for j in range(GB):
                    t = slice(j * P, (j + 1) * P)
                    ins = mm(B[5][:, t], v2[:, t], pt2[:, t], start=True, stop=True)
                ins.then_inc(sem("av_mm2"), 1)
                pe.wait_ge(sem("aq_ready2"), g + 1)
                pe.wait_ge(sem("ysb_ready"), s)
                mm(Y[:], S("oWT"), aq2[:], start=True, stop=True).then_inc(sem("y_ready"), 1)

        def p2_act(act):
            p = 2
            for g, _, _, h in stages(act, p):
                s = NG * p + g
                act.wait_ge(sem("k_mm2"), g + 1)
                nc.scalar.activation(k2[:], B[0][:], ACT.Identity, bias=bcols[:, 1:2]).then_inc(sem("qk_ready2"), 1)
                act.wait_ge(sem("q_mm2"), g + 1)
                nc.scalar.activation(q2[:], B[2][:], ACT.Identity, bias=bcols[:, 0:1]).then_inc(sem("qk_ready2"), 1)
                act.wait_ge(sem("nb_ready2"), g + 1)
                for j in range(GB):
                    t = slice(j * P, (j + 1) * P)
                    ins = nc.scalar.activation(pr2[:, t], B[3][:, t], ACT.Exp, bias=nb2[:, j:j + 1], scale=SCALE2,
                                               accum_out=rs2[:, j:j + 1])
                ins.then_inc(sem("exp_ready2"), 1)
                norm_act(act, s + 1, 1 - h)
                act.wait_ge(sem("pt_mm2"), g + 1)
                nc.scalar.copy(pt2[:], B[4][:]).then_inc(sem("pt_ready2"), 1)
                result_act(act, p, s)

        def p2_dve(dve, st):
            p, v = 2, nc.vector
            for g, before, after, h in stages(dve, p, st):
                s = NG * p + g
                dve.wait_ge(sem("v_mm2"), g + 1)
                v.tensor_copy(v2[:], B[1][:]).then_inc(sem("v_ready2"), 1)
                finish_dve(dve, before, s)
                dve.wait_ge(sem("score_mm2"), g + 1)
                st.add(v.tensor_reduce(mx2[:], B[3][:].rearrange("p (j k) -> p j k", j=GB), AX.X, ALU.max))
                st.settle()
                v.tensor_scalar(nb2[:], mx2[:], -SCALE2, None, ALU.mult).then_inc(sem("nb_ready2"), 1)
                norm(dve, st, after, (s + 1, 1 - h))
                dve.wait_ge(sem("exp_ready2"), g + 1)
                st.add(v.reciprocal(ri2[:], rs2[:]))
                st.settle()
                v.tensor_tensor(pn2[:].rearrange("p (j k) -> p j k", j=GB), pr2[:].rearrange("p (j k) -> p j k", j=GB),
                                ri2[:].unsqueeze(2).to_broadcast([P, GB, P]), ALU.mult).then_inc(sem("pn_ready2"), 1)
                dve.wait_ge(sem("av_mm2"), g + 1)
                v.tensor_tensor(aq2[:], B[5][:], q2[:], ALU.add).then_inc(sem("aq_ready2"), 1)

        area4 = Area()
        qh = [area4.tile([P, TG]) for i in range(HEAD_TILES)]
        kh = [[area4.tile([P, TG]) for i in range(HEAD_TILES)] for v in range(2)]
        sd = [area4.tile([P, TG]) for i in range(2)]
        es = [area4.tile([P, TG]) for i in range(2)]
        pt = [area4.tile([P, TG]) for i in range(2)]
        os = area4.tile([P, TG])
        osb = area4.tile([P, GB, HEADS, DK])
        oT = area4.tile([P, TG])
        oc = area4.tile([P, 2, HEADS // 2, DK])
        vh = sb("vh", [P, GB * HEADS, VW])
        vc = sb("vc", [P, GB * HEADS // 4, 2 * VW])
        mxh = [sb(f"mxh{i}", [P, HEAD_TILES]) for i in range(2)]
        rden = sb("rden", [P, GB * HEAD_TILES])
        bkm = {p: sb(f"bkm{p}", [P, 2, HEAD_TILES]) for p in (4, 6)}
        SCALEH = float(DK) ** -0.5
        UNITS = [(j, a) for a in range(HEADS // HEAD_TILES) for j in range(GB)]
        NU = len(UNITS)

        def coarse(p, a):
            return p == 6 and a >= 2

        def width(p, a):
            return HALF if coarse(p, a) else P

        def heads_pe(pe, p):
            mm = nc.tensor.matmul
            base = 0 if p == 4 else NG
            for g, _, _, h in stages(pe, p):
                s = NG * p + g
                pe.wait_ge(sem("cg_ready"), NG * (1 if p == 4 else 2) + g + 1)
                for i in range(HEAD_TILES):
                    mm(B[i][:], S(f"Wk{p}", i * P, (i + 1) * P), cg[h][:], start=True, stop=True)\
                        .then_inc(sem(f"proj_mm{p}"), 1)
                for j in range(GB):
                    ins = mm(B[4][:, j * P:(j + 1) * P], cg[h][:, j * P:(j + 1) * P], S(f"Wv{p}"),
                             start=True, stop=True)
                if p == 6:
                    rows, at, _ = SMALL_AT["Wv6"]
                    for j in range(GB):
                        ins = mm(B[5][0:HALF, j * HALF:(j + 1) * HALF], cg[h][:, j * P:(j + 1) * P:2],
                                 small[:, at + HALF:at + P], start=True, stop=True)
                ins.then_inc(sem(f"v_mm{p}"), 1)
                pe.wait_ge(sem("xhat_t_ready"), s + 1)
                for i in range(HEAD_TILES):
                    pe.wait_ge(sem(f"proj_{'act' if i < 2 else 'dve'}{p}"), 4 * g + i % 2 + 1)
                    mm(B[i][:], S(f"Wq{p}", i * P, (i + 1) * P), xhat_t[h][:], start=True, stop=True)\
                        .then_inc(sem(f"proj_mm{p}"), 1)
                finish_pe(pe, s)
                pe.wait_ge(sem(f"proj_act{p}"), 4 * g + 4)
                pe.wait_ge(sem(f"proj_dve{p}"), 4 * g + 4)
                pe.wait_ge(sem(f"v_ready{p}"), g + 1)
                for t in range(NU + 6):
                    if t < NU:
                        j, a = UNITS[t]
                        w, rows = width(p, a), slice(64 * (a // 2), 64 * (a // 2) + 64)
                        if t >= 2:
                            pe.wait_ge(sem(f"sd_ready{p}"), NU * g + t - 1)
                        bank = B[t % 2]
                        if p == 4:
                            mm(bank[:], identb, maskb[:].rearrange("p a k -> p (a k)"), start=True, stop=False,
                               skip_group_check=True)
                        elif w < P:
                            mm(bank[:, 0:2], identb, identb[:, 0:2], start=True, stop=True)
                        for i in range(HEAD_TILES):
                            cols = slice(j * P, (j + 1) * P, P // w)
                            ins = mm(bank[0:w, i * w:(i + 1) * w], qh[i][rows, cols], kh[a % 2][i][rows, cols],
                                     start=(p == 6), stop=True, skip_group_check=(p == 4))
                        ins.then_inc(sem(f"score_mm{p}"), 1)
                    if t == 9:
                        norm_pe(pe, s + 1, 1 - h)
                    u = t - 2
                    if 0 <= u < NU:
                        j, a = UNITS[u]
                        w = width(p, a)
                        pe.wait_ge(sem(f"es_ready{p}"), NU * g + u + 1)
                        if u >= 2:
                            pe.wait_ge(sem(f"pt_ready{p}"), NU * g + u - 1)
                        for i in range(4 * w // P):
                            c = slice(i * P, (i + 1) * P)
                            ins = nc.tensor.transpose(B[2 + u % 2][:, c], es[u % 2][:, c], ident)
                        ins.then_inc(sem(f"pt_mm{p}"), 1)
                    u = t - 3
                    if 0 <= u < NU:
                        j, a = UNITS[u]
                        w = width(p, a)
                        pe.wait_ge(sem(f"pt_ready{p}"), NU * g + u + 1)
                        if j == 0 and a >= 2:
                            pe.wait_ge(sem(f"os_ready{p}"), 4 * g + a - 1)
                        heads = P // w
                        for i in range(0, HEAD_TILES, heads):
                            if coarse(p, a):
                                val = vc[:, j * (HEADS // 4) + 2 * (a - 2) + i // 2, :]
                            else:
                                val = vh[:, j * HEADS + 4 * a + i, :]
                            ins = mm(B[4 + a % 2][VW * i:VW * (i + heads), j * w:(j + 1) * w], val,
                                     pt[u % 2][:, i // heads * w:(i // heads + 1) * w], start=True, stop=True)
                        ins.then_inc(sem(f"pv_mm{p}"), 1)
                    a = t // 4 - 2
                    if t % 4 == 0 and a >= 0:
                        pe.wait_ge(sem(f"os_ready{p}"), 4 * g + a + 1)
                        if a == 0:
                            pe.wait_ge(sem("ysb_ready"), s)
                        else:
                            pe.wait_ge(sem(f"osb_ready{p}"), 4 * g + a)
                        for x in range(GB * width(p, a) // P):
                            ins = nc.tensor.transpose(Y[:, x * P:(x + 1) * P], os[:, x * P:(x + 1) * P], ident)
                        ins.then_inc(sem(f"ob_mm{p}"), 1)
                pe.wait_ge(sem(f"osb_ready{p}"), 4 * g + 4)
                if p == 6:
                    for y in range(2):
                        ins = mm(B[2][:, y * P:(y + 1) * P], K("up")[:, y * P:(y + 1) * P],
                                 oc[:].rearrange("p x n d -> p (x n d)"), start=True, stop=True)
                    ins.then_inc(sem("up_mm"), 1)
                    pe.wait_ge(sem("up_ready"), g + 1)
                for j in range(GB):
                    ins = nc.tensor.transpose(B[3][:, j * P:(j + 1) * P],
                                              osb[:, j, :, :].rearrange("p n d -> p (n d)"), ident)
                ins.then_inc(sem(f"oT_mm{p}"), 1)
                pe.wait_ge(sem(f"oT_ready{p}"), g + 1)
                mm(Y[:], S(f"Wo{p}"), oT[:], start=True, stop=True).then_inc(sem("y_ready"), 1)

        def heads_act(act, p):
            for g, _, _, h in stages(act, p):
                s = NG * p + g
                n = 2 * HEAD_TILES * g
                for i in range(2):
                    act.wait_ge(sem(f"proj_mm{p}"), n + i + 1)
                    for v in range(2):
                        ins = nc.scalar.activation(kh[v][i][:], B[i][:], ACT.Identity, scale=K("rowmask")[:, v:v + 1],
                                                   bias=bkm[p][:, v, i:i + 1])
                    ins.then_inc(sem(f"proj_act{p}"), 1)
                for i in range(2):
                    act.wait_ge(sem(f"proj_mm{p}"), n + HEAD_TILES + i + 1)
                    nc.scalar.activation(qh[i][:], B[i][:], ACT.Identity, bias=S(f"bq{p}", i, i + 1))\
                        .then_inc(sem(f"proj_act{p}"), 1)
                for t in range(NU + 4):
                    a = (t - 7) // 4
                    if t >= 7 and (t - 7) % 4 == 0:
                        act.wait_ge(sem(f"pv_mm{p}"), NU * g + 4 * a + 4)
                        if a >= 1:
                            act.wait_ge(sem(f"ob_mm{p}"), 4 * g + a)
                        nc.scalar.copy(os[:, 0:GB * width(p, a)], B[4 + a % 2][:, 0:GB * width(p, a)])\
                            .then_inc(sem(f"os_ready{p}"), 1)
                    if t < NU:
                        j, a = UNITS[t]
                        w = width(p, a)
                        act.wait_ge(sem(f"sd_ready{p}"), NU * g + t + 1)
                        if t >= 2:
                            act.wait_ge(sem(f"pt_mm{p}"), NU * g + t - 1)
                        nc.scalar.activation(es[t % 2][0:w, 0:4 * w], sd[t % 2][0:w, 0:4 * w], ACT.Exp,
                                             scale=SCALEH).then_inc(sem(f"es_ready{p}"), 1)
                    if t == 10:
                        norm_act(act, s + 1, 1 - h)
                    u = t - 1
                    if 0 <= u < NU:
                        j, a = UNITS[u]
                        w = width(p, a)
                        act.wait_ge(sem(f"pt_mm{p}"), NU * g + u + 1)
                        if u >= 2:
                            act.wait_ge(sem(f"pv_mm{p}"), NU * g + u - 1)
                        nc.scalar.copy(pt[u % 2][:, 0:4 * w * w // P].rearrange("p (i q) -> p i q", q=w),
                                       B[2 + u % 2][:, 0:4 * w].rearrange("p (i q) -> p i q", q=P)[:, :, 0:w])\
                            .then_inc(sem(f"pt_ready{p}"), 1)
                act.wait_ge(sem(f"oT_mm{p}"), g + 1)
                nc.scalar.copy(oT[:], B[3][:]).then_inc(sem(f"oT_ready{p}"), 1)
                result_act(act, p, s)

        def heads_dve(dve, st, p):
            v = nc.vector
            for g, before, after, h in stages(dve, p, st):
                s = NG * p + g
                n = 2 * HEAD_TILES * g
                for i in range(2, HEAD_TILES):
                    dve.wait_ge(sem(f"proj_mm{p}"), n + i + 1)
                    for k in range(2):
                        ins = v.tensor_scalar(kh[k][i][:], B[i][:], K("rowmask")[:, k:k + 1], bkm[p][:, k, i:i + 1],
                                              ALU.mult, ALU.add)
                    ins.then_inc(sem(f"proj_dve{p}"), 1)
                dve.wait_ge(sem(f"v_mm{p}"), g + 1)
                ins = v.tensor_copy(vh[:, :, 0:DK], B[4][:].rearrange("p (n d) -> p n d", d=DK))
                if p == 6:
                    for k in range(2):
                        ins = v.tensor_copy(
                            vc[k * HALF:(k + 1) * HALF, :, k * VW:k * VW + DK],
                            B[5][0:HALF, 0:GB * HALF].rearrange("p (n k d) -> p n k d", k=2, d=DK)[:, :, k, :])
                ins.then_inc(sem(f"v_ready{p}"), 1)
                for i in range(2, HEAD_TILES):
                    dve.wait_ge(sem(f"proj_mm{p}"), n + HEAD_TILES + i + 1)
                    v.tensor_scalar(qh[i][:], B[i][:], S(f"bq{p}", i, i + 1), None, ALU.add)\
                        .then_inc(sem(f"proj_dve{p}"), 1)
                finish_dve(dve, before, s)
                for t in range(NU + 6):
                    a = (t - 9) // 4
                    if t >= 9 and (t - 9) % 4 == 0:
                        c = coarse(p, a)
                        n = GB * width(p, a) // 32
                        back = Y[:, 0:n * 32].rearrange("p (n d) -> p n d", d=32)
                        dve.wait_ge(sem(f"ob_mm{p}"), 4 * g + a + 1)
                        st.add(v.reciprocal(rden[:, 0:n], back[:, :, DK]))
                        st.settle()
                        dst = oc[:, :, 4 * (a - 2):4 * (a - 1), :] if c else osb[:, :, 4 * a:4 * a + 4, :]
                        v.tensor_tensor(dst, back[:, :, 0:DK].rearrange("p (x i) d -> p x i d", i=HEAD_TILES),
                                        rden[:, 0:n].rearrange("p (x i) -> p x i", i=HEAD_TILES).unsqueeze(3)
                                        .to_broadcast([P, n // 4, 4, DK]), ALU.mult).then_inc(sem(f"osb_ready{p}"), 1)
                    if t >= NU:
                        continue
                    j, a = UNITS[t]
                    w = width(p, a)
                    bank = B[t % 2][0:w, 0:4 * w].rearrange("p (i k) -> p i k", i=4)
                    dve.wait_ge(sem(f"score_mm{p}"), NU * g + t + 1)
                    st.add(v.tensor_reduce(mxh[t % 2][0:w, :], bank, AX.X, ALU.max))
                    st.settle()
                    if t >= 2:
                        dve.wait_ge(sem(f"es_ready{p}"), NU * g + t - 1)
                    v.tensor_tensor(sd[t % 2][0:w, 0:4 * w].rearrange("p (i k) -> p i k", i=4), bank,
                                    mxh[t % 2][0:w, :].unsqueeze(2).to_broadcast([w, 4, w]), ALU.subtract)\
                        .then_inc(sem(f"sd_ready{p}"), 1)
                    if t == 4:
                        norm_stats(st, after)
                    if t == 6:
                        norm_apply(dve, after, s + 1, 1 - h)
                if p == 6:
                    dve.wait_ge(sem("up_mm"), g + 1)
                    v.tensor_copy(osb[:, :, 8:16, :].rearrange("p (x y) n d -> p y x (n d)", y=2),
                                  B[2][:, 0:2 * P].rearrange("p (y x n) -> p y x n", y=2, x=2))\
                        .then_inc(sem("up_ready"), 1)

        h5 = sb("h5", [SLOT_HID + 1, TG])
        area5 = Area()
        lg5 = area5.tile([P, GB, SLOTS])
        m85 = area5.tile([P, GB, 8])
        wk5 = area5.tile([P, GB, SLOTS])
        e5 = area5.tile([P, GB, SLOTS])
        tot5 = sb("tot5", [P, GB])
        rec5 = sb("rec5", [P, GB])
        al5 = area5.tile([P, GB, SLOTS])
        at5 = area5.tile([SLOTS, TG])
        ones5 = sb("ones5", [P, P])
        NS = GB * SLOTS
        ws5 = area5.tile([P, NS])
        gi5 = area5.tile([P, NS])
        rz5 = area5.tile([P, 2, NS])
        t5 = area5.tile([P, NS])
        n5 = area5.tile([P, NS])
        hn5 = area5.tile([P, NS])
        sv5 = area5.tile([SLOTS, TG])

        def p5_pe(pe):
            p, mm = 5, nc.tensor.matmul
            for g, _, _, h in stages(pe, p):
                s = NG * p + g
                pe.wait_ge(sem("xhat_t_ready"), s + 1)
                mm(B[0][0:SLOT_HID, :], S("w1x"), xhat_t[h][:], start=True, stop=True).then_inc(sem("h_mm5"), 1)
                finish_pe(pe, s)
                pe.wait_ge(sem("h_ready5"), g + 1)
                for j in range(GB):
                    ins = mm(B[1][:, j * SLOTS:(j + 1) * SLOTS], h5[:, j * P:(j + 1) * P], S("w2"), start=True, stop=True)
                ins.then_inc(sem("logit_mm5"), 1)
                norm_pe(pe, s + 1, 1 - h)
                pe.wait_ge(sem("al_ready5"), g + 1)
                for j in range(GB):
                    mm(B[2][:, j * SLOTS:(j + 1) * SLOTS], xhat[h][:, j * P:(j + 1) * P], al5[:, j, :], start=True, stop=True)
                mm(B[3][:, 0:NS], ones5[:], al5[:].rearrange("p j s -> p (j s)"), start=True, stop=True)\
                    .then_inc(sem("in_mm5"), 1)
                for j in range(GB):
                    ins = nc.tensor.transpose(B[0][0:SLOTS, j * P:(j + 1) * P], al5[:, j, :], ident)
                ins.then_inc(sem("at_mm5"), 1)
                pe.wait_ge(sem("gi_ready5"), g + 1)
                for c in range(2):
                    mm(B[4][:, c * NS:(c + 1) * NS], S("wih", c * P, (c + 1) * P), gi5[:], start=True, stop=True)
                mm(B[5][:, 0:NS], S("wih", 2 * P, 3 * P), gi5[:], start=True, stop=True).then_inc(sem("gx_mm5"), 1)
                pe.wait_ge(sem("hn_ready5"), g + 1)
                for j in range(GB):
                    ins = mm(B[1][0:SLOTS, j * P:(j + 1) * P], hn5[:, j * SLOTS:(j + 1) * SLOTS], wvo[:],
                             start=True, stop=True)
                ins.then_inc(sem("sv_mm5"), 1)
                pe.wait_ge(sem("at_ready5"), g + 1)
                pe.wait_ge(sem("sv_ready5"), g + 1)
                pe.wait_ge(sem("ysb_ready"), s)
                for j in range(GB):
                    t = slice(j * P, (j + 1) * P)
                    ins = mm(Y[:, t], sv5[:, t], at5[:, t], start=True, stop=True)
                ins.then_inc(sem("y_ready"), 1)

        def p5_act(act):
            p = 5
            for g, _, _, h in stages(act, p):
                s = NG * p + g
                act.wait_ge(sem("h_mm5"), g + 1)
                nc.scalar.activation(h5[0:SLOT_HID, :], B[0][0:SLOT_HID, :], ACT.Gelu, bias=b1x[:])\
                    .then_inc(sem("h_ready5"), 1)
                act.wait_ge(sem("shift_ready5"), g + 1)
                nc.scalar.activation(e5[:], e5[:], ACT.Exp, scale=rtau[:]).then_inc(sem("exp_ready5"), 1)
                norm_act(act, s + 1, 1 - h)
                act.wait_ge(sem("at_mm5"), g + 1)
                nc.scalar.copy(at5[:], B[0][0:SLOTS, :]).then_inc(sem("at_ready5"), 1)
                act.wait_ge(sem("rzx_ready5"), g + 1)
                nc.scalar.activation(rz5[:], rz5[:], ACT.Sigmoid).then_inc(sem("rz_ready5"), 1)
                act.wait_ge(sem("nx_ready5"), g + 1)
                nc.scalar.activation(n5[:], t5[:], ACT.Tanh, bias=S("bih", 2, 3)).then_inc(sem("n_ready5"), 1)
                act.wait_ge(sem("sv_mm5"), g + 1)
                nc.scalar.copy(sv5[:], B[1][0:SLOTS, :]).then_inc(sem("sv_ready5"), 1)
                result_act(act, p, s)

        def p5_dve(dve, st):
            p, v = 5, nc.vector

            def bs(a):
                return a.unsqueeze(1).to_broadcast([P, GB, SLOTS])

            def js(a):
                return a.rearrange("p (j s) -> p j s", j=GB)

            for g, before, after, h in stages(dve, p, st):
                s = NG * p + g
                finish_dve(dve, before, s)
                dve.wait_ge(sem("logit_mm5"), g + 1)
                st.add(v.tensor_copy(lg5[:], js(B[1][:, 0:NS])))
                st.settle()
                for j in range(GB):
                    st.add(v.max(out=m85[:, j, :], in_=lg5[:, j, :]))
                st.settle()
                v.tensor_tensor(e5[:], lg5[:], m85[:, :, 0:1].to_broadcast([P, GB, SLOTS]), ALU.subtract)\
                    .then_inc(sem("shift_ready5"), 1)
                for j in range(GB):
                    st.add(v.match_replace(out=wk5[:, j, :], in_to_replace=m85[:, j, :], in_values=lg5[:, j, :],
                                           imm_value=TAKEN))
                st.settle()
                st.add(v.tensor_scalar(wk5[:], wk5[:], TAKEN, None, ALU.is_equal))
                st.settle()
                dve.wait_ge(sem("exp_ready5"), g + 1)
                st.add(v.tensor_tensor(al5[:], e5[:], wk5[:], ALU.mult))
                st.settle()
                st.add(v.tensor_reduce(tot5[:], al5[:], AX.X, ALU.add))
                st.settle()
                st.add(v.reciprocal(rec5[:], tot5[:]))
                st.settle()
                v.tensor_tensor(al5[:], al5[:], rec5[:].unsqueeze(2).to_broadcast([P, GB, SLOTS]), ALU.mult)\
                    .then_inc(sem("al_ready5"), 1)
                norm(dve, st, after, (s + 1, 1 - h))
                dve.wait_ge(sem("in_mm5"), g + 1)
                st.add(v.tensor_scalar(ws5[:], B[3][:, 0:NS], 1e-8, None, ALU.add))
                st.settle()
                st.add(v.reciprocal(ws5[:], ws5[:]))
                st.settle()
                v.tensor_tensor(gi5[:], B[2][:, 0:NS], ws5[:], ALU.mult).then_inc(sem("gi_ready5"), 1)
                dve.wait_ge(sem("gx_mm5"), g + 1)
                for c in range(2):
                    ins = v.tensor_tensor(js(rz5[:, c, :]), js(B[4][:, c * NS:(c + 1) * NS]), bs(gh_rz[:, c, :]), ALU.add)
                ins.then_inc(sem("rzx_ready5"), 1)
                dve.wait_ge(sem("rz_ready5"), g + 1)
                st.add(v.tensor_tensor(js(t5[:]), js(rz5[:, 0, :]), bs(gh_n[:]), ALU.mult))
                st.settle()
                v.tensor_tensor(t5[:], t5[:], B[5][:, 0:NS], ALU.add).then_inc(sem("nx_ready5"), 1)
                dve.wait_ge(sem("n_ready5"), g + 1)
                st.add(v.tensor_tensor(js(hn5[:]), bs(hs_t[:]), js(n5[:]), ALU.subtract))
                st.settle()
                st.add(v.tensor_tensor(hn5[:], hn5[:], rz5[:, 1, :], ALU.mult))
                st.settle()
                v.tensor_tensor(hn5[:], hn5[:], n5[:], ALU.add).then_inc(sem("hn_ready5"), 1)

        block = ctx.enter_context(nc.Block())

        @block.sync
        def _(sp):
            for g in range(NG):
                c = slice(g * TG, (g + 1) * TG)
                sp.dma_start(X[:, c], x_d[:, c]).then_inc(sem(f"x_loaded{g}"), 16)
                if g == 0:
                    sp.dma_start(const[:], const_d).then_inc(sem("const_loaded"), 16)
                sp.dma_start(CT[:, c], ctx_d[:, c]).then_inc(sem(f"ctx_loaded{g}"), 16)
            sp.dma_start(mask_i[:], mask_d).then_inc(sem("small_loaded"), 16)
            for p in MOE:
                if phases <= SPLIT_IN[p]:
                    continue
                if p > 1:
                    sp.wait_ge(sem("y_ready"), NG * SPLIT_IN[p])
                n = MOE[p]["NC"] * P // NG
                for g in range(NG):
                    for k in range(3):
                        sp.dma_start(w_raw[k][:, g * n:(g + 1) * n], moe_d[p][k][:, g * n:(g + 1) * n])\
                            .then_inc(sem(f"raw{p}"), 16)
                    sp.wait_ge(sem(f"raw{p}"), 48 * (g + 1))
            for g in range(NG):
                sp.wait_ge(sem("x_updated"), last - NG + 1 + g)
                c = slice(g * TG, (g + 1) * TG)
                sp.dma_start(out_d[:, c], X[:, c]).then_inc(sem("stored"), 16)
            sp.wait_ge(sem("stored"), 16 * NG)
            if phases < PHASES:
                sp.wait_ge(sem("constb_loaded"), 16)

        @block.gpsimd
        def _(pool):
            gp = nc.gpsimd
            gp.memset(minus_half[:], -0.5).then_inc(sem("rstd_ready"), 1)
            pool.wait_ge(sem("rstd_ready"), 1)

            def power(s):
                pool.wait_ge(sem("var_ready"), s + 1)
                gp.tensor_tensor(rstd[:], var[:], minus_half[:], ALU.pow).then_inc(sem("rstd_ready"), 1)

            power(0)
            for g in range(NG):
                power(g + 1)
                weights_lo(pool, 1, g)
            for c in range(NG):
                pool.wait_ge(sem(f"ctx_loaded{c}"), 16)
            gp.tensor_copy(cg[0][:], CT[:, 0:TG]).then_inc(sem("cg_ready"), 1)
            for p in range(1, phases):
                for g, _, after, h in stages(pool, p):
                    s = NG * p + g
                    power(s + 1)
                    if p in (2, 4, 6):
                        pool.wait_ge(sem("y_ready"), s)
                        gp.tensor_copy(cg[1 - h][:], CT[:, bass.ds(after * TG, TG)]).then_inc(sem("cg_ready"), 1)
                    if p in MOE:
                        moe_pool(pool, p, g)
                    if p in (2, 4):
                        weights_lo(pool, {2: 3, 4: 7}[p], g)

        @block.scalar
        def _(act):
            act.dma_start(small[:], small_d).then_inc(sem("gates_loaded"), 16)
            act.dma_start(constb[:], constb_d).then_inc(sem("constb_loaded"), 16)
            act.wait_ge(sem("gates_loaded"), 16)
            nc.scalar.activation(tgate[:], S("gates"), ACT.Tanh).then_inc(sem("tgate_ready"), 1)
            act.wait_ge(sem("tgate_ready"), 1)
            act.wait_ge(sem("bias0_ready"), 1)
            norm_act(act, 0, 0)
            p0_act(act)
            act.wait_ge(sem("setup_done"), 1)
            for p in range(1, phases):
                if p in MOE:
                    moe_act(act, p)
                elif p == 2:
                    p2_act(act)
                elif p == 5:
                    p5_act(act)
                else:
                    heads_act(act, p)

        @block.tensor
        def _(pe):
            pe.wait_ge(sem("const_loaded"), 16)
            norm_pe(pe, 0, 0)
            p0_pe(pe)
            pe.wait_ge(sem("gates_loaded"), 16)
            setup_pe(pe)
            pe.wait_ge(sem("setup_done"), 1)
            for p in range(1, phases):
                if p in MOE:
                    moe_pe(pe, p)
                elif p == 2:
                    p2_pe(pe)
                elif p == 5:
                    p5_pe(pe)
                else:
                    heads_pe(pe, p)
            finish_pe(pe, last)

        @block.vector
        def _(dve):
            st = Steps(dve, sem("dve_steps"))
            nc.vector.memset(ybias[:], 0.0).then_inc(sem("bias0_ready"), 1)
            st.add(nc.vector.memset(ones5[:], 1.0))
            st.add(nc.vector.memset(h5[:], 1.0))
            st.add(nc.vector.memset(vh[:], 0.0))
            st.add(nc.vector.memset(vc[:], 0.0))
            st.settle()
            st.add(nc.vector.memset(vh[:, :, DK], 1.0))
            for k in range(2):
                st.add(nc.vector.memset(vc[k * HALF:(k + 1) * HALF, :, k * VW + DK], 1.0))
            route_setup(st)
            dve.wait_ge(sem("const_loaded"), 16)
            dve.wait_ge(sem("x_loaded0"), 16)
            norm(dve, st, 0, (0, 0))
            p0_dve(dve, st)
            dve.wait_ge(sem("tgate_ready"), 1)
            dve.wait_ge(sem("gates_loaded"), 16)
            setup_dve(dve, st)
            for p in range(1, phases):
                dve.wait_ge(sem("y_ready"), NG * p)
                if p in MOE:
                    moe_dve(dve, st, p)
                elif p == 2:
                    p2_dve(dve, st)
                elif p == 5:
                    p5_dve(dve, st)
                else:
                    heads_dve(dve, st, p)
            finish_dve(dve, NG - 1, last)


def packed(table, at, n, arrays):
    out = np.zeros((P, n), np.float32)
    for name, (rows, start, cols) in at.items():
        out[0:rows, start:start + cols] = arrays[name]
    return out


def head_tiles(w):
    lead = w.shape[:-1]
    out = np.zeros(lead + (HEAD_TILES, HEADS // HEAD_TILES, 32), w.dtype)
    src = w.reshape(lead + (HEADS // HEAD_TILES, HEAD_TILES, DK))
    for i in range(HEAD_TILES):
        out[..., i, :, 0:DK] = src[..., :, i, :]
    return out.reshape(lead + (HEAD_TILES * P,))


def constants():
    up = np.zeros((HALF, P), np.float32)
    for t in range(P):
        at = max((t + 0.5) * 0.5 - 0.5, 0.0)
        i0 = int(at)
        up[i0, t] += 1.0 - (at - i0)
        up[min(i0 + 1, HALF - 1), t] += at - i0
    up2 = np.zeros((2, HALF, 2, P), np.float32)
    up2[0, :, 0], up2[1, :, 1] = up, up
    rowmask = np.zeros((4, 32, 2), np.float32)
    rowmask[0::2, :, 0] = rowmask[1::2, :, 1] = 1.0
    return dict(ident=np.eye(P, dtype=np.float32), causal=np.triu(np.ones((P, P), np.float32)),
                up=up2.reshape(P, 2 * P), rowmask=rowmask.reshape(P, 2))


def selectors(dtype):
    out = np.zeros((P, SEL_N), np.float32)
    out[:, 0:P] = np.eye(P)
    for p, m in MOE.items():
        f = np.arange(m["NR"] * P)
        for part in range(3):
            out[part * m["E"] + f // m["F"], SEL_AT[p] + f] = 1.0
    return out.astype(dtype)


def layout(**inputs):
    A = {k: np.asarray(v) for k, v in inputs.items()}

    def col(a):
        return a.reshape(-1, 1)

    def per_partition(a):
        return np.broadcast_to(a.reshape(1, -1), (P, a.size))

    x2, f2, x4 = "L1_xattn_", "L2_ffn_", "L2_xattn_"
    x6 = "L3_xattn_"
    small = dict(
        gates=per_partition(np.stack([A["g_xattn"], A["g_ffn"]], 1)),
        Wr1=A["L0_ffn_Wr"], Wr3=A["L1_ffn_router_w"].T, Wr7=A["L3_ffn_gate_w"].T,
        rb3=per_partition(A["L1_ffn_bias"]), rb7=per_partition(A["L3_ffn_gate_bias"]),
        hW=A[x2 + "hW"], qWT=A[x2 + "qW"].T, cW=A[x2 + "cW"], kWT=A[x2 + "kW"].T, vWT=A[x2 + "vW"].T,
        oWT=A[x2 + "oW"].T, **{b: col(A[x2 + b]) for b in ("hb", "qb", "cb", "kb", "vb", "ob")},
        Wq4=head_tiles(A[x4 + "Wq"].T), Wk4=head_tiles(A[x4 + "Wk"].T), Wv4=A[x4 + "Wv"].T, Wo4=A[x4 + "Wo"].T,
        Wq6=head_tiles(A[x6 + "w_q"]), Wk6=head_tiles(A[x6 + "w_k"]), Wv6=A[x6 + "w_v"], Wo6=A[x6 + "w_o"],
        bq4=head_tiles(A[x4 + "bq"]).reshape(HEAD_TILES, P).T, bk4=head_tiles(A[x4 + "bk"]).reshape(HEAD_TILES, P).T,
        bq6=head_tiles(A[x6 + "b_q"]).reshape(HEAD_TILES, P).T, bk6=head_tiles(A[x6 + "b_k"]).reshape(HEAD_TILES, P).T,
        bv4=col(A[x4 + "bv"]), bo4=col(A[x4 + "bo"]), bv6=col(A[x6 + "b_v"]), bo6=col(A[x6 + "b_o"]),
        slot_init=A[f2 + "slot_init"], slot_scale=A[f2 + "slot_scale"],
        w1x=A[f2 + "w1"][:, 0:P].T, w1m=A[f2 + "w1"][:, P:].T, b1=col(A[f2 + "b1"]),
        w2=np.concatenate([A[f2 + "w2"].T, A[f2 + "b2"][None]], 0),
        wih=A[f2 + "gru_wih"].T, whh=A[f2 + "gru_whh"].T,
        bih=A[f2 + "gru_bih"].reshape(3, P).T, bhh=A[f2 + "gru_bhh"].reshape(3, P).T,
        wv=A[f2 + "wv"], woT=A[f2 + "wo"].T, bv5=col(A[f2 + "bv"]), bo5=col(A[f2 + "bo"]),
        tau=per_partition(A[f2 + "tau"]),
    )

    def wide(w):
        return w.transpose(1, 0, 2).reshape(P, -1)

    def chunks(w):
        return w.reshape(-1, P, P).transpose(1, 0, 2).reshape(P, -1)

    l1, l3 = "L1_ffn_", "L3_ffn_"
    moe = {
        1: [wide(A["L0_ffn_Wg"]), wide(A["L0_ffn_Wu"]), chunks(A["L0_ffn_Wd"].reshape(-1, P))],
        3: [np.concatenate([wide(A[l1 + "gate_w"]), A[l1 + "sh_gate_w"]], 1),
            np.concatenate([wide(A[l1 + "up_w"]), A[l1 + "sh_up_w"]], 1),
            np.concatenate([chunks(A[l1 + "down_w"].reshape(-1, P)), chunks(A[l1 + "sh_down_w"])], 1)],
        7: [np.concatenate([A[l3 + "w_gate"].reshape(-1, P).T, A[l3 + "sh_gate"].T], 1),
            np.concatenate([A[l3 + "w_up"].reshape(-1, P).T, A[l3 + "sh_up"].T], 1),
            np.concatenate([chunks(A[l3 + "w_down"].transpose(0, 2, 1).reshape(-1, P)), chunks(A[l3 + "sh_down"].T)], 1)],
    }
    arrays = dict(
        in_small=packed(SMALL, SMALL_AT, SMALL_N, small),
        in_const=packed(CONST, CONST_AT, CONST_N, constants()),
        in_constb=selectors(mybir.dt.np(BF16)),
        in_x=A["x"].transpose(1, 0, 2).reshape(P, NB * P),
        in_ctx_t=A["ctx_1024"].transpose(2, 0, 1).reshape(P, NB * P),
        in_mask=A["mask_1x1xSxS2_ik0"].reshape(P, P),
        **{f"in_moe{p}_{k}": w for p, ws in moe.items() for k, w in enumerate(ws)},
    )
    return {name: np.ascontiguousarray(a) for name, a in arrays.items()}


def describe(nc, arrays, phases=PHASES):
    d = {name: nc.dram_tensor(name, a.shape, mybir.dt.from_np(a.dtype), kind="ExternalInput").ap()
         for name, a in arrays.items()}
    out = nc.dram_tensor("out", (P, NB * P), F32, kind="ExternalOutput").ap()
    build(nc, d["in_small"], d["in_const"], d["in_constb"], d["in_x"], d["in_ctx_t"], d["in_mask"],
          {p: [d[f"in_moe{p}_{k}"] for k in range(3)] for p in MOE}, out, phases=phases)


def kernel(**inputs):
    import concourse.bacc as bacc
    from concourse.bass_utils import run_bass_kernel_spmd as run
    arrays = layout(**inputs)
    nc = bacc.Bacc("TRN2", target_bir_lowering=False, num_devices=1)
    describe(nc, arrays)
    out = run(nc, [arrays], core_ids=[0]).results[0]["out"]
    return np.ascontiguousarray(out.reshape(P, NB, P).transpose(1, 0, 2))
```

```python
from contextlib import ExitStack

import numpy as np

import concourse.bass as bass
from concourse import mybir

F32 = mybir.dt.float32
BF16 = mybir.dt.bfloat16
I32 = mybir.dt.int32
F32R = mybir.dt.float32r
ALU = mybir.AluOpType
ACT = mybir.ActivationFunctionType
AX = mybir.AxisListType

P = 128
NB = 16
GB = 4
NG = NB // GB
TG = GB * P
PHASES = 8
LN_EPS = 1e-5
LOWEST = -3.0e38
TAKEN = 3.0e38
MASKED = -1.0e30

HEADS, DK = 16, 8
HEAD_TILES = 4
VW = 32
HALF = P // 2

SLOTS = 64
SLOT_HID = 64
SLOT_TOP = 8

MOE = {
    1: dict(E=8, F=256, SH=0, K=2, GK=0),
    3: dict(E=16, F=128, SH=256, K=4, GK=2),
    7: dict(E=32, F=64, SH=128, K=8, GK=4),
}
for _m in MOE.values():
    _m["NR"] = _m["E"] * _m["F"] // P
    _m["NC"] = _m["NR"] + _m["SH"] // P
    _m["EG"] = 4
SCALE_ROUTED = 2.5
TURN = 8
DOWN = TURN + 4
RING = DOWN + 2
HI_RING = 5
SPLIT_IN = {1: 0, 3: 2, 7: 5}

SMALL = dict(
    gates=(P, PHASES),
    hW=(P, P), qWT=(P, P), cW=(P, P), kWT=(P, P), vWT=(P, P), oWT=(P, P),
    hb=(P, 1), qb=(P, 1), cb=(P, 1), kb=(P, 1), vb=(P, 1), ob=(P, 1),
    Wr1=(P, 8), Wr3=(P, 16), Wr7=(P, 32), rb3=(P, 16), rb7=(P, 32),
    Wq4=(P, HEAD_TILES * P), Wk4=(P, HEAD_TILES * P), Wv4=(P, P), Wo4=(P, P),
    bq4=(P, HEAD_TILES), bk4=(P, HEAD_TILES), bv4=(P, 1), bo4=(P, 1),
    Wq6=(P, HEAD_TILES * P), Wk6=(P, HEAD_TILES * P), Wv6=(P, P), Wo6=(P, P),
    bq6=(P, HEAD_TILES), bk6=(P, HEAD_TILES), bv6=(P, 1), bo6=(P, 1),
    slot_init=(SLOTS, P), slot_scale=(SLOTS, 1), w1x=(P, SLOT_HID), w1m=(P, SLOT_HID),
    b1=(SLOT_HID, 1), w2=(SLOT_HID + 1, SLOTS), wih=(P, 3 * P), whh=(P, 3 * P),
    bih=(P, 3), bhh=(P, 3), wv=(P, P), woT=(P, P), bv5=(P, 1), bo5=(P, 1), tau=(P, 1),
)
CONST = dict(ident=(P, P), causal=(P, P), up=(P, 2 * P), rowmask=(P, HEAD_TILES), low=(P, 2), sign=(P, 2))


def columns(table):
    at, n = {}, 0
    for name, (rows, cols) in table.items():
        at[name] = (rows, n, cols)
        n += cols
    return at, n


SMALL_AT, SMALL_N = columns(SMALL)
CONST_AT, CONST_N = columns(CONST)
SEL_AT, SEL_N = {}, P
for _p, _m in MOE.items():
    SEL_AT[_p] = SEL_N
    SEL_N += _m["NR"] * P


class Steps:

    def __init__(self, eng, sem):
        self.eng, self.sem, self.n = eng, sem, 0

    def add(self, instruction):
        instruction.then_inc(self.sem, 1)
        self.n += 1
        return self.n

    def settle(self, n=None):
        self.eng.wait_ge(self.sem, self.n if n is None else n)

    def restart(self):
        if self.n:
            self.settle()
        self.eng.sem_clear(self.sem)
        self.n = 0


def build(nc, small_d, const_d, constb_d, x_d, ctx_d, mask_d, moe_d, out_d, phases=PHASES):
    last = NG * phases
    with ExitStack() as ctx:
        def sb(name, shape, dt=F32):
            return ctx.enter_context(nc.sbuf_tensor(name, shape, dt))

        def two_views(name, shape):
            with nc.sbuf_tensor(name, shape, F32) as full:
                pass
            return full, sb(name + "_r", shape, F32R)

        sems = {}

        def sem(name):
            if name not in sems:
                sems[name] = ctx.enter_context(nc.semaphore(name))
            return sems[name]

        T = ctx.enter_context(nc.psum_tensor("T", [P, TG], F32))
        Y = ctx.enter_context(nc.psum_tensor("Y", [P, TG], F32))
        B = [ctx.enter_context(nc.psum_tensor(f"B{i}", [P, TG], F32)) for i in range(6)]

        X = sb("X", [P, NB * P])
        CT = sb("CT", [P, NB * P])
        small = sb("small", [P, SMALL_N])
        const = sb("const", [P, CONST_N])
        constb = sb("constb", [P, SEL_N], BF16)
        mask_i = sb("mask_i", [P, P], I32)
        WCOLS = max(m["NC"] for m in MOE.values()) * P
        w_hi = [sb(f"{n}_hi", [P, WCOLS], F32R) for n in ("gate", "up", "down")]
        w_raw, w_lo = zip(*[two_views(f"{n}_lo", [P, WCOLS]) for n in ("gate", "up", "down")])

        def S(name, a=0, b=None):
            rows, at, cols = SMALL_AT[name]
            return small[0:rows, at + a:at + (cols if b is None else b)]

        def K(name):
            rows, at, cols = CONST_AT[name]
            return const[0:rows, at:at + cols]

        ident = K("ident")
        identb = constb[:, 0:P]

        xhat = [sb(f"xhat{i}", [P, TG]) for i in range(2)]
        xhat_t = [sb(f"xhat_t{i}", [P, TG]) for i in range(2)]
        cg = [sb(f"cg{i}", [P, TG]) for i in range(2)]
        ysb = sb("ysb", [P, TG])
        tgate = sb("tgate", [P, PHASES])
        ybias = sb("ybias", [P, PHASES])

        stats = sb("stats", [P, GB, 6])
        mv = sb("mv", [P, GB, 2])
        var = sb("var", [P, GB])
        rstd = sb("rstd", [P, GB])
        minus_half = sb("minus_half", [P, GB])
        spare = sb("spare", [P, 2])

        shared, shared_r = two_views("shared", [P, 29 * TG])

        class Area:
            def __init__(self):
                self.at = 0

            def tile(self, shape, of=shared):
                n = int(np.prod(shape[1:]))
                a = of[0:shape[0], self.at:self.at + n]
                self.at += n
                assert self.at <= 29 * TG
                if len(shape) == 3:
                    a = a.rearrange("p (a b) -> p a b", a=shape[1])
                elif len(shape) == 4:
                    a = a.rearrange("p (a b c) -> p a b c", a=shape[1], b=shape[2])
                return a

        def token_tile(g, j):
            return X[:, bass.ds(g * TG + j * P, P)]

        def norm(dve, st, g, s):
            norm_stats(st, g)
            norm_apply(dve, g, *s)

        def norm_stats(st, g):
            for j in range(GB):
                st.add(nc.vector.bn_stats(out=stats[:, j, :], in_=token_tile(g, j)))
            st.settle()
            for j in range(GB):
                st.add(nc.vector.bn_aggr(out=mv[:, j, :], in_=stats[:, j, :]))
            st.settle()
            nc.vector.tensor_scalar(var[:], mv[:, :, 1], LN_EPS, None, ALU.add).then_inc(sem("var_ready"), 1)

        def norm_apply(dve, g, s, h):
            dve.wait_ge(sem("rstd_ready"), s + 2)
            for j in range(GB):
                ins = nc.vector.tensor_scalar(xhat[h][:, j * P:(j + 1) * P], token_tile(g, j),
                                              mv[:, j, 0:1], rstd[:, j:j + 1], ALU.subtract, ALU.mult)
            ins.then_inc(sem("xhat_ready"), 1)

        def finish_dve(dve, g, s):
            dve.wait_ge(sem("yt_ready"), s)
            nc.vector.tensor_tensor(X[:, bass.ds(g * TG, TG)], X[:, bass.ds(g * TG, TG)], T[:],
                                    ALU.add).then_inc(sem("x_updated"), 1)
            dve.wait_ge(sem("x_updated"), s)

        def finish_pe(pe, s):
            pe.wait_ge(sem("xhat_t_ready"), s + 1)
            pe.wait_ge(sem("ysb_ready"), s)
            for j in range(GB):
                ins = nc.tensor.transpose(T[:, j * P:(j + 1) * P], ysb[:, j * P:(j + 1) * P], ident)
            ins.then_inc(sem("yt_ready"), 1)

        def norm_pe(pe, s, h):
            pe.wait_ge(sem("xhat_ready"), s + 1)
            if not isinstance(s, int) or s > 1:
                pe.wait_ge(sem("x_updated"), s - 1)
            elif s == 1:
                pe.wait_ge(sem("xhat_t_ready"), s)
            for j in range(GB):
                ins = nc.tensor.transpose(T[:, j * P:(j + 1) * P], xhat[h][:, j * P:(j + 1) * P], ident)
            ins.then_inc(sem("xt_ready"), 1)

        def norm_act(act, s, h):
            act.wait_ge(sem("xt_ready"), s + 1)
            nc.scalar.copy(xhat_t[h][:], T[:]).then_inc(sem("xhat_t_ready"), 1)

        def result_act(act, p, s):
            act.wait_ge(sem("y_ready"), s + 1)
            if not isinstance(s, int) or s > 0:
                act.wait_ge(sem("yt_ready"), s)
            nc.scalar.activation(ysb[:], Y[:], ACT.Identity, bias=ybias[:, p:p + 1],
                                 scale=tgate[:, p:p + 1]).then_inc(sem("ysb_ready"), 1)

        def weights_hi(act, p, g, which=(0, 1, 2)):
            n = MOE[p]["NC"] * P // NG
            act.wait_ge(sem(f"raw{p}"), 48 * (g + 1))
            for k in which:
                nc.scalar.copy(w_hi[k][:, bass.ds(g * n, n)], w_raw[k][:, bass.ds(g * n, n)])\
                    .then_inc(sem(f"w_hi{p}"), 1)

        def weights_lo(pool, p, g, h):
            n = MOE[p]["NC"] * P // NG
            if p == 7:
                pool.wait_ge(sem(f"raw{p}"), 48 * (g + 1))
                for k in range(3):
                    c = bass.ds(g * n, n)
                    nc.gpsimd.tensor_copy(w_hi[k][:, c], w_raw[k][:, c]).then_inc(sem(f"w_hi{p}"), 1)
            pool.wait_ge(sem(f"w_hi{p}"), 3 * g + 3)
            if p > 1:
                nc.gpsimd.tensor_tensor(spare[:, h:h + 1], minus_half[:, 0:1], minus_half[:, 0:1], ALU.add)
            for k in range(3):
                c = bass.ds(g * n, n)
                ins = nc.gpsimd.tensor_tensor(w_lo[k][:, c], w_raw[k][:, c], w_hi[k][:, c].bitcast(F32),
                                              ALU.subtract)
            ins.then_inc(sem(f"w_lo{p}"), 1)

        def stages(eng, p, st=None):
            if st:
                st.restart()
            with eng.Fori(0, NG // 2) as r:
                for g, before, after, h in ((2 * r, r * -2 + 3, 2 * r + 1, 0), (2 * r + 1, 2 * r, r * -2 + 2, 1)):
                    yield g, before, after, h
                    if st:
                        st.restart()

        def pairs(eng, p, st=None):
            if st:
                st.restart()
            with eng.Fori(0, NG // 2) as r:
                yield 2 * r, 2 * r + 1, r * -2 + 2
                if st:
                    st.restart()

        area0 = Area()
        sm = [area0.tile([P, TG]) for i in range(2)]

        def p0_pe(pe):
            for g in range(NG):
                h = g % 2
                pe.wait_ge(sem(f"ctx_loaded{g}"), 16)
                if g >= 2:
                    pe.wait_ge(sem("p0_masked"), g - 1)
                for j in range(GB):
                    kt = CT[:, g * TG + j * P:g * TG + (j + 1) * P]
                    ins = nc.tensor.matmul(B[h][:, j * P:(j + 1) * P], kt, kt, start=True, stop=True)
                ins.then_inc(sem("p0_scores"), 1)
                if g > 0:
                    finish_pe(pe, g)
                pe.wait_ge(sem("p0_masked"), g + 1)
                pe.wait_ge(sem("xhat_ready"), g + 1)
                if g > 0:
                    pe.wait_ge(sem("ysb_ready"), g)
                for j in range(GB):
                    o, q = Y[:, j * P:(j + 1) * P], xhat[h][:, j * P:(j + 1) * P]
                    nc.tensor.matmul(o, q, sm[h][:, j * P:(j + 1) * P], start=True, stop=False)
                    ins = nc.tensor.matmul(o, q, ident, start=False, stop=True)
                ins.then_inc(sem("y_ready"), 1)
                norm_pe(pe, g + 1, 1 - h)

        def p0_dve(dve, st):
            for g in range(NG):
                h = g % 2
                st.restart()
                dve.wait_ge(sem("p0_scores"), g + 1)
                if g >= 2:
                    dve.wait_ge(sem("y_ready"), g - 1)
                nc.vector.tensor_tensor(
                    sm[h][:].rearrange("p (j t) -> p j t", j=GB),
                    B[h][:].rearrange("p (j t) -> p j t", j=GB),
                    K("causal").unsqueeze(1).to_broadcast([P, GB, P]), ALU.mult).then_inc(sem("p0_masked"), 1)
                if g > 0:
                    finish_dve(dve, g - 1, g)
                if g + 1 < NG:
                    dve.wait_ge(sem(f"x_loaded{g + 1}"), 16)
                norm(dve, st, (g + 1) % NG, (g + 1, 1 - h))

        def p0_act(act):
            for g in range(NG):
                result_act(act, 0, g)
                norm_act(act, g + 1, (g + 1) % 2)
                weights_hi(act, 1, g)

        wqh = sb("wqh", [P, P])
        wkc = sb("wkc", [P, P])
        wvc = sb("wvc", [P, P])
        wvo = sb("wvo", [P, P])
        bcols = sb("bcols", [P, 16])
        slots = sb("slots", [SLOTS, P])
        mean_w = sb("mean_w", [SLOTS, 1])
        hs_t = sb("hs_t", [P, SLOTS])
        mean_t = sb("mean_t", [P, 1])
        b1x = sb("b1x", [SLOT_HID, 1])
        gh_rz = sb("gh_rz", [P, 2, SLOTS])
        gh_n = sb("gh_n", [P, SLOTS])
        brz = sb("brz", [P, 2])
        rtau = sb("rtau", [P, 1])
        maskb = sb("maskb", [P, GB, P], BF16)
        mtmp = sb("mtmp", [P, P])

        def setup_pe(pe):
            pe.wait_ge(sem("small_loaded"), 16)
            mm = nc.tensor.matmul
            mm(B[2][:, 0:P], S("hW"), S("qWT"), start=True, stop=True)
            mm(B[2][:, P:2 * P], S("cW"), S("kWT"), start=True, stop=True)
            mm(B[2][:, 2 * P:3 * P], S("cW"), S("vWT"), start=True, stop=True)
            mm(B[2][:, 3 * P:4 * P], S("wv"), S("woT"), start=True, stop=True)
            mm(B[3][:, 0:1], S("qWT"), S("hb"), start=True, stop=True)
            mm(B[3][:, 1:2], S("kWT"), S("cb"), start=True, stop=True)
            mm(B[3][:, 2:3], S("vWT"), S("cb"), start=True, stop=True)
            mm(B[3][:, 3:4], S("Wo4"), S("bv4"), start=True, stop=True)
            mm(B[3][:, 4:5], S("woT"), S("bv5"), start=True, stop=True)
            mm(B[3][:, 5:6], S("Wo6"), S("bv6"), start=True, stop=True).then_inc(sem("setup_mm"), 1)
            pe.wait_ge(sem("setup_slots"), 1)
            nc.tensor.transpose(B[4][:, 0:SLOTS], slots[:], ident[0:SLOTS, 0:SLOTS])
            mm(B[4][:, SLOTS:SLOTS + 1], slots[:], mean_w[:], start=True, stop=True).then_inc(sem("setup_mm"), 1)
            pe.wait_ge(sem("setup_slots"), 2)
            mm(B[5][0:SLOT_HID, 0:1], S("w1m"), mean_t[:], start=True, stop=True)
            for c in range(3):
                mm(B[5][:, SLOTS * (c + 1):SLOTS * (c + 2)], S("whh", c * P, (c + 1) * P), hs_t[:],
                   start=True, stop=True)
            pe.wait_ge(sem("setup_slots"), 3)
            mm(B[4][:, P:P + 1], S("oWT"), bcols[:, 2:3], start=True, stop=True).then_inc(sem("setup_mm"), 1)

        def setup_dve(dve, st):
            st.restart()
            v = nc.vector
            dve.wait_ge(sem("small_loaded"), 16)
            st.add(v.memset(mean_w[:], 1.0 / SLOTS))
            v.tensor_scalar(slots[:], S("slot_init"), S("slot_scale"), None, ALU.mult).then_inc(sem("setup_slots"), 1)
            dve.wait_ge(sem("setup_mm"), 1)
            for k, w in enumerate((wqh, wkc, wvc, wvo)):
                st.add(v.tensor_copy(w[:], B[2][:, k * P:(k + 1) * P]))
            for k, b in enumerate(("qb", "kb", "vb", "bo4", "bo5", "bo6")):
                st.add(v.tensor_tensor(bcols[:, k:k + 1], B[3][:, k:k + 1], S(b), ALU.add))
            st.add(v.tensor_tensor(brz[:], S("bih", 0, 2), S("bhh", 0, 2), ALU.add))
            st.add(v.tensor_scalar(rtau[:], S("tau"), -1.0, None, ALU.mult))
            st.settle()
            st.add(v.tensor_tensor(rtau[:], rtau[:], S("tau"), ALU.max))
            st.settle()
            st.add(v.tensor_scalar(rtau[:], rtau[:], 0.1, None, ALU.add))
            st.settle()
            st.add(v.reciprocal(rtau[:], rtau[:]))
            dve.wait_ge(sem("setup_mm"), 2)
            st.add(v.tensor_copy(hs_t[:], B[4][:, 0:SLOTS]))
            st.add(v.tensor_copy(mean_t[:], B[4][:, SLOTS:SLOTS + 1]))
            st.settle()
            v.engine_nop().then_inc(sem("setup_slots"), 2)
            dve.wait_ge(sem("setup_mm"), 3)
            st.add(v.tensor_tensor(b1x[:], B[5][0:SLOT_HID, 0:1], S("b1"), ALU.add))
            for c in range(2):
                st.add(v.tensor_scalar(gh_rz[:, c, :], B[5][:, SLOTS * (c + 1):SLOTS * (c + 2)],
                                       brz[:, c:c + 1], None, ALU.add))
            st.add(v.tensor_scalar(gh_n[:], B[5][:, 3 * SLOTS:4 * SLOTS], S("bhh", 2, 3), None, ALU.add))
            st.add(v.tensor_tensor(bcols[:, 6:7], B[4][:, P:P + 1], S("ob"), ALU.add))
            st.settle()
            for p, k in ((2, 6), (4, 3), (5, 4), (6, 5)):
                st.add(v.tensor_tensor(ybias[:, p:p + 1], bcols[:, k:k + 1], tgate[:, p:p + 1], ALU.mult))
            for p in (4, 6):
                for k in range(2):
                    st.add(v.tensor_scalar(b_low[p][:, k, :], S(f"b{'qk'[k]}{p}"), K("low")[:, k:k + 1], None, ALU.mult))
            st.add(v.tensor_scalar(mtmp[:], mask_i[:], 0, None, ALU.is_equal))
            st.settle()
            st.add(v.tensor_scalar(maskb[:], mtmp[:].unsqueeze(1).to_broadcast([P, GB, P]), MASKED, None, ALU.mult))
            st.settle()
            v.engine_nop().then_inc(sem("setup_done"), 1)

        area1 = Area()
        su_lo = [area1.tile([P, TG], shared_r) for i in range(RING)]
        area1.at = 0
        su = [area1.tile([P, TG]) for i in range(RING)]
        sg = [area1.tile([P, TG]) for i in range(2)]
        su_hi = [area1.tile([P, TG], shared_r) for i in range(HI_RING)]
        x_hi = area1.tile([P, TG], shared_r)
        x_lo = area1.tile([P, TG], shared_r)
        cw_t = sb("cw_t", [96, TG], BF16)
        parts = sb("parts", [P, GB, 96], BF16)
        route = {}
        for p, m in MOE.items():
            E, NGR = m["E"], m["E"] // m["EG"]
            t = dict(
                vals=sb(f"vals{p}", [P, GB, E + 8 - m["K"]]), rep=sb(f"rep{p}", [P, GB, 8]),
                work=sb(f"work{p}", [P, GB, E + 8 - m["K"]]), m8=sb(f"m8_{p}", [P, GB, 8]),
                msk=sb(f"msk{p}", [P, GB, E]), sig=sb(f"sig{p}", [P, GB, E]),
                w=sb(f"w{p}", [P, GB, E]), tot=sb(f"tot{p}", [P, GB]), rec=sb(f"rec{p}", [P, GB]),
                comb=sb(f"comb{p}", [P, GB, E]), r1=sb(f"r1_{p}", [P, GB, E]),
                parts=parts)
            t["part"] = t["parts"][:, :, 0:3 * E].rearrange("p j (a e) -> p j a e", a=3)
            if m["GK"]:
                t.update(
                    s=sb(f"s{p}", [P, GB * NGR, 4]), pair=sb(f"pair{p}", [P, GB * NGR, 6]),
                    gv=sb(f"gv{p}", [P, GB, NGR + 8 - m["GK"]]), grep=sb(f"grep{p}", [P, GB, 8]),
                    gwork=sb(f"gwork{p}", [P, GB, NGR + 8 - m["GK"]]), gm=sb(f"gm{p}", [P, GB, NGR]),
                    gz=sb(f"gz{p}", [P, GB, NGR]), ms=sb(f"ms{p}", [P, GB * NGR, 4]))
            route[p] = t

        def route_setup(st):
            st.add(nc.vector.memset(parts[:], 0.0))
            for p, m in MOE.items():
                t = route[p]
                st.add(nc.vector.memset(t["vals"][:], LOWEST))
                st.add(nc.vector.memset(t["rep"][:], LOWEST))
                if m["GK"]:
                    st.add(nc.vector.memset(t["gv"][:], LOWEST))
                    st.add(nc.vector.memset(t["grep"][:], LOWEST))
            st.settle()

        def top_k(st, vals, m8, rep, work, k):
            for j in range(GB):
                st.add(nc.vector.max(out=m8[:, j, :], in_=vals[:, j, :]))
            st.settle()
            if k < 8:
                st.add(nc.vector.tensor_copy(rep[:, :, 0:k], m8[:, :, 0:k]))
                st.settle()
            else:
                rep = m8
            yield
            for j in range(GB):
                st.add(nc.vector.match_replace(out=work[:, j, :], in_to_replace=rep[:, j, :],
                                               in_values=vals[:, j, :], imm_value=TAKEN))
            st.settle()

        def split(st, t):
            v, parts = nc.vector, t["part"]
            st.add(v.tensor_copy(parts[:, :, 0, :], t["comb"][:]))
            st.settle()
            st.add(v.tensor_tensor(t["r1"][:], t["comb"][:], parts[:, :, 0, :], ALU.subtract))
            st.settle()
            st.add(v.tensor_copy(parts[:, :, 1, :], t["r1"][:]))
            st.settle()
            v.tensor_tensor(parts[:, :, 2, :], t["r1"][:], parts[:, :, 1, :], ALU.subtract)\
                .then_inc(sem("weights_ready"), 1)

        def per_expert(a, E):
            return a.unsqueeze(2).to_broadcast([P, GB, E])

        def normed(dve, st, t, E, factor, eps):
            v = nc.vector
            st.add(v.tensor_reduce(t["tot"][:], t["w"][:], AX.X, ALU.add))
            st.settle()
            st.add(v.tensor_scalar(t["tot"][:], t["tot"][:], eps, None, ALU.add))
            st.settle()
            st.add(v.reciprocal(t["rec"][:], t["tot"][:]))
            st.settle()
            yield
            st.add(v.scalar_tensor_tensor(t["comb"][:], t["w"][:], factor, per_expert(t["rec"][:], E),
                                          ALU.mult, ALU.mult))
            st.settle()

        def logits_of(p):
            return T[:, 0:GB * MOE[p]["E"]].rearrange("p (j e) -> p j e", j=GB)

        def route_begin(dve, st, p, g):
            m, t, v = MOE[p], route[p], nc.vector
            E = m["E"]
            dve.wait_ge(sem(f"logits{p}"), g + 2)
            v.tensor_copy(t["vals"][:, :, 0:E], logits_of(p)).then_inc(sem(f"logits_read{p}"), 1)
            dve.wait_ge(sem(f"logits_read{p}"), g + 2)
            yield
            yield from top_k(st, t["vals"], t["m8"], t["rep"], t["work"], m["K"])
            v.tensor_tensor(t["r1"][:], t["vals"][:, :, 0:E], t["m8"][:, :, 0:1].to_broadcast([P, GB, E]),
                            ALU.subtract).then_inc(sem("shifted"), 1)
            st.add(v.tensor_scalar(t["msk"][:], t["work"][:, :, 0:E], TAKEN, None, ALU.is_equal))
            st.settle()

        def route_top2(dve, st, p, g):
            t, v = route[p], nc.vector
            E = MOE[p]["E"]
            dve.wait_ge(sem("exp_ready"), g + 1)
            st.add(v.tensor_tensor(t["w"][:], t["sig"][:], t["msk"][:], ALU.mult))
            st.settle()
            yield from normed(dve, st, t, E, 1.0, 0.0)
            yield
            split(st, t)

        def route_groups(dve, st, p, g):
            m, t, v = MOE[p], route[p], nc.vector
            E, NGR = m["E"], m["E"] // m["EG"]
            dve.wait_ge(sem(f"logits_read{p}"), g + 1)
            st.add(v.tensor_tensor(t["s"][:].rearrange("p (j n) e -> p j (n e)", j=GB), t["sig"][:],
                                   S(f"rb{p}").unsqueeze(1).to_broadcast([P, GB, E]), ALU.add))
            st.settle()
            at = 0
            for d in (1, 2, 3):
                st.add(v.tensor_tensor(t["pair"][:, :, at:at + 4 - d], t["s"][:, :, 0:4 - d],
                                       t["s"][:, :, d:4], ALU.add))
                at += 4 - d
            st.settle()
            st.add(v.tensor_reduce(t["gv"][:, :, 0:NGR], t["pair"][:].rearrange("p (j n) e -> p j n e", j=GB),
                                   AX.X, ALU.max))
            st.settle()
            yield
            yield from top_k(st, t["gv"], t["m8"], t["grep"], t["gwork"], m["GK"])
            st.add(v.tensor_scalar(t["gm"][:], t["gwork"][:, :, 0:NGR], TAKEN, None, ALU.is_equal))
            st.settle()
            yield
            fill = -1.0 if p == 3 else 0.0
            gm = t["gm"][:].rearrange("p j n -> p (j n)").unsqueeze(2).to_broadcast([P, GB * NGR, 4])
            st.add(v.tensor_tensor(t["ms"][:], t["s"][:], gm, ALU.mult))
            if fill:
                st.add(v.tensor_scalar(t["gz"][:], t["gm"][:], 1.0, -fill, ALU.subtract, ALU.mult))
            st.settle()
            vals = t["vals"][:, :, 0:E]
            if fill:
                gz = t["gz"][:].rearrange("p j n -> p (j n)").unsqueeze(2).to_broadcast([P, GB * NGR, 4])
                st.add(v.tensor_tensor(t["ms"][:], t["ms"][:], gz, ALU.add))
                st.settle()
            st.add(v.tensor_scalar(vals, t["ms"][:].rearrange("p (j n) e -> p j (n e)", j=GB), 0.0, None, ALU.add))
            st.settle()
            yield
            yield from top_k(st, t["vals"], t["m8"], t["rep"], t["work"], m["K"])
            st.add(v.tensor_scalar(t["msk"][:], t["work"][:, :, 0:E], TAKEN, None, ALU.is_equal))
            st.settle()
            st.add(v.tensor_tensor(t["w"][:], t["sig"][:], t["msk"][:], ALU.mult))
            st.settle()
            yield from normed(dve, st, t, E, SCALE_ROUTED, 1e-20)
            yield
            split(st, t)

        FINISH_AT, STATS_AT, NORM_AT, NORMED_AT = 9, 7, 12, 14
        MOE_NO = {1: 0, 3: 1, 7: 2}
        SCORES_AT = {p: m["NC"] + (4 if m["GK"] else 7) for p, m in MOE.items()}
        def by_pool(c):
            return c % 2 == 1

        def product(out, w, cols, hi, lo, start=True, stop=True):
            nc.tensor.matmul(out, w_hi[w][:, cols], lo, start=start, stop=False)
            nc.tensor.matmul(out, w_hi[w][:, cols], hi, start=False, stop=False)
            return nc.tensor.matmul(out, w_lo[w][:, cols], hi, start=False, stop=stop)

        def moe_pe(pe, p):
            m = MOE[p]
            NC, NR, E = m["NC"], m["NR"], m["E"]
            pe.wait_ge(sem(f"w_lo{p}"), NG)
            pe.wait_ge(sem("constb_loaded"), 16)

            def logits(s, h):
                pe.wait_ge(sem("xhat_t_ready"), s + 1)
                for j in range(GB):
                    ins = nc.tensor.matmul(logits_of(p)[:, j, :], xhat_t[h][:, j * P:(j + 1) * P], S(f"Wr{p}"),
                                           start=True, stop=True)
                ins.then_inc(sem(f"logits{p}"), 1)

            logits(NG * p, 0)
            for g, _, _, h in stages(pe, p):
                s = NG * p + g
                pe.wait_ge(sem("x_lo_ready"), (NG + 1) * MOE_NO[p] + g + 1)
                for i in range(NC + DOWN):
                    if i < NC:
                        if i >= 2:
                            pe.wait_ge(sem(f"su_ready{p}"), g * NC + i - 1)
                        w = slice(i * P, (i + 1) * P)
                        product(B[i % 2][:], 0, w, x_hi, x_lo).then_inc(sem(f"gate_mm{p}"), 1)
                        product(B[2 + i % 2][:], 1, w, x_hi, x_lo).then_inc(sem(f"up_mm{p}"), 1)
                    if i == TURN - 1:
                        pe.wait_ge(sem("weights_ready"), NG * MOE_NO[p] + g + 1)
                        for j in range(GB):
                            ins = nc.tensor.transpose(
                                B[4][0:96, 0:TG // 2].bitcast(BF16)[:, j * P:(j + 1) * P],
                                route[p]["parts"][:, j, :], identb)
                        ins.then_inc(sem(f"cw_mm{p}"), 1)
                    if i == FINISH_AT:
                        pe.wait_ge(sem(f"logits_read{p}"), g + 1)
                        finish_pe(pe, s)
                    if i == NORMED_AT:
                        norm_pe(pe, s + 1, 1 - h)
                    if i == NC + 3:
                        logits(s + 1, 1 - h)
                    c = i - TURN
                    if 0 <= c < NR:
                        if c == 0:
                            pe.wait_ge(sem(f"cw_ready{p}"), g + 1)
                        if c >= 2:
                            pe.wait_ge(sem(f"hh_ready{p}"), g * NR + c - 1)
                        at = SEL_AT[p] + c * P
                        nc.tensor.matmul(B[4 + c % 2][:], constb[0:3 * E, at:at + P], cw_t[0:3 * E, :],
                                         start=True, stop=True).then_inc(sem(f"bc_mm{p}"), 1)
                    c = i - DOWN
                    if 0 <= c < NC:
                        if c == 0:
                            pe.wait_ge(sem("ysb_ready"), s)
                        if by_pool(c):
                            pe.wait_ge(sem(f"lo_pool{p}"), g * (NC // 2) + c // 2 + 1)
                        else:
                            pe.wait_ge(sem(f"lo_dve{p}"), g * (NC - NC // 2) + c // 2 + 1)
                        product(Y[:], 2, slice(c * P, (c + 1) * P), su_hi[c % HI_RING], su_lo[c % RING],
                                start=(c == 0), stop=(c == NC - 1))\
                            .then_inc(sem(f"down_mm{p}") if c < NC - 1 else sem("y_ready"), 1)
            pe.wait_ge(sem(f"logits_read{p}"), NG + 1)

        def x_parts_act(act, p, s, h):
            act.wait_ge(sem("xhat_t_ready"), s + 1)
            nc.scalar.copy(x_hi, xhat_t[h][:]).then_inc(sem("x_hi_ready"), 1)

        def x_parts_dve(dve, p, g, h):
            dve.wait_ge(sem("x_hi_ready"), (NG + 1) * MOE_NO[p] + g + 2)
            nc.vector.tensor_tensor(x_lo, xhat_t[h][:], x_hi.bitcast(F32), ALU.subtract).then_inc(sem("x_lo_ready"), 1)

        def moe_act(act, p):
            m = MOE[p]
            NC, NR, E = m["NC"], m["NR"], m["E"]
            act.wait_ge(sem("y_ready"), NG * p)
            x_parts_act(act, p, NG * p, 0)

            def scores(g):
                if m["GK"]:
                    act.wait_ge(sem(f"logits{p}"), g + 2)
                    nc.scalar.activation(route[p]["sig"][:], logits_of(p), ACT.Sigmoid)\
                        .then_inc(sem(f"logits_read{p}"), 1)
                else:
                    act.wait_ge(sem("shifted"), g + 2)
                    nc.scalar.activation(route[p]["sig"][:], route[p]["r1"][:], ACT.Exp)\
                        .then_inc(sem("exp_ready"), 1)


            scores(-1)
            for g, _, _, h in stages(act, p):
                s = NG * p + g
                for i in range(NC + DOWN):
                    if i < NC:
                        act.wait_ge(sem(f"gate_mm{p}"), g * NC + i + 1)
                        if i >= 2:
                            act.wait_ge(sem(f"su_ready{p}"), g * NC + i - 1)
                        nc.scalar.activation(sg[i % 2][:], B[i % 2][:], ACT.Silu).then_inc(sem(f"sg_ready{p}"), 1)
                    if i == SCORES_AT[p]:
                        act.wait_ge(sem("weights_ready"), NG * MOE_NO[p] + g + 1)
                        scores(g)
                    if i == TURN - 1:
                        act.wait_ge(sem(f"cw_mm{p}"), g + 1)
                        nc.scalar.copy(cw_t[0:3 * E, :], B[4][0:3 * E, 0:TG // 2].bitcast(BF16))\
                            .then_inc(sem(f"cw_ready{p}"), 1)
                    if i == NORMED_AT:
                        norm_act(act, s + 1, 1 - h)
                    if i == NC + 1:
                        act.wait_ge(sem(f"up_mm{p}"), NC * (g + 1))
                        x_parts_act(act, p, s + 1, 1 - h)
                    c = i - TURN - 1
                    if 0 <= c < NC:
                        if c < NR:
                            act.wait_ge(sem(f"hh_ready{p}"), g * NR + c + 1)
                        else:
                            act.wait_ge(sem(f"su_ready{p}"), g * NC + c + 1)
                        if c >= HI_RING:
                            act.wait_ge(sem(f"down_mm{p}"), g * (NC - 1) + c - HI_RING + 1)
                        nc.scalar.copy(su_hi[c % HI_RING], su[c % RING]).then_inc(sem(f"hi_ready{p}"), 1)
                result_act(act, p, s)

        def low_part(eng, ops, p, g, c, name):
            eng.wait_ge(sem(f"hi_ready{p}"), g * MOE[p]["NC"] + c + 1)
            ops.tensor_tensor(su_lo[c % RING], su[c % RING], su_hi[c % HI_RING].bitcast(F32), ALU.subtract)\
                .then_inc(sem(f"{name}{p}"), 1)

        def moe_pool(pool, p, g):
            for c in range(MOE[p]["NC"]):
                if by_pool(c):
                    low_part(pool, nc.gpsimd, p, g, c, "lo_pool")

        def moe_dve(dve, st, p):
            m = MOE[p]
            NC, NR = m["NC"], m["NR"]
            x_parts_dve(dve, p, -1, 0)
            if not m["GK"]:
                for _ in route_begin(dve, st, p, -1):
                    pass
            for g, before, after, h in stages(dve, p, st):
                s = NG * p + g
                pieces = route_groups(dve, st, p, g) if m["GK"] else route_top2(dve, st, p, g)
                begin = iter(()) if m["GK"] else route_begin(dve, st, p, g)
                for i in range(NC + DOWN):
                    next(pieces if i < NC + 4 else begin, None)
                    if i < NC:
                        dve.wait_ge(sem(f"sg_ready{p}"), g * NC + i + 1)
                        dve.wait_ge(sem(f"up_mm{p}"), g * NC + i + 1)
                        if i == 0:
                            dve.wait_ge(sem("y_ready"), s)
                        elif i >= RING:
                            dve.wait_ge(sem(f"down_mm{p}"), g * (NC - 1) + i - RING + 1)
                        nc.vector.tensor_tensor(su[i % RING], sg[i % 2][:], B[2 + i % 2][:], ALU.mult)\
                            .then_inc(sem(f"su_ready{p}"), 1)
                    if i == FINISH_AT:
                        finish_dve(dve, before, s)
                    if i == STATS_AT:
                        norm_stats(st, after)
                    if i == NORM_AT:
                        norm_apply(dve, after, s + 1, 1 - h)
                    if i == NC + 2:
                        x_parts_dve(dve, p, g, 1 - h)
                    c = i - TURN
                    if 0 <= c < NR:
                        dve.wait_ge(sem(f"bc_mm{p}"), g * NR + c + 1)
                        dve.wait_ge(sem(f"su_ready{p}"), g * NC + c + 1)
                        nc.vector.tensor_tensor(su[c % RING], su[c % RING], B[4 + c % 2][:], ALU.mult)\
                            .then_inc(sem(f"hh_ready{p}"), 1)
                    c -= 2
                    if 0 <= c < NC and not by_pool(c):
                        low_part(dve, nc.vector, p, g, c, "lo_dve")

        area2 = Area()
        k2, q2, v2, pr2, pn2, pt2, aq2 = ([area2.tile([P, TG]) for i in range(2)] for _ in range(7))
        mx2, nb2, rs2, ri2 = ([sb(f"{n}{i}", [P, GB]) for i in range(2)] for n in ("mx2_", "nb2_", "rs2_", "ri2_"))
        SCALE2 = float(P) ** -0.5

        def tiles(j):
            return slice(j * P, (j + 1) * P)

        def p2_pe(pe):
            p, mm = 2, nc.tensor.matmul

            def kv(g, h):
                pe.wait_ge(sem("cg_ready"), g + 1)
                mm(B[3 * h][:], wkc[:], cg[h][:], start=True, stop=True).then_inc(sem("k_mm2"), 1)
                for j in range(GB):
                    ins = mm(B[3 * h + 1][:, tiles(j)], cg[h][:, tiles(j)], wvc[:], start=True, stop=True)
                ins.then_inc(sem("v_mm2"), 1)

            def q(g, h):
                pe.wait_ge(sem("xhat_t_ready"), NG * p + g + 1)
                mm(B[3 * h + 2][:], wqh[:], xhat_t[h][:], start=True, stop=True).then_inc(sem("q_mm2"), 1)

            def score(g, h):
                pe.wait_ge(sem("qk_ready2"), 2 * g + 2)
                for j in range(GB):
                    ins = mm(B[3 * h][:, tiles(j)], q2[h][:, tiles(j)], k2[h][:, tiles(j)], start=True, stop=True)
                ins.then_inc(sem("score_mm2"), 1)

            def turn(g, h):
                pe.wait_ge(sem("pn_ready2"), g + 1)
                pe.wait_ge(sem("v_ready2"), g + 1)
                for j in range(GB):
                    ins = nc.tensor.transpose(B[3 * h + 1][:, tiles(j)], pn2[h][:, tiles(j)], ident)
                ins.then_inc(sem("pt_mm2"), 1)

            def values(g, h):
                pe.wait_ge(sem("pt_ready2"), g + 1)
                for j in range(GB):
                    ins = mm(B[3 * h + 2][:, tiles(j)], v2[h][:, tiles(j)], pt2[h][:, tiles(j)], start=True, stop=True)
                ins.then_inc(sem("av_mm2"), 1)

            def result(g, h):
                pe.wait_ge(sem("aq_ready2"), g + 1)
                pe.wait_ge(sem("ysb_ready"), NG * p + g)
                mm(Y[:], S("oWT"), aq2[h][:], start=True, stop=True).then_inc(sem("y_ready"), 1)

            for a, b, _ in pairs(pe, p):
                s = NG * p + a
                kv(a, 0)
                q(a, 0)
                finish_pe(pe, s)
                kv(b, 1)
                norm_pe(pe, s + 1, 1)
                score(a, 0)
                q(b, 1)
                score(b, 1)
                turn(a, 0)
                values(a, 0)
                turn(b, 1)
                result(a, 0)
                values(b, 1)
                finish_pe(pe, s + 1)
                result(b, 1)
                norm_pe(pe, s + 2, 0)

        def p2_act(act):
            p = 2

            def k(g, h):
                act.wait_ge(sem("k_mm2"), g + 1)
                nc.scalar.activation(k2[h][:], B[3 * h][:], ACT.Identity, bias=bcols[:, 1:2])\
                    .then_inc(sem("qk_ready2"), 1)

            def q(g, h):
                act.wait_ge(sem("q_mm2"), g + 1)
                nc.scalar.activation(q2[h][:], B[3 * h + 2][:], ACT.Identity, bias=bcols[:, 0:1])\
                    .then_inc(sem("qk_ready2"), 1)

            def exp(g, h):
                act.wait_ge(sem("nb_ready2"), g + 1)
                for j in range(GB):
                    ins = nc.scalar.activation(pr2[h][:, tiles(j)], B[3 * h][:, tiles(j)], ACT.Exp,
                                               bias=nb2[h][:, j:j + 1], scale=SCALE2, accum_out=rs2[h][:, j:j + 1])
                ins.then_inc(sem("exp_ready2"), 1)

            def turned(g, h):
                act.wait_ge(sem("pt_mm2"), g + 1)
                nc.scalar.copy(pt2[h][:], B[3 * h + 1][:]).then_inc(sem("pt_ready2"), 1)

            for a, b, _ in pairs(act, p):
                s = NG * p + a
                k(a, 0)
                q(a, 0)
                k(b, 1)
                norm_act(act, s + 1, 1)
                exp(a, 0)
                q(b, 1)
                turned(a, 0)
                exp(b, 1)
                weights_hi(act, 3, a, (0,))
                turned(b, 1)
                weights_hi(act, 3, a, (1,))
                result_act(act, p, s)
                weights_hi(act, 3, a, (2,))
                weights_hi(act, 3, b, (0,))
                result_act(act, p, s + 1)
                norm_act(act, s + 2, 0)
                weights_hi(act, 3, b, (1, 2))

        def p2_dve(dve, st):
            p, v = 2, nc.vector

            def js(a):
                return a.rearrange("p (j k) -> p j k", j=GB)

            def values(g, h):
                dve.wait_ge(sem("v_mm2"), g + 1)
                v.tensor_copy(v2[h][:], B[3 * h + 1][:]).then_inc(sem("v_ready2"), 1)

            def maxima(g, h):
                dve.wait_ge(sem("score_mm2"), g + 1)
                st.add(v.tensor_reduce(mx2[h][:], js(B[3 * h][:]), AX.X, ALU.max))
                st.settle()
                v.tensor_scalar(nb2[h][:], mx2[h][:], -SCALE2, None, ALU.mult).then_inc(sem("nb_ready2"), 1)

            def normed(g, h):
                dve.wait_ge(sem("exp_ready2"), g + 1)
                st.add(v.reciprocal(ri2[h][:], rs2[h][:]))
                st.settle()
                v.tensor_tensor(js(pn2[h][:]), js(pr2[h][:]), ri2[h][:].unsqueeze(2).to_broadcast([P, GB, P]),
                                ALU.mult).then_inc(sem("pn_ready2"), 1)

            def plus_q(g, h):
                dve.wait_ge(sem("av_mm2"), g + 1)
                v.tensor_tensor(aq2[h][:], B[3 * h + 2][:], q2[h][:], ALU.add).then_inc(sem("aq_ready2"), 1)

            for a, b, after in pairs(dve, p, st):
                s = NG * p + a
                norm_stats(st, b)
                values(a, 0)
                finish_dve(dve, after + 1, s)
                norm_apply(dve, b, s + 1, 1)
                values(b, 1)
                maxima(a, 0)
                normed(a, 0)
                maxima(b, 1)
                norm_stats(st, after)
                plus_q(a, 0)
                normed(b, 1)
                finish_dve(dve, a, s + 1)
                norm_apply(dve, after, s + 2, 0)
                plus_q(b, 1)

        area4 = Area()
        qh = [area4.tile([P, TG], shared_r) for i in range(HEAD_TILES)]
        kh = [area4.tile([P, TG], shared_r) for i in range(HEAD_TILES)]
        k_each = [area4.tile([P, HEAD_TILES, TG], shared_r) for i in range(2)]
        hi_act = area4.tile([P, TG], shared_r)
        full_act = area4.tile([P, TG])
        low_dve = area4.tile([P, TG], shared_r)
        sd = [area4.tile([P, TG]) for i in range(2)]
        es = [area4.tile([P, TG]) for i in range(2)]
        pt = [area4.tile([P, TG]) for i in range(2)]
        os = area4.tile([P, TG])
        osb = area4.tile([P, GB, HEADS, DK])
        oT = area4.tile([P, TG])
        oc = area4.tile([P, 2, HEADS // 2, DK])
        vh = sb("vh", [P, GB * HEADS, VW])
        vc = sb("vc", [P, GB * HEADS // 4, 2 * VW])
        mxh = [sb(f"mxh{i}", [P, HEAD_TILES]) for i in range(2)]
        rden = sb("rden", [P, GB * HEAD_TILES])
        b_low = {p: sb(f"b_low{p}", [P, 2, HEAD_TILES]) for p in (4, 6)}
        SCALEH = float(DK) ** -0.5
        UNITS = [(j, a) for a in range(HEADS // HEAD_TILES) for j in range(GB)]
        NU = len(UNITS)

        TILES = [("k", 0), ("k", 1), ("q", 0), ("q", 1), ("k", 2), ("k", 3), ("q", 2), ("q", 3)]
        NT = len(TILES)
        BANK = (0, 1, 2, 3, 0, 1, 0, 1)

        def coarse(p, a):
            return p == 6 and a >= 2

        def width(p, a):
            return HALF if coarse(p, a) else P

        def heads_pe(pe, p):
            mm = nc.tensor.matmul
            base = 0 if p == 4 else NG
            def tile(g, s, h, x):
                kq, i = TILES[x]
                if x == 0:
                    pe.wait_ge(sem("cg_ready"), NG * (1 if p == 4 else 2) + g + 1)
                if x == 2:
                    pe.wait_ge(sem("xhat_t_ready"), s + 1)
                if x >= 4:
                    before = max(y for y in range(x) if BANK[y] == BANK[x])
                    pe.wait_ge(sem(f"parts{p}"), NT * g + before + 1)
                mm(B[BANK[x]][:], S(f"W{kq}{p}", i * P, (i + 1) * P), (cg if kq == "k" else xhat_t)[h][:],
                   start=True, stop=True).then_inc(sem(f"proj_mm{p}"), 1)

            def values(h):
                for j in range(GB):
                    ins = mm(B[4][:, j * P:(j + 1) * P], cg[h][:, j * P:(j + 1) * P], S(f"Wv{p}"),
                             start=True, stop=True)
                if p == 6:
                    rows, at, _ = SMALL_AT["Wv6"]
                    for j in range(GB):
                        ins = mm(B[5][0:HALF, j * HALF:(j + 1) * HALF], cg[h][:, j * P:(j + 1) * P:2],
                                 small[:, at + HALF:at + P], start=True, stop=True)
                ins.then_inc(sem(f"v_mm{p}"), 1)

            for x in range(NT):
                tile(0, NG * p, 0, x)
            values(0)
            for g, _, _, h in stages(pe, p):
                s = NG * p + g
                for t in range(NU + 6):
                    if t < NU:
                        j, a = UNITS[t]
                        w, cols = width(p, a), slice(j * P, (j + 1) * P, P // width(p, a))
                        if t < 2:
                            pe.wait_ge(sem(f"parts{p}"), NT * (g + 1) - 1 + t)
                        if j == 0:
                            pe.wait_ge(sem(f"k_each{p}"), HEAD_TILES * g + a + 1)
                        if t >= 2:
                            pe.wait_ge(sem(f"sd_ready{p}"), NU * g + t - 1)
                        bank = B[t % 2]
                        if p == 4:
                            mm(bank[:], identb, maskb[:].rearrange("p a k -> p (a k)"), start=True, stop=False)
                        mm(bank[0:w, 0:4 * w].rearrange("p (i k) -> p i k", i=HEAD_TILES), qh[a][:, cols],
                           k_each[a % 2][:, :, cols], start=(p == 6), stop=True).then_inc(sem(f"score_mm{p}"), 1)
                    if t >= NU:
                        if t == NU:
                            pe.wait_ge(sem(f"sd_ready{p}"), NU * (g + 1))
                        if t in (NU + 1, NU + 2):
                            pe.wait_ge(sem(f"pt_ready{p}"), NU * g + t - 2)
                        for x in {NU: (0, 1), NU + 1: (2,), NU + 2: (3,), NU + 3: (4,), NU + 4: (5,), NU + 5: (6,)}[t]:
                            tile(g + 1, s + 1, 1 - h, x)
                    if t == 3:
                        finish_pe(pe, s)
                    if t == 8:
                        norm_pe(pe, s + 1, 1 - h)
                    u = t - 2
                    if 0 <= u < NU:
                        j, a = UNITS[u]
                        w = width(p, a)
                        pe.wait_ge(sem(f"es_ready{p}"), NU * g + u + 1)
                        if u == 0:
                            pe.wait_ge(sem(f"v_ready{p}"), g + 1)
                        if u >= 2:
                            pe.wait_ge(sem(f"pt_ready{p}"), NU * g + u - 1)
                        for i in range(4 * w // P):
                            c = slice(i * P, (i + 1) * P)
                            ins = nc.tensor.transpose(B[2 + u % 2][:, c], es[u % 2][:, c], ident)
                        ins.then_inc(sem(f"pt_mm{p}"), 1)
                    u = t - 3
                    if 0 <= u < NU:
                        j, a = UNITS[u]
                        w = width(p, a)
                        pe.wait_ge(sem(f"pt_ready{p}"), NU * g + u + 1)
                        if j == 0 and a >= 2:
                            pe.wait_ge(sem(f"os_ready{p}"), 4 * g + a - 1)
                        heads = P // w
                        for i in range(0, HEAD_TILES, heads):
                            if coarse(p, a):
                                val = vc[:, j * (HEADS // 4) + 2 * (a - 2) + i // 2, :]
                            else:
                                val = vh[:, j * HEADS + 4 * a + i, :]
                            ins = mm(B[4 + a % 2][VW * i:VW * (i + heads), j * w:(j + 1) * w], val,
                                     pt[u % 2][:, i // heads * w:(i // heads + 1) * w], start=True, stop=True)
                        ins.then_inc(sem(f"pv_mm{p}"), 1)
                    a = t // 4 - 2
                    if t % 4 == 0 and a >= 0:
                        pe.wait_ge(sem(f"os_ready{p}"), 4 * g + a + 1)
                        if a == 0:
                            pe.wait_ge(sem("ysb_ready"), s)
                        else:
                            pe.wait_ge(sem(f"osb_ready{p}"), 4 * g + a)
                        for x in range(GB * width(p, a) // P):
                            ins = nc.tensor.transpose(Y[:, x * P:(x + 1) * P], os[:, x * P:(x + 1) * P], ident)
                        ins.then_inc(sem(f"ob_mm{p}"), 1)
                pe.wait_ge(sem(f"osb_ready{p}"), 4 * g + 4)
                if p == 6:
                    for y in range(2):
                        ins = mm(B[2][:, y * P:(y + 1) * P], K("up")[:, y * P:(y + 1) * P],
                                 oc[:].rearrange("p x n d -> p (x n d)"), start=True, stop=True)
                    ins.then_inc(sem("up_mm"), 1)
                    pe.wait_ge(sem("up_ready"), g + 1)
                values(1 - h)
                for j in range(GB):
                    ins = nc.tensor.transpose(B[3][:, j * P:(j + 1) * P],
                                              osb[:, j, :, :].rearrange("p n d -> p (n d)"), ident)
                ins.then_inc(sem(f"oT_mm{p}"), 1)
                tile(g + 1, s + 1, 1 - h, 7)
                pe.wait_ge(sem(f"oT_ready{p}"), g + 1)
                mm(Y[:], S(f"Wo{p}"), oT[:], start=True, stop=True).then_inc(sem("y_ready"), 1)
            pe.wait_ge(sem(f"parts{p}"), NT * (NG + 1))
            pe.wait_ge(sem(f"v_ready{p}"), NG + 1)

        def heads_act(act, p):
            def tile(g, x):
                kq, i = TILES[x]
                c = "qk".index(kq)
                act.wait_ge(sem(f"proj_mm{p}"), NT * g + x + 1)
                if x > 1:
                    act.wait_ge(sem(f"parts{p}"), NT * g + x - 1)
                nc.scalar.activation(hi_act[:], B[BANK[x]][:], ACT.Identity, bias=S(f"b{kq}{p}", i, i + 1))
                nc.scalar.activation(full_act[:], B[BANK[x]][:], ACT.Identity, scale=K("low")[:, c:c + 1],
                                     bias=b_low[p][:, c, i:i + 1]).then_inc(sem(f"hi_act{p}"), 1)

            for x in (1, 3, 5, 7):
                tile(0, x)
            for g, _, _, h in stages(act, p):
                s = NG * p + g
                for t in range(NU + 4):
                    a = (t - 7) // 4
                    if t >= 7 and (t - 7) % 4 == 0:
                        act.wait_ge(sem(f"pv_mm{p}"), NU * g + 4 * a + 4)
                        if a >= 1:
                            act.wait_ge(sem(f"ob_mm{p}"), 4 * g + a)
                        nc.scalar.copy(os[:, 0:GB * width(p, a)], B[4 + a % 2][:, 0:GB * width(p, a)])\
                            .then_inc(sem(f"os_ready{p}"), 1)
                    if t < NU:
                        j, a = UNITS[t]
                        w = width(p, a)
                        act.wait_ge(sem(f"sd_ready{p}"), NU * g + t + 1)
                        if t >= 2:
                            act.wait_ge(sem(f"pt_mm{p}"), NU * g + t - 1)
                        nc.scalar.activation(es[t % 2][0:w, 0:4 * w], sd[t % 2][0:w, 0:4 * w], ACT.Exp,
                                             scale=SCALEH).then_inc(sem(f"es_ready{p}"), 1)
                    if t == 9:
                        norm_act(act, s + 1, 1 - h)
                    if t >= NU and t != NU + 2:
                        tile(g + 1, {NU: 1, NU + 1: 3, NU + 3: 5}[t])
                    u = t - 1
                    if 0 <= u < NU:
                        j, a = UNITS[u]
                        w = width(p, a)
                        act.wait_ge(sem(f"pt_mm{p}"), NU * g + u + 1)
                        if u >= 2:
                            act.wait_ge(sem(f"pv_mm{p}"), NU * g + u - 1)
                        nc.scalar.copy(pt[u % 2][:, 0:4 * w * w // P].rearrange("p (i q) -> p i q", q=w),
                                       B[2 + u % 2][:, 0:4 * w].rearrange("p (i q) -> p i q", q=P)[:, :, 0:w])\
                            .then_inc(sem(f"pt_ready{p}"), 1)
                act.wait_ge(sem(f"oT_mm{p}"), g + 1)
                nc.scalar.copy(oT[:], B[3][:]).then_inc(sem(f"oT_ready{p}"), 1)
                tile(g + 1, 7)
                result_act(act, p, s)
            act.wait_ge(sem(f"parts{p}"), NT * (NG + 1))

        def heads_pool(pool, p, g, groups):
            for a in groups:
                cols = slice(0, TG, P // width(p, a))
                pool.wait_ge(sem(f"parts{p}"), NT * g + TILES.index(("k", a)) + 1)
                if a >= 2:
                    pool.wait_ge(sem(f"score_mm{p}"), NU * g + GB * (a - 1))
                for i in range(HEAD_TILES):
                    ins = nc.gpsimd.tensor_tensor(k_each[a % 2][:, i, cols], kh[a][:, cols].bitcast(F32),
                                                  K("rowmask")[:, i:i + 1].to_broadcast([P, TG * width(p, a) // P]),
                                                  ALU.mult)
                ins.then_inc(sem(f"k_each{p}"), 1)

        def heads_dve(dve, st, p):
            v = nc.vector

            def tile(g, x):
                kq, i = TILES[x]
                c = "qk".index(kq)
                out = (kh if kq == "k" else qh)[i]
                if x % 2:
                    dve.wait_ge(sem(f"hi_act{p}"), NT // 2 * g + x // 2 + 1)
                    ins = v.scalar_tensor_tensor(out[:], hi_act.bitcast(F32), K("sign")[:, c:c + 1], full_act[:],
                                                 ALU.mult, ALU.add)
                else:
                    dve.wait_ge(sem(f"proj_mm{p}"), NT * g + x + 1)
                    if x:
                        dve.wait_ge(sem(f"parts{p}"), NT * g + x - 1)
                    bias = S(f"b{kq}{p}", i, i + 1)
                    st.add(v.tensor_scalar(low_dve[:], B[BANK[x]][:], bias, K("low")[:, c:c + 1], ALU.add, ALU.mult))
                    st.settle()
                    ins = v.scalar_tensor_tensor(out[:], B[BANK[x]][:], bias, low_dve.bitcast(F32), ALU.add, ALU.subtract)
                ins.then_inc(sem(f"parts{p}"), 1)

            def values(g):
                dve.wait_ge(sem(f"v_mm{p}"), g + 1)
                ins = v.tensor_copy(vh[:, :, 0:DK], B[4][:].rearrange("p (n d) -> p n d", d=DK))
                if p == 6:
                    for k in range(2):
                        ins = v.tensor_copy(
                            vc[k * HALF:(k + 1) * HALF, :, k * VW:k * VW + DK],
                            B[5][0:HALF, 0:GB * HALF].rearrange("p (n k d) -> p n k d", k=2, d=DK)[:, :, k, :])
                ins.then_inc(sem(f"v_ready{p}"), 1)

            for x in range(NT):
                tile(0, x)
            values(0)
            for g, before, after, h in stages(dve, p, st):
                s = NG * p + g
                for t in range(NU + 6):
                    a = (t - 9) // 4
                    if t >= 9 and (t - 9) % 4 == 0:
                        c = coarse(p, a)
                        n = GB * width(p, a) // 32
                        back = Y[:, 0:n * 32].rearrange("p (n d) -> p n d", d=32)
                        dve.wait_ge(sem(f"ob_mm{p}"), 4 * g + a + 1)
                        st.add(v.reciprocal(rden[:, 0:n], back[:, :, DK]))
                        st.settle()
                        dst = oc[:, :, 4 * (a - 2):4 * (a - 1), :] if c else osb[:, :, 4 * a:4 * a + 4, :]
                        v.tensor_tensor(dst, back[:, :, 0:DK].rearrange("p (x i) d -> p x i d", i=HEAD_TILES),
                                        rden[:, 0:n].rearrange("p (x i) -> p x i", i=HEAD_TILES).unsqueeze(3)
                                        .to_broadcast([P, n // 4, 4, DK]), ALU.mult).then_inc(sem(f"osb_ready{p}"), 1)
                    if t >= NU and t < NU + 5:
                        tile(g + 1, t - NU)
                    if t >= NU:
                        continue
                    if t == 2:
                        norm_stats(st, after)
                    if t == 4:
                        finish_dve(dve, before, s)
                    j, a = UNITS[t]
                    w = width(p, a)
                    bank = B[t % 2][0:w, 0:4 * w].rearrange("p (i k) -> p i k", i=4)
                    dve.wait_ge(sem(f"score_mm{p}"), NU * g + t + 1)
                    st.add(v.tensor_reduce(mxh[t % 2][0:w, :], bank, AX.X, ALU.max))
                    st.settle()
                    if t >= 2:
                        dve.wait_ge(sem(f"es_ready{p}"), NU * g + t - 1)
                    v.tensor_tensor(sd[t % 2][0:w, 0:4 * w].rearrange("p (i k) -> p i k", i=4), bank,
                                    mxh[t % 2][0:w, :].unsqueeze(2).to_broadcast([w, 4, w]), ALU.subtract)\
                        .then_inc(sem(f"sd_ready{p}"), 1)
                    if t == 6:
                        norm_apply(dve, after, s + 1, 1 - h)
                if p == 6:
                    dve.wait_ge(sem("up_mm"), g + 1)
                    v.tensor_copy(osb[:, :, 8:16, :].rearrange("p (x y) n d -> p y x (n d)", y=2),
                                  B[2][:, 0:2 * P].rearrange("p (y x n) -> p y x n", y=2, x=2))\
                        .then_inc(sem("up_ready"), 1)
                tile(g + 1, 5)
                values(g + 1)
                tile(g + 1, 6)
                tile(g + 1, 7)

        area5 = Area()
        NS = GB * SLOTS
        h5 = [area5.tile([SLOT_HID + 1, TG]) for i in range(2)]
        lg5, wk5, e5, al5 = ([area5.tile([P, GB, SLOTS]) for i in range(2)] for _ in range(4))
        m85 = [area5.tile([P, GB, 8]) for i in range(2)]
        tot5, rec5 = ([sb(f"{n}{i}", [P, GB]) for i in range(2)] for n in ("tot5_", "rec5_"))
        at5, sv5 = ([area5.tile([SLOTS, TG]) for i in range(2)] for _ in range(2))
        ws5, gi5, t5, n5, hn5 = ([area5.tile([P, NS]) for i in range(2)] for _ in range(5))
        rz5 = [area5.tile([P, 2, NS]) for i in range(2)]
        ones5 = sb("ones5", [P, P])

        def p5_pe(pe):
            p, mm = 5, nc.tensor.matmul

            def hidden(g, h):
                pe.wait_ge(sem("xhat_t_ready"), NG * p + g + 1)
                mm(B[3 * h][0:SLOT_HID, :], S("w1x"), xhat_t[h][:], start=True, stop=True).then_inc(sem("h_mm5"), 1)

            def logits(g, h):
                pe.wait_ge(sem("h_ready5"), g + 1)
                for j in range(GB):
                    ins = mm(B[3 * h + 1][:, j * SLOTS:(j + 1) * SLOTS], h5[h][:, tiles(j)], S("w2"),
                             start=True, stop=True)
                ins.then_inc(sem("logit_mm5"), 1)

            def gather(g, h):
                pe.wait_ge(sem("al_ready5"), g + 1)
                for j in range(GB):
                    mm(B[3 * h + 2][:, j * SLOTS:(j + 1) * SLOTS], xhat[h][:, tiles(j)], al5[h][:, j, :],
                       start=True, stop=True)
                mm(B[3 * h + 2][:, NS:2 * NS], ones5[:], al5[h][:].rearrange("p j s -> p (j s)"),
                   start=True, stop=True).then_inc(sem("in_mm5"), 1)
                for j in range(GB):
                    ins = nc.tensor.transpose(B[3 * h][0:SLOTS, tiles(j)], al5[h][:, j, :], ident)
                ins.then_inc(sem("at_mm5"), 1)

            def gru(g, h):
                pe.wait_ge(sem("gi_ready5"), g + 1)
                for c in range(2):
                    mm(B[3 * h + 1][:, c * NS:(c + 1) * NS], S("wih", c * P, (c + 1) * P), gi5[h][:],
                       start=True, stop=True)
                mm(B[3 * h + 2][:, 0:NS], S("wih", 2 * P, 3 * P), gi5[h][:], start=True, stop=True)\
                    .then_inc(sem("gx_mm5"), 1)

            def slot_values(g, h):
                pe.wait_ge(sem("hn_ready5"), g + 1)
                pe.wait_ge(sem("at_ready5"), g + 1)
                for j in range(GB):
                    ins = mm(B[3 * h][0:SLOTS, tiles(j)], hn5[h][:, j * SLOTS:(j + 1) * SLOTS], wvo[:],
                             start=True, stop=True)
                ins.then_inc(sem("sv_mm5"), 1)

            def result(g, h):
                pe.wait_ge(sem("sv_ready5"), g + 1)
                pe.wait_ge(sem("ysb_ready"), NG * p + g)
                for j in range(GB):
                    ins = mm(Y[:, tiles(j)], sv5[h][:, tiles(j)], at5[h][:, tiles(j)], start=True, stop=True)
                ins.then_inc(sem("y_ready"), 1)

            pe.wait_ge(sem("ones_ready5"), 2)
            for a, b, _ in pairs(pe, p):
                s = NG * p + a
                hidden(a, 0)
                finish_pe(pe, s)
                logits(a, 0)
                norm_pe(pe, s + 1, 1)
                hidden(b, 1)
                logits(b, 1)
                for step in (gather, gru, slot_values):
                    step(a, 0)
                    step(b, 1)
                result(a, 0)
                finish_pe(pe, s + 1)
                result(b, 1)
                norm_pe(pe, s + 2, 0)

        def p5_act(act):
            p = 5

            def hidden(g, h):
                act.wait_ge(sem("h_mm5"), g + 1)
                nc.scalar.activation(h5[h][0:SLOT_HID, :], B[3 * h][0:SLOT_HID, :], ACT.Gelu, bias=b1x[:])\
                    .then_inc(sem("h_ready5"), 1)

            def exp(g, h):
                act.wait_ge(sem("shift_ready5"), g + 1)
                nc.scalar.activation(e5[h][:], e5[h][:], ACT.Exp, scale=rtau[:]).then_inc(sem("exp_ready5"), 1)

            def turned(g, h):
                act.wait_ge(sem("at_mm5"), g + 1)
                nc.scalar.copy(at5[h][:], B[3 * h][0:SLOTS, :]).then_inc(sem("at_ready5"), 1)

            def gates(g, h):
                act.wait_ge(sem("rzx_ready5"), g + 1)
                nc.scalar.activation(rz5[h][:], rz5[h][:], ACT.Sigmoid).then_inc(sem("rz_ready5"), 1)

            def candidate(g, h):
                act.wait_ge(sem("nx_ready5"), g + 1)
                nc.scalar.activation(n5[h][:], t5[h][:], ACT.Tanh, bias=S("bih", 2, 3)).then_inc(sem("n_ready5"), 1)

            def slot_values(g, h):
                act.wait_ge(sem("sv_mm5"), g + 1)
                nc.scalar.copy(sv5[h][:], B[3 * h][0:SLOTS, :]).then_inc(sem("sv_ready5"), 1)

            for a, b, _ in pairs(act, p):
                s = NG * p + a
                hidden(a, 0)
                norm_act(act, s + 1, 1)
                hidden(b, 1)
                for step in (exp, turned, gates, candidate, slot_values):
                    step(a, 0)
                    step(b, 1)
                result_act(act, p, s)
                result_act(act, p, s + 1)
                norm_act(act, s + 2, 0)

        def p5_dve(dve, st):
            p, v = 5, nc.vector

            def bs(a):
                return a.unsqueeze(1).to_broadcast([P, GB, SLOTS])

            def js(a):
                return a.rearrange("p (j s) -> p j s", j=GB)

            def shift(g, h):
                dve.wait_ge(sem("logit_mm5"), g + 1)
                st.add(v.tensor_copy(lg5[h][:], js(B[3 * h + 1][:, 0:NS])))
                st.settle()
                for j in range(GB):
                    st.add(v.max(out=m85[h][:, j, :], in_=lg5[h][:, j, :]))
                st.settle()
                v.tensor_tensor(e5[h][:], lg5[h][:], m85[h][:, :, 0:1].to_broadcast([P, GB, SLOTS]), ALU.subtract)\
                    .then_inc(sem("shift_ready5"), 1)

            def chosen(g, h):
                for j in range(GB):
                    st.add(v.match_replace(out=wk5[h][:, j, :], in_to_replace=m85[h][:, j, :],
                                           in_values=lg5[h][:, j, :], imm_value=TAKEN))
                st.settle()
                st.add(v.tensor_scalar(wk5[h][:], wk5[h][:], TAKEN, None, ALU.is_equal))
                st.settle()

            def weights(g, h):
                dve.wait_ge(sem("exp_ready5"), g + 1)
                st.add(v.tensor_tensor(al5[h][:], e5[h][:], wk5[h][:], ALU.mult))
                st.settle()
                st.add(v.tensor_reduce(tot5[h][:], al5[h][:], AX.X, ALU.add))
                st.settle()
                st.add(v.reciprocal(rec5[h][:], tot5[h][:]))
                st.settle()
                v.tensor_tensor(al5[h][:], al5[h][:], rec5[h][:].unsqueeze(2).to_broadcast([P, GB, SLOTS]), ALU.mult)\
                    .then_inc(sem("al_ready5"), 1)

            def gathered(g, h):
                dve.wait_ge(sem("in_mm5"), g + 1)
                st.add(v.tensor_scalar(ws5[h][:], B[3 * h + 2][:, NS:2 * NS], 1e-8, None, ALU.add))
                st.settle()
                st.add(v.reciprocal(ws5[h][:], ws5[h][:]))
                st.settle()
                v.tensor_tensor(gi5[h][:], B[3 * h + 2][:, 0:NS], ws5[h][:], ALU.mult).then_inc(sem("gi_ready5"), 1)

            def gates(g, h):
                dve.wait_ge(sem("gx_mm5"), g + 1)
                for c in range(2):
                    ins = v.tensor_tensor(js(rz5[h][:, c, :]), js(B[3 * h + 1][:, c * NS:(c + 1) * NS]),
                                          bs(gh_rz[:, c, :]), ALU.add)
                ins.then_inc(sem("rzx_ready5"), 1)

            def candidate(g, h):
                dve.wait_ge(sem("rz_ready5"), g + 1)
                st.add(v.tensor_tensor(js(t5[h][:]), js(rz5[h][:, 0, :]), bs(gh_n[:]), ALU.mult))
                st.settle()
                v.tensor_tensor(t5[h][:], t5[h][:], B[3 * h + 2][:, 0:NS], ALU.add).then_inc(sem("nx_ready5"), 1)

            def new_state(g, h):
                dve.wait_ge(sem("n_ready5"), g + 1)
                st.add(v.tensor_tensor(js(hn5[h][:]), bs(hs_t[:]), js(n5[h][:]), ALU.subtract))
                st.settle()
                st.add(v.tensor_tensor(hn5[h][:], hn5[h][:], rz5[h][:, 1, :], ALU.mult))
                st.settle()
                v.tensor_tensor(hn5[h][:], hn5[h][:], n5[h][:], ALU.add).then_inc(sem("hn_ready5"), 1)

            for i in range(2):
                v.memset(h5[i][SLOT_HID:SLOT_HID + 1, :], 1.0).then_inc(sem("ones_ready5"), 1)
            for a, b, after in pairs(dve, p, st):
                s = NG * p + a
                norm_stats(st, b)
                finish_dve(dve, after + 1, s)
                norm_apply(dve, b, s + 1, 1)
                shift(a, 0)
                chosen(a, 0)
                shift(b, 1)
                weights(a, 0)
                chosen(b, 1)
                weights(b, 1)
                norm_stats(st, after)
                for step in (gathered, gates, candidate, new_state):
                    step(a, 0)
                    step(b, 1)
                norm_apply(dve, after, s + 2, 0)
                finish_dve(dve, a, s + 1)
                st.add(v.memset(tot5[0][:], 0.0))

        block = ctx.enter_context(nc.Block())

        @block.sync
        def _(sp):
            for g in range(NG):
                c = slice(g * TG, (g + 1) * TG)
                sp.dma_start(X[:, c], x_d[:, c]).then_inc(sem(f"x_loaded{g}"), 16)
                if g == 0:
                    n = 2 * P
                    sp.dma_start(const[:, 0:n], const_d[:, 0:n]).then_inc(sem("const_loaded"), 16)
                sp.dma_start(CT[:, c], ctx_d[:, c]).then_inc(sem(f"ctx_loaded{g}"), 16)
            sp.dma_start(mask_i[:], mask_d).then_inc(sem("small_loaded"), 16)
            sp.dma_start(const[:, 2 * P:], const_d[:, 2 * P:]).then_inc(sem("const_rest_loaded"), 16)
            for p in MOE:
                if phases <= SPLIT_IN[p]:
                    continue
                if p > 1:
                    sp.wait_ge(sem("y_ready"), NG * SPLIT_IN[p])
                n = MOE[p]["NC"] * P // NG
                for g in range(NG):
                    for k in range(3):
                        sp.dma_start(w_raw[k][:, g * n:(g + 1) * n], moe_d[p][k][:, g * n:(g + 1) * n])\
                            .then_inc(sem(f"raw{p}"), 16)
                    sp.wait_ge(sem(f"raw{p}"), 48 * (g + 1))
            for g in range(NG):
                sp.wait_ge(sem("x_updated"), last - NG + 1 + g)
                c = slice(g * TG, (g + 1) * TG)
                sp.dma_start(out_d[:, c], X[:, c]).then_inc(sem("stored"), 16)
            sp.wait_ge(sem("stored"), 16 * NG)
            if phases < PHASES:
                sp.wait_ge(sem("constb_loaded"), 16)

        @block.gpsimd
        def _(pool):
            gp = nc.gpsimd
            gp.memset(minus_half[:], -0.5).then_inc(sem("rstd_ready"), 1)
            pool.wait_ge(sem("rstd_ready"), 1)

            def power(s):
                pool.wait_ge(sem("var_ready"), s + 1)
                gp.tensor_tensor(rstd[:], var[:], minus_half[:], ALU.pow).then_inc(sem("rstd_ready"), 1)

            power(0)
            for g in range(NG):
                power(g + 1)
                weights_lo(pool, 1, g, 0)
            for c in range(NG):
                pool.wait_ge(sem(f"ctx_loaded{c}"), 16)
            gp.tensor_copy(cg[0][:], CT[:, 0:TG]).then_inc(sem("cg_ready"), 1)
            def context(g, s, h):
                pool.wait_ge(sem("y_ready"), s - 1)
                gp.tensor_copy(cg[h][:], CT[:, bass.ds(g * TG, TG)]).then_inc(sem("cg_ready"), 1)

            for p in range(1, phases):
                if p in (5, 7):
                    pool.wait_ge(sem(f"parts{p - 1}"), NT * (NG + 1))
                if p == 2:
                    for a, b, after in pairs(pool, p):
                        s = NG * p + a
                        context(b, s + 1, 1)
                        power(s + 1)
                        power(s + 2)
                        context(after, s + 2, 0)
                        weights_lo(pool, 3, a, 0)
                        weights_lo(pool, 3, b, 1)
                    continue
                if p == 5:
                    for a, b, _ in pairs(pool, p):
                        s = NG * p + a
                        power(s + 1)
                        power(s + 2)
                        weights_lo(pool, 7, a, 0)
                        weights_lo(pool, 7, b, 1)
                    continue
                for g, _, after, h in stages(pool, p):
                    s = NG * p + g
                    if p in (4, 6):
                        heads_pool(pool, p, g, (0, 1))
                    power(s + 1)
                    if p in (4, 6):
                        heads_pool(pool, p, g, (2, 3))
                        context(after, s + 1, 1 - h)
                    if p in MOE:
                        moe_pool(pool, p, g)

        @block.scalar
        def _(act):
            act.dma_start(small[:, 0:PHASES], small_d[:, 0:PHASES]).then_inc(sem("gates_loaded"), 16)
            act.wait_ge(sem("gates_loaded"), 16)
            nc.scalar.activation(tgate[:], S("gates"), ACT.Tanh).then_inc(sem("tgate_ready"), 1)
            act.wait_ge(sem("tgate_ready"), 1)
            act.wait_ge(sem("bias0_ready"), 1)
            norm_act(act, 0, 0)
            act.dma_start(small[:, PHASES:], small_d[:, PHASES:]).then_inc(sem("weights_loaded"), 16)
            act.dma_start(constb[:], constb_d).then_inc(sem("constb_loaded"), 16)
            p0_act(act)
            act.wait_ge(sem("setup_done"), 1)
            for p in range(1, phases):
                if p in MOE:
                    moe_act(act, p)
                elif p == 2:
                    p2_act(act)
                elif p == 5:
                    p5_act(act)
                else:
                    heads_act(act, p)

        @block.tensor
        def _(pe):
            pe.wait_ge(sem("const_loaded"), 16)
            norm_pe(pe, 0, 0)
            p0_pe(pe)
            pe.wait_ge(sem("weights_loaded"), 16)
            pe.wait_ge(sem("const_rest_loaded"), 16)
            setup_pe(pe)
            pe.wait_ge(sem("setup_done"), 1)
            for p in range(1, phases):
                if p in MOE:
                    moe_pe(pe, p)
                elif p == 2:
                    p2_pe(pe)
                elif p == 5:
                    p5_pe(pe)
                else:
                    heads_pe(pe, p)
            finish_pe(pe, last)

        @block.vector
        def _(dve):
            st = Steps(dve, sem("dve_steps"))
            nc.vector.memset(ybias[:], 0.0).then_inc(sem("bias0_ready"), 1)
            st.add(nc.vector.memset(ones5[:], 1.0))
            st.add(nc.vector.memset(vh[:], 0.0))
            st.add(nc.vector.memset(vc[:], 0.0))
            st.settle()
            st.add(nc.vector.memset(vh[:, :, DK], 1.0))
            for k in range(2):
                st.add(nc.vector.memset(vc[k * HALF:(k + 1) * HALF, :, k * VW + DK], 1.0))
            route_setup(st)
            dve.wait_ge(sem("const_loaded"), 16)
            dve.wait_ge(sem("x_loaded0"), 16)
            norm(dve, st, 0, (0, 0))
            p0_dve(dve, st)
            dve.wait_ge(sem("tgate_ready"), 1)
            dve.wait_ge(sem("weights_loaded"), 16)
            dve.wait_ge(sem("const_rest_loaded"), 16)
            setup_dve(dve, st)
            for p in range(1, phases):
                dve.wait_ge(sem("y_ready"), NG * p)
                if p in MOE:
                    moe_dve(dve, st, p)
                elif p == 2:
                    p2_dve(dve, st)
                elif p == 5:
                    p5_dve(dve, st)
                else:
                    heads_dve(dve, st, p)
            finish_dve(dve, NG - 1, last)


def packed(table, at, n, arrays):
    out = np.zeros((P, n), np.float32)
    for name, (rows, start, cols) in at.items():
        out[0:rows, start:start + cols] = arrays[name]
    return out


def head_tiles(w):
    lead = w.shape[:-1]
    src = w.reshape(lead + (HEADS // HEAD_TILES, HEAD_TILES, 1, DK))
    out = np.broadcast_to(src, lead + (HEADS // HEAD_TILES, HEAD_TILES, 32 // DK, DK))
    return out.reshape(lead + (HEAD_TILES * P,))


def constants():
    up = np.zeros((HALF, P), np.float32)
    for t in range(P):
        at = max((t + 0.5) * 0.5 - 0.5, 0.0)
        i0 = int(at)
        up[i0, t] += 1.0 - (at - i0)
        up[min(i0 + 1, HALF - 1), t] += at - i0
    up2 = np.zeros((2, HALF, 2, P), np.float32)
    up2[0, :, 0], up2[1, :, 1] = up, up
    rowmask = np.kron(np.eye(HEAD_TILES), np.ones((32, 1))).astype(np.float32)
    copy = np.arange(P) // DK % 4
    low = np.stack([copy >= 2, copy % 2 == 1], 1).astype(np.float32)
    return dict(ident=np.eye(P, dtype=np.float32), causal=np.triu(np.ones((P, P), np.float32)),
                up=up2.reshape(P, 2 * P), rowmask=rowmask, low=low, sign=1.0 - 2.0 * low)


def selectors(dtype):
    out = np.zeros((P, SEL_N), np.float32)
    out[:, 0:P] = np.eye(P)
    for p, m in MOE.items():
        f = np.arange(m["NR"] * P)
        for part in range(3):
            out[part * m["E"] + f // m["F"], SEL_AT[p] + f] = 1.0
    return out.astype(dtype)


def layout(**inputs):
    A = {k: np.asarray(v) for k, v in inputs.items()}

    def col(a):
        return a.reshape(-1, 1)

    def per_partition(a):
        return np.broadcast_to(a.reshape(1, -1), (P, a.size))

    x2, f2, x4 = "L1_xattn_", "L2_ffn_", "L2_xattn_"
    x6 = "L3_xattn_"
    small = dict(
        gates=per_partition(np.stack([A["g_xattn"], A["g_ffn"]], 1)),
        Wr1=A["L0_ffn_Wr"], Wr3=A["L1_ffn_router_w"].T, Wr7=A["L3_ffn_gate_w"].T,
        rb3=per_partition(A["L1_ffn_bias"]), rb7=per_partition(A["L3_ffn_gate_bias"]),
        hW=A[x2 + "hW"], qWT=A[x2 + "qW"].T, cW=A[x2 + "cW"], kWT=A[x2 + "kW"].T, vWT=A[x2 + "vW"].T,
        oWT=A[x2 + "oW"].T, **{b: col(A[x2 + b]) for b in ("hb", "qb", "cb", "kb", "vb", "ob")},
        Wq4=head_tiles(A[x4 + "Wq"].T), Wk4=head_tiles(A[x4 + "Wk"].T), Wv4=A[x4 + "Wv"].T, Wo4=A[x4 + "Wo"].T,
        Wq6=head_tiles(A[x6 + "w_q"]), Wk6=head_tiles(A[x6 + "w_k"]), Wv6=A[x6 + "w_v"], Wo6=A[x6 + "w_o"],
        bq4=head_tiles(A[x4 + "bq"]).reshape(HEAD_TILES, P).T, bk4=head_tiles(A[x4 + "bk"]).reshape(HEAD_TILES, P).T,
        bq6=head_tiles(A[x6 + "b_q"]).reshape(HEAD_TILES, P).T, bk6=head_tiles(A[x6 + "b_k"]).reshape(HEAD_TILES, P).T,
        bv4=col(A[x4 + "bv"]), bo4=col(A[x4 + "bo"]), bv6=col(A[x6 + "b_v"]), bo6=col(A[x6 + "b_o"]),
        slot_init=A[f2 + "slot_init"], slot_scale=A[f2 + "slot_scale"],
        w1x=A[f2 + "w1"][:, 0:P].T, w1m=A[f2 + "w1"][:, P:].T, b1=col(A[f2 + "b1"]),
        w2=np.concatenate([A[f2 + "w2"].T, A[f2 + "b2"][None]], 0),
        wih=A[f2 + "gru_wih"].T, whh=A[f2 + "gru_whh"].T,
        bih=A[f2 + "gru_bih"].reshape(3, P).T, bhh=A[f2 + "gru_bhh"].reshape(3, P).T,
        wv=A[f2 + "wv"], woT=A[f2 + "wo"].T, bv5=col(A[f2 + "bv"]), bo5=col(A[f2 + "bo"]),
        tau=per_partition(A[f2 + "tau"]),
    )

    def wide(w):
        return w.transpose(1, 0, 2).reshape(P, -1)

    def chunks(w):
        return w.reshape(-1, P, P).transpose(1, 0, 2).reshape(P, -1)

    l1, l3 = "L1_ffn_", "L3_ffn_"
    moe = {
        1: [wide(A["L0_ffn_Wg"]), wide(A["L0_ffn_Wu"]), chunks(A["L0_ffn_Wd"].reshape(-1, P))],
        3: [np.concatenate([wide(A[l1 + "gate_w"]), A[l1 + "sh_gate_w"]], 1),
            np.concatenate([wide(A[l1 + "up_w"]), A[l1 + "sh_up_w"]], 1),
            np.concatenate([chunks(A[l1 + "down_w"].reshape(-1, P)), chunks(A[l1 + "sh_down_w"])], 1)],
        7: [np.concatenate([A[l3 + "w_gate"].reshape(-1, P).T, A[l3 + "sh_gate"].T], 1),
            np.concatenate([A[l3 + "w_up"].reshape(-1, P).T, A[l3 + "sh_up"].T], 1),
            np.concatenate([chunks(A[l3 + "w_down"].transpose(0, 2, 1).reshape(-1, P)), chunks(A[l3 + "sh_down"].T)], 1)],
    }
    arrays = dict(
        in_small=packed(SMALL, SMALL_AT, SMALL_N, small),
        in_const=packed(CONST, CONST_AT, CONST_N, constants()),
        in_constb=selectors(mybir.dt.np(BF16)),
        in_x=A["x"].transpose(1, 0, 2).reshape(P, NB * P),
        in_ctx_t=A["ctx_1024"].transpose(2, 0, 1).reshape(P, NB * P),
        in_mask=A["mask_1x1xSxS2_ik0"].reshape(P, P),
        **{f"in_moe{p}_{k}": w for p, ws in moe.items() for k, w in enumerate(ws)},
    )
    return {name: np.ascontiguousarray(a) for name, a in arrays.items()}


def describe(nc, arrays, phases=PHASES):
    d = {name: nc.dram_tensor(name, a.shape, mybir.dt.from_np(a.dtype), kind="ExternalInput").ap()
         for name, a in arrays.items()}
    out = nc.dram_tensor("out", (P, NB * P), F32, kind="ExternalOutput").ap()
    build(nc, d["in_small"], d["in_const"], d["in_constb"], d["in_x"], d["in_ctx_t"], d["in_mask"],
          {p: [d[f"in_moe{p}_{k}"] for k in range(3)] for p in MOE}, out, phases=phases)


def kernel(**inputs):
    import concourse.bacc as bacc
    from concourse.bass_utils import run_bass_kernel_spmd as run
    arrays = layout(**inputs)
    nc = bacc.Bacc("TRN2", target_bir_lowering=False, num_devices=1)
    describe(nc, arrays)
    out = run(nc, [arrays], core_ids=[0]).results[0]["out"]
    return np.ascontiguousarray(out.reshape(P, NB, P).transpose(1, 0, 2))
```
